# Optimizing a Trainium2 kernel written in Bass

```python
import numpy as np
import jax
import jax.numpy as jnp

def _softmax(x, axis=-1):
    return jax.nn.softmax(x, axis=axis)

def _gelu(x):
    return jax.nn.gelu(x, approximate=True)

def _silu(x):
    return jax.nn.silu(x)

def _sigmoid(x):
    return jax.nn.sigmoid(x)

def _layernorm(x, axis=-1, eps=1e-05):
    m = jnp.mean(x, axis=axis, keepdims=True)
    v = jnp.var(x, axis=axis, keepdims=True)
    return (x - m) / jnp.sqrt(v + eps)

def _scatter_add(tgt, idx, src, axis=0):
    return tgt.at[idx].add(src)

def _segment_sum(src, seg, n):
    return jax.ops.segment_sum(src, seg, n)
kernel_name = 'mk_adaln_d1_jaxref_r8_68f77c'

def setup_inputs(seed: int=0):
    np.random.seed(seed)
    _w = jnp.asarray

    def _L0_attn_setup():
        import jax, jax.numpy as jnp
        import numpy as np
        BETA = 0.3
        THRESH = 0.05
        ATAN_ALPHA = 2.0
        EPS = 1e-06

        @jax.custom_vjp
        def spike_fn(u):
            return (u > 0).astype(u.dtype)

        def _spike_fwd(u):
            return (spike_fn(u), u)

        def _spike_bwd(u, g):
            return (g * (ATAN_ALPHA / 2) / (1 + (jnp.pi / 2 * ATAN_ALPHA * u) ** 2),)
        spike_fn.defvjp(_spike_fwd, _spike_bwd)
        key = jax.random.key(seed)
        ks = jax.random.split(key, 10)
        B, T, D = (4, 512, 128)
        s = 1.0 / np.sqrt(D)
        u = lambda k, shape: jax.random.uniform(k, shape, jnp.float32, -s, s)
        return {'x': jax.random.normal(ks[0], (B, T, D), jnp.float32), 'W_r': u(ks[1], (D, D)), 'b_r': u(ks[2], (D,)), 'W_k': u(ks[3], (D, D)), 'b_k': u(ks[4], (D,)), 'W_v': u(ks[5], (D, D)), 'b_v': u(ks[6], (D,)), 'W_td': u(ks[7], (D, D)), 'b_td': u(ks[8], (D,)), 'global_decay': jax.random.normal(ks[9], (D,), jnp.float32)}
    _L0_attn_in = _L0_attn_setup()

    def _L0_ffn_setup():
        import jax, jax.numpy as jnp
        import numpy as np
        B, T, C, H, E, K, F = (2, 256, 128, 16, 8, 2, 256)
        EPS = 1e-05

        def layernorm(x, w):
            m = x.mean(-1, keepdims=True)
            v = x.var(-1, keepdims=True)
            return (x - m) * jax.lax.rsqrt(v + EPS) * w

        def attention(x, c_attn_w, c_proj_w):
            b, t, c = x.shape
            hd = c // H
            q, k, v = jnp.split(x @ c_attn_w, 3, axis=-1)
            q = q.reshape(b, t, H, hd).transpose(0, 2, 1, 3)
            k = k.reshape(b, t, H, hd).transpose(0, 2, 1, 3)
            v = v.reshape(b, t, H, hd).transpose(0, 2, 1, 3)
            att = jnp.einsum('bhqd,bhkd->bhqk', q, k) / jnp.sqrt(jnp.asarray(hd, x.dtype))
            causal = jnp.tril(jnp.ones((t, t), bool))
            att = jnp.where(causal, att, jnp.asarray(-jnp.inf, att.dtype))
            att = jax.nn.softmax(att, axis=-1)
            y = jnp.einsum('bhqk,bhkd->bhqd', att, v)
            y = y.transpose(0, 2, 1, 3).reshape(b, t, c)
            return y @ c_proj_w

        def moe_mlp(x, router_w, w1, w2):
            b, t, c = x.shape
            xf = x.reshape(-1, c)
            router_logits = xf @ router_w
            probs = jax.nn.softmax(router_logits.astype(jnp.float32), axis=-1)
            rw, sel = jax.lax.top_k(probs, K)
            rw = rw / rw.sum(axis=-1, keepdims=True)
            rw = rw.astype(x.dtype)
            w1e = w1.reshape(c, E, F).transpose(1, 0, 2)
            w2e = w2.reshape(E, F, c)
            h = jax.nn.gelu(jnp.einsum('nc,ecf->enf', xf, w1e), approximate=False)
            y_all = jnp.einsum('enf,efc->nec', h, w2e)
            y_sel = jnp.take_along_axis(y_all, sel[:, :, None], axis=1)
            y = (y_sel * rw[:, :, None]).sum(axis=1)
            return y.reshape(b, t, c)
        key = jax.random.key(seed)
        ks = jax.random.split(key, 6)
        s = 0.02
        return {'x': jax.random.normal(ks[0], (B, T, C), jnp.float32), 'ln1_w': jnp.ones((C,), jnp.float32), 'c_attn_w': jax.random.normal(ks[1], (C, 3 * C), jnp.float32) * s, 'c_proj_w': jax.random.normal(ks[2], (C, C), jnp.float32) * s, 'ln2_w': jnp.ones((C,), jnp.float32), 'router_w': jax.random.normal(ks[3], (C, E), jnp.float32) * s, 'w1': jnp.clip(jax.random.normal(ks[4], (C, E * F), jnp.float32) * s, -0.06, 0.06), 'w2': jnp.clip(jax.random.normal(ks[5], (E * F, C), jnp.float32) * s, -0.06, 0.06)}
    _L0_ffn_in = _L0_ffn_setup()
    _L0_c = _w((lambda *s: np.random.randn(*s).astype(np.float32) * 0.05)(16, 128))
    _L0_wmod = _w((lambda *s: np.random.randn(*s).astype(np.float32) * 0.05)(128, 6 * 128) * 128 ** (-0.5))
    _d = {'L0_attn_x': _L0_attn_in['x'], 'L0_attn_W_r': _L0_attn_in['W_r'], 'L0_attn_b_r': _L0_attn_in['b_r'], 'L0_attn_W_k': _L0_attn_in['W_k'], 'L0_attn_b_k': _L0_attn_in['b_k'], 'L0_attn_W_v': _L0_attn_in['W_v'], 'L0_attn_b_v': _L0_attn_in['b_v'], 'L0_attn_W_td': _L0_attn_in['W_td'], 'L0_attn_b_td': _L0_attn_in['b_td'], 'L0_attn_global_decay': _L0_attn_in['global_decay'], 'L0_ffn_ln1_w': _L0_ffn_in['ln1_w'], 'L0_ffn_c_attn_w': _L0_ffn_in['c_attn_w'], 'L0_ffn_c_proj_w': _L0_ffn_in['c_proj_w'], 'L0_ffn_ln2_w': _L0_ffn_in['ln2_w'], 'L0_ffn_router_w': _L0_ffn_in['router_w'], 'L0_ffn_w1': _L0_ffn_in['w1'], 'L0_ffn_w2': _L0_ffn_in['w2'], 'L0_c': _L0_c, 'L0_wmod': _L0_wmod}
    _x0 = _d['L0_attn_x']
    _d['L0_attn_x'] = jax.random.normal(jax.random.fold_in(jax.random.key(seed), 1), (16, 512, 128), dtype=_x0.dtype)
    del _x0
    return _d

def reference(L0_attn_x, L0_attn_W_r, L0_attn_b_r, L0_attn_W_k, L0_attn_b_k, L0_attn_W_v, L0_attn_b_v, L0_attn_W_td, L0_attn_b_td, L0_attn_global_decay, L0_ffn_ln1_w, L0_ffn_c_attn_w, L0_ffn_c_proj_w, L0_ffn_ln2_w, L0_ffn_router_w, L0_ffn_w1, L0_ffn_w2, L0_c, L0_wmod):

    def _L0_attn_ref(x, W_r, b_r, W_k, b_k, W_v, b_v, W_td, b_td, global_decay):
        import jax, jax.numpy as jnp
        import numpy as np
        BETA = 0.3
        THRESH = 0.05
        ATAN_ALPHA = 2.0
        EPS = 1e-06

        @jax.custom_vjp
        def spike_fn(u):
            return (u > 0).astype(u.dtype)

        def _spike_fwd(u):
            return (spike_fn(u), u)

        def _spike_bwd(u, g):
            return (g * (ATAN_ALPHA / 2) / (1 + (jnp.pi / 2 * ATAN_ALPHA * u) ** 2),)
        spike_fn.defvjp(_spike_fwd, _spike_bwd)
        B, T, D = x.shape
        r = jax.nn.sigmoid(jnp.einsum('btd,ed->bte', x, W_r) + b_r)
        ek = jnp.exp(jnp.einsum('btd,ed->bte', x, W_k) + b_k)
        v = jnp.einsum('btd,ed->bte', x, W_v) + b_v
        td = jnp.exp(b_td)
        g = jnp.exp(global_decay)

        def step(carry, inputs):
            sa, sb, mem = carry
            ek_t, v_t, r_t = inputs
            sa = ek_t * v_t + td * sa
            sb = ek_t + td * sb
            wkv = (g * ek_t * v_t + sa) / (g * ek_t + sb + EPS)
            inp_t = r_t * wkv
            reset = spike_fn(mem - THRESH)
            mem = BETA * mem + inp_t - reset * THRESH
            spk = spike_fn(mem - THRESH)
            return ((sa, sb, mem), spk)
        z = jnp.zeros((B, D), x.dtype)
        xs = (jnp.swapaxes(ek, 0, 1), jnp.swapaxes(v, 0, 1), jnp.swapaxes(r, 0, 1))
        _, spks = jax.lax.scan(step, (z, z, z), xs)
        return jnp.swapaxes(spks, 0, 1)

    def _L0_ffn_ref(x, ln1_w, c_attn_w, c_proj_w, ln2_w, router_w, w1, w2):
        import jax, jax.numpy as jnp
        import numpy as np
        B, T, C, H, E, K, F = (2, 256, 128, 16, 8, 2, 256)
        EPS = 1e-05

        def layernorm(x, w):
            m = x.mean(-1, keepdims=True)
            v = x.var(-1, keepdims=True)
            return (x - m) * jax.lax.rsqrt(v + EPS) * w

        def attention(x, c_attn_w, c_proj_w):
            b, t, c = x.shape
            hd = c // H
            q, k, v = jnp.split(x @ c_attn_w, 3, axis=-1)
            q = q.reshape(b, t, H, hd).transpose(0, 2, 1, 3)
            k = k.reshape(b, t, H, hd).transpose(0, 2, 1, 3)
            v = v.reshape(b, t, H, hd).transpose(0, 2, 1, 3)
            att = jnp.einsum('bhqd,bhkd->bhqk', q, k) / jnp.sqrt(jnp.asarray(hd, x.dtype))
            causal = jnp.tril(jnp.ones((t, t), bool))
            att = jnp.where(causal, att, jnp.asarray(-jnp.inf, att.dtype))
            att = jax.nn.softmax(att, axis=-1)
            y = jnp.einsum('bhqk,bhkd->bhqd', att, v)
            y = y.transpose(0, 2, 1, 3).reshape(b, t, c)
            return y @ c_proj_w

        def moe_mlp(x, router_w, w1, w2):
            b, t, c = x.shape
            xf = x.reshape(-1, c)
            router_logits = xf @ router_w
            probs = jax.nn.softmax(router_logits.astype(jnp.float32), axis=-1)
            rw, sel = jax.lax.top_k(probs, K)
            rw = rw / rw.sum(axis=-1, keepdims=True)
            rw = rw.astype(x.dtype)
            w1e = w1.reshape(c, E, F).transpose(1, 0, 2)
            w2e = w2.reshape(E, F, c)
            h = jax.nn.gelu(jnp.einsum('nc,ecf->enf', xf, w1e), approximate=False)
            y_all = jnp.einsum('enf,efc->nec', h, w2e)
            y_sel = jnp.take_along_axis(y_all, sel[:, :, None], axis=1)
            y = (y_sel * rw[:, :, None]).sum(axis=1)
            return y.reshape(b, t, c)
        x = x + attention(layernorm(x, ln1_w), c_attn_w, c_proj_w)
        x = x + moe_mlp(layernorm(x, ln2_w), router_w, w1, w2)
        return x
    x = L0_attn_x
    mod = (_silu(L0_c) @ L0_wmod).reshape(L0_c.shape[0], 6, 1, -1)
    sa, ca, ga, sb, cb, gb = (mod[:, 0], mod[:, 1], mod[:, 2], mod[:, 3], mod[:, 4], mod[:, 5])
    ga = (2 * (ga >= 0) - 1) * jnp.maximum(jnp.abs(ga), 0.25)
    gb = (2 * (gb >= 0) - 1) * jnp.maximum(jnp.abs(gb), 0.25)
    h = _layernorm(x, axis=-1) * (1 + ca) + sa
    x = x + ga * _L0_attn_ref(h, L0_attn_W_r, L0_attn_b_r, L0_attn_W_k, L0_attn_b_k, L0_attn_W_v, L0_attn_b_v, L0_attn_W_td, L0_attn_b_td, L0_attn_global_decay)
    h = _layernorm(x, axis=-1) * (1 + cb) + sb
    x = x + gb * _L0_ffn_ref(h, L0_ffn_ln1_w, L0_ffn_c_attn_w, L0_ffn_c_proj_w, L0_ffn_ln2_w, L0_ffn_router_w, L0_ffn_w1, L0_ffn_w2)
    return x

_drawn_inputs = setup_inputs


def setup_inputs(seed=0):
    import zlib

    import numpy as np

    out = dict(_drawn_inputs(seed))
    spreads = {'L0_ffn_ln1_w': (1.0, 0.6), 'L0_ffn_ln2_w': (1.0, 0.6)}
    factors = {'L0_ffn_c_attn_w': 8.0,
     'L0_ffn_c_proj_w': 8.0,
     'L0_ffn_router_w': 8.0,
     'L0_ffn_w1': 8.0,
     'L0_ffn_w2': 8.0}
    for name, (base, spread) in spreads.items():
        noise = np.random.default_rng([zlib.crc32(name.encode()), seed]).standard_normal(out[name].shape)
        drawn = base * np.exp(spread * noise) if base else spread * noise
        out[name] = jnp.asarray(drawn.astype(out[name].dtype))
    for name, factor in factors.items():
        out[name] = (out[name] * factor).astype(out[name].dtype)
    return out
```

```python
import math

import concourse.bass as bass
from concourse import mybir
from contextlib import ExitStack

FP32 = mybir.dt.float32
BF16 = mybir.dt.bfloat16
ALU = mybir.AluOpType
ACT = mybir.ActivationFunctionType
AX = mybir.AxisListType

THRESH = 0.05
BETA = 0.3
WKV_EPS = 1e-6
LN_EPS = 1e-5
GATE_MIN = 0.25
MASKED = -3.0e38


def adaln_spiking_moe_layer(nc, x, W_r, b_r, W_k, b_k, W_v, b_v, W_td, b_td, global_decay, ln1_w, c_attn_w,
                            c_proj_w, ln2_w, router_w, w1, w2, c, wmod, out):
    B, T, D = x.shape
    P = 128
    NT = T // P
    HEADS, HD = 16, 8
    QUADS = 4
    HQ = HEADS // QUADS
    E = router_w.shape[1]
    F = w1.shape[1] // E
    FH = F // P
    SCORES = P * NT * (NT + 1) // 2
    NBLK = NT * (NT + 1) // 2
    TERMS = 6
    SPLIT = 3
    PROD = TERMS * HD
    SHIFT = 96
    U = 32
    Q_AT = {3: 0, 2: 512, 0: 896, 1: 1024}
    K_AT = {0: 0, 1: 512, 3: 896, 2: 1024}


    mod_rows = nc.dram_tensor("mod_rows", [B, 3, D], FP32).ap()
    mid = nc.dram_tensor("mid", [B, P, NT, D], FP32).ap()
    q_terms = [nc.dram_tensor(f"q_terms{i}", [D, TERMS, T], BF16).ap() for i in range(2)]
    k_terms = [nc.dram_tensor(f"k_terms{i}", [D, TERMS, T], BF16).ap() for i in range(2)]
    x_v = x.rearrange("b (i p) d -> b p i d", p=P)
    out_v = out.rearrange("b (i p) d -> b p i d", p=P)

    ctx = ExitStack()
    with ctx:
        def sb(name, shape, dt=FP32):
            return ctx.enter_context(nc.sbuf_tensor(name, shape, dt))

        def pb(name, shape):
            return ctx.enter_context(nc.psum_tensor(name, shape, FP32))

        sems = {}

        def sem(name):
            if name not in sems:
                sems[name] = ctx.enter_context(nc.semaphore(name))
            return sems[name]

        def wait(eng, name, value):
            if not isinstance(value, int) or value > 0:
                eng.wait_ge(sem(name), value)

        def wait_apart(eng, who, name, value):
            wait(eng, name, value)
            if not isinstance(value, int):
                eng.sem_inc(sem(f"{who}_passed"), 1)

        def ds(b):
            return slice(b, b + 1) if isinstance(b, int) else bass.ds(b, 1)

        def dram(ap, b):
            return ap[ds(b)].rearrange("o p i d -> (o p) i d")

        row_all = sb("row_all", [P, B, T])
        logits_all = sb("logits_all", [P, B, NT, E])
        ident = sb("ident", [P, P])
        ident_h = sb("ident_h", [P, P], BF16)
        causal = sb("causal", [P, P], BF16)
        half = sb("half", [P, NT])
        wT = sb("wT", [P, 3, D])
        wqkv = sb("wqkv", [P, 3 * D])
        wproj = sb("wproj", [P, D])
        wrout = sb("wrout", [P, E])
        cols = sb("cols", [P, 8])
        BR, BK, BV, TD, GD, LN1, LN2 = (cols[:, i:i + 1] for i in range(7))
        mod_cm = sb("mod_cm", [P, 3, B])

        ARENA = 26 * 1024
        arena = sb("arena", [P, ARENA])

        def carver():
            at = [0]

            def take(n, dt=FP32):
                words = n if dt == FP32 else n // 2
                v = arena[:, at[0]:at[0] + words]
                at[0] += words
                assert at[0] <= ARENA, at[0]
                return v if dt == FP32 else v.bitcast(dt)
            return take

        take = carver()
        c_in = take(D)
        wmod_in = take(6 * D)
        w_in = take(3 * D).rearrange("p (a d) -> p a d", a=3)
        silu_c = take(B)
        silu_t = take(2 * B).rearrange("p (a b) -> p a b", a=2)
        gate_t = take(2 * B).rearrange("p (a b) -> p a b", a=2)
        row_t = take(3 * D).rearrange("p (a d) -> p a d", a=3)
        row_g = take(2 * D).rearrange("p (a d) -> p a d", a=2)

        def two(n):
            return [take(n) for _ in range(2)]

        a_x = [v.rearrange("p (i d) -> p i d", i=NT) for v in two(T)]
        a_stats = [v.rearrange("p (i s) -> p i s", i=NT) for v in two(NT * 6)]
        a_mv = [v.rearrange("p (i s) -> p i s", i=NT) for v in two(NT * 2)]
        a_var = two(NT)
        a_rstd = two(NT)
        a_xhat = [v.rearrange("p (i d) -> p i d", i=NT) for v in two(T)]
        a_hT = two(T)
        a_ek = two(T)
        a_er = two(T)
        a_er1, a_kv, a_sa, a_sb, a_num, a_den0, a_den, a_rec = (take(T) for _ in range(8))

        take = carver()
        q_stack = [take(HEADS * T, BF16).rearrange("p (h t) -> p h t", h=HEADS) for _ in range(2)]
        k_stack = [take(HEADS * T, BF16).rearrange("p (h t) -> p h t", h=HEADS) for _ in range(2)]
        probs = [take(HQ * SCORES).rearrange("p (h s) -> p h s", h=HQ) for _ in range(2)]

        NL = B * NT
        take = carver()
        w1_sb = take(E * F)
        w2_sb = take(E * FH * D).rearrange("p (f d) -> p f d", d=D)
        hid = [take(FH * T).rearrange("p (f t) -> p f t", f=FH) for _ in range(2)]
        rw_b = take(NT * E).rearrange("p (i e) -> p i e", e=E)
        acc = take(T).rearrange("p (i d) -> p i d", i=NT)
        gate_c = take(D)
        base_c = take(T).rearrange("p (i d) -> p i d", i=NT)
        place = take(E)
        r_eq, r_l2, r_k, r_o1, r_o2, rw = (take(NL * E).rearrange("p (i e) -> p i e", e=E) for _ in range(6))
        r_m1, r_m2, r_f1, r_f2, r_d, r_e2, r_s, r_r1, r_r2 = (take(NL) for _ in range(9))

        v_aug = [sb(f"v_aug{i}", [P, NT, HEADS, HD + 1]) for i in range(2)]

        def buf(name):
            return sb(name, [P, NT, D])

        f_x, f_x1, f_z, f_h, b_y, b_x2, b_z2, b_x1 = (buf(n) for n in (
            "f_x", "f_x1", "f_z", "f_h", "b_y", "b_x2", "b_z2", "b_x1"))
        f_spk = sb("f_spk", [P, T])
        f_z1T = sb("f_z1T", [P, T])
        f_fp = sb("f_fp", [P, 2, T])
        f_parts = sb("f_parts", [P, 2, SPLIT, T], BF16)
        f_v = sb("f_v", [P, NT, D])
        f_mod = sb("f_mod", [P, 2, D])
        b_gate = sb("b_gate", [P, D])
        b_yT = sb("b_yT", [P, T])
        b_z2T = sb("b_z2T", [P, T])
        ln_stats = [sb(f"ln_stats{i}", [P, NT, 6]) for i in range(3)]
        ln_mv = [sb(f"ln_mv{i}", [P, NT, 2]) for i in range(3)]
        ln_var = [sb(f"ln_var{i}", [P, NT]) for i in range(3)]
        ln_rstd = [sb(f"ln_rstd{i}", [P, NT]) for i in range(3)]
        blkmax = [sb(f"blkmax{i}", [P, HQ, NBLK]) for i in range(2)]
        rowmax = [sb(f"rowmax{i}", [P, HQ, NT]) for i in range(2)]
        shift = [sb(f"shift{i}", [HQ * NT, 2, P], BF16) for i in range(2)]
        o_sb = sb("o_sb", [P, T])
        o_rec = sb("o_rec", [P, NT, HQ])
        m_in = f_fp[:, 0, 0:B * U].rearrange("p (b u) -> p b u", b=B)
        m_out = f_fp[:, 1, 0:B * U].rearrange("p (b u) -> p b u", b=B)
        m_tmp = b_gate[:, 0:B]

        S_ps = pb("S_ps", [P, 3 * 512])
        T_ps = pb("T_ps", [P, 3 * 512])
        O_ps = pb("O_ps", [P, 512])
        M_ps = pb("M_ps", [P, 512])
        M_tiles = M_ps[:, :].rearrange("p (i d) -> p i d", i=NT)

        def bcast(ap, shape):
            return ap.broadcast_to(shape)

        JOBS = [("o", 0, -2), ("max", 0, 1), ("spk", 0, 2), ("route", 0, -2),
                ("o", 1, -1), ("max", 1, 2), ("y", 1, -1), ("proj", 1, -1),
                ("o", 2, 0), ("max", 2, 3), ("z1", 2, 2), ("q", 2, 2),
                ("o", 3, 1), ("max", 3, 4), ("k", 3, 2), ("v", 3, 2), ("z2", 3, -1)]
        READER = {"o": "y_made", "max": "shift_made", "spk": "x1_made", "route": "logits_made", "y": "yT_made",
                  "proj": "x2_made", "z1": "z1T_made", "q": "q_out", "k": "k_out", "v": "v_out", "z2": "z2T_made"}
        PER_QUAD = ("o", "max")

        def job_index(job, k):
            kind, _, lag = job
            n = QUADS * k + lag if kind in PER_QUAD else k + lag
            last = QUADS * B if kind in PER_QUAD else B
            return n if not isinstance(k, int) or 0 <= n < last else None

        def wait_M_free(eng, kind, u, k):
            at = next(i for i, j in enumerate(JOBS) if j[0] == kind and j[1] == u)
            back = 0
            while True:
                at -= 1
                if at < 0:
                    at, back = len(JOBS) - 1, back + 1
                if back > 2:
                    return
                n = job_index(JOBS[at], k - back)
                if n is not None:
                    wait(eng, READER[JOBS[at][0]], n + 1)
                    return

        def there(b):
            return not isinstance(b, int) or 0 <= b < B

        def iterations(run):
            def program(eng):
                for k in range(-2, 2):
                    run(k, k % 2)
                with eng.Fori(1, B // 2 - 1) as i:
                    run(i * 2, 0)
                    run(i * 2 + 1, 1)
                for k in range(B - 2, B + 2):
                    run(k, k % 2)
            return program

        block = ctx.enter_context(nc.Block())

        @block.sync
        def _(sp):
            for dst, src in ((c_in[0:B, :], c), (wmod_in, wmod), (w_in[:, 0], W_r), (w_in[:, 1], W_k), (w_in[:, 2], W_v),
                             (wqkv[:], c_attn_w), (wproj[:], c_proj_w), (wrout[:], router_w)):
                sp.dma_start(dst, src).then_inc(sem("weights_in"), 16)
            for i, v in enumerate((b_r, b_k, b_v, b_td, global_decay, ln1_w, ln2_w)):
                sp.dma_start(cols[:, i:i + 1], v.rearrange("(p o) -> p o", o=1)).then_inc(sem("weights_in"), 16)
            sp.wait_ge(sem("rows_made"), 1)
            sp.dma_start(mod_rows, row_t[0:B]).then_inc(sem("rows_saved"), 16)
            sp.wait_ge(sem("rows_saved"), 16)

            def load_x(b, p):
                wait_apart(sp, "sp", "xhat_a", b - 1)
                sp.dma_start(a_x[p], dram(x_v, b)).then_inc(sem(f"x_in{p}"), 16)
            load_x(0, 0)
            load_x(1, 1)
            with sp.Fori(1, B // 2) as i:
                load_x(i * 2, 0)
                load_x(i * 2 + 1, 1)

            def shift_rows(k, p, q):
                n = QUADS * k + q
                b, u, pp = k + q // QUADS, q % QUADS, (p + q // QUADS) % 2
                if there(b):
                    wait_apart(sp, "sp", "shift_made", n + 1)
                    for r in range(2):
                        dst = q_stack[pp][SHIFT + r:SHIFT + r + 1, HQ * u:HQ * (u + 1), :]
                        sp.dma_start(dst.rearrange("o h (i t) -> o (h i) t", i=NT),
                                     shift[u % 2][:, r, :]).then_inc(sem(f"shift_in{u % 2}"), 16)

            def run(k, p):
                if there(k + 2):
                    load_front(k + 2)
                shift_rows(k, p, 1)
                if there(k + 1):
                    b, pp = k + 1, 1 - p
                    wait_apart(sp, "sp", "parts_made", b + 1)
                    wait_apart(sp, "sp", "stacks_in", 32 * (b - 1))
                    q1, q2, q3 = (f_parts[:, 0, i:i + 1, :] for i in range(3))
                    sp.dma_start(q_terms[pp][:, 0:3], bcast(q1, [D, 3, T])).then_inc(sem("terms_out"), 16)
                    sp.dma_start(q_terms[pp][:, 3:5], bcast(q2, [D, 2, T])).then_inc(sem("terms_out"), 16)
                    sp.dma_start(q_terms[pp][:, 5:6], q3).then_inc(sem("terms_out"), 16)
                    sp.dma_start(k_terms[pp][:, 0:3], f_parts[:, 1, 0:3]).then_inc(sem("terms_out"), 16)
                    sp.dma_start(k_terms[pp][:, 3:5], f_parts[:, 1, 0:2]).then_inc(sem("terms_out"), 16)
                    sp.dma_start(k_terms[pp][:, 5:6], f_parts[:, 1, 0:1]).then_inc(sem("terms_out"), 16)
                    wait_apart(sp, "sp", "terms_out", 96 * (b + 1))
                    wait_apart(sp, "sp", "T_mm", HEADS * (b - 1))
                    if isinstance(b, int) and b < 2:
                        sp.wait_ge(sem("pads_set"), 1)
                    for stack, terms in ((q_stack[pp], q_terms[pp]), (k_stack[pp], k_terms[pp])):
                        sp.dma_start(stack[0:PROD], terms.rearrange("(h d) s t -> (d s) h t", d=HD)
                                     ).then_inc(sem("stacks_in"), 16)
                if there(k + 2):
                    wait_apart(sp, "sp", "x1_made", k + 3)
                    sp.dma_start(dram(mid, k + 2), f_x1[:]).then_inc(sem("x1_saved"), 16)
                shift_rows(k, p, 2)
                if there(k - 1):
                    b = k - 1
                    wait_apart(sp, "sp", "base_out", 16 * b)
                    wait_apart(sp, "sp", "x1_saved", 16 * (b + 1))
                    sp.dma_start(b_x1[:], dram(mid, b)).then_inc(sem("x1_back"), 16)
                    sp.dma_start(b_gate[:], bcast(mod_rows[ds(b), 2, :], [P, D])).then_inc(sem("x1_back"), 16)
                shift_rows(k, p, 3)
                shift_rows(k, p, 4)
                if there(k - 1):
                    wait_apart(sp, "sp", "base_made", k)
                    sp.dma_start(dram(out_v, k - 1), b_x1[:]).then_inc(sem("base_out"), 16)

            def load_front(b):
                wait_apart(sp, "sp", "x1_made", b)
                sp.dma_start(f_x[:], dram(x_v, b)).then_inc(sem("x_in_f"), 16)
                wait_apart(sp, "sp", "h_made", b)
                sp.dma_start(f_mod[:], bcast(mod_rows[ds(b), 0:2, :], [P, 2, D])).then_inc(sem("x_in_f"), 16)

            iterations(run)(sp)
            sp.wait_ge(sem("base_out"), 16 * B)

            for dst, src in ((w1_sb, w1), (w2_sb, w2.rearrange("(f p) d -> p f d", p=P))):
                sp.wait_ge(sem("z2_kept"), B)
                sp.wait_ge(sem("pv_mm"), QUADS * B)
                sp.dma_start(dst, src).then_inc(sem("w12_in"), 16)
            with sp.Fori(0, B) as b:
                sp.dma_start(base_c, dram(out_v, b)).then_inc(sem("base_in"), 16)
                sp.dma_start(gate_c, bcast(mod_rows[ds(b), 2, :], [P, D])).then_inc(sem("base_in"), 16)
                wait_apart(sp, "sp", "out_made", b + 1)
                sp.dma_start(dram(out_v, b), base_c).then_inc(sem("out_saved"), 16)
                wait_apart(sp, "sp", "out_saved", b * 16 + 16)

        @block.gpsimd
        def _(pool):
            g = nc.gpsimd
            g.memset(ident[:], 0.0).then_inc(sem("id0"), 1)
            g.memset(half[:], -0.5).then_inc(sem("half_set"), 1)
            g.memset(m_tmp, 0.0)
            g.memset(causal[:], 0.0).then_inc(sem("id0"), 1)
            pool.wait_ge(sem("id0"), 2)
            g.affine_select(out=ident[:], in_=ident[:], compare_op=ALU.not_equal, fill=1.0, base=0,
                            pattern=[[-1, P]], channel_multiplier=1).then_inc(sem("id1"), 1)
            g.affine_select(out=causal[:], in_=causal[:], compare_op=ALU.is_ge, fill=MASKED, base=0,
                            pattern=[[-1, P]], channel_multiplier=1).then_inc(sem("id1"), 1)
            pool.wait_ge(sem("id1"), 2)
            g.tensor_copy(ident_h[:], ident[:]).then_inc(sem("consts"), 1)
            for v in v_aug:
                g.memset(v[:, :, :, HD:HD + 1], 1.0).then_inc(sem("ones_set"), 1)

            pool.wait_ge(sem("half_set"), 1)

            def rstd_a(b, p):
                pool.wait_ge(sem("var_a"), b + 1)
                g.tensor_tensor(a_rstd[p], a_var[p], half[:], ALU.pow).then_inc(sem("rstd_a"), 1)
            with pool.Fori(0, B // 2) as i:
                rstd_a(i * 2, 0)
                rstd_a(i * 2 + 1, 1)

            pool.wait_ge(sem("inp_a"), B)
            for t in q_stack + k_stack:
                g.memset(t[0:SHIFT].bitcast(FP32), 0.0)
            for t in k_stack:
                last = g.memset(t[SHIFT:SHIFT + 2], 1.0)
            last.then_inc(sem("pads_set"), 1)
            pool.wait_ge(sem("pads_set"), 1)

            def rstd(i, b):
                pool.wait_ge(sem(f"var{i}"), b + 1)
                g.tensor_tensor(ln_rstd[i][:], ln_var[i][:], half[:], ALU.pow).then_inc(sem(f"rstd{i}"), 1)

            def keep(src, b):
                return g.tensor_copy(row_all[:, ds(b), :].rearrange("p o t -> p (o t)"), src)

            def mask(k, p, u):
                if there(k):
                    wait_apart(pool, "pool", "exp_made", HEADS * k + HQ * (u + 1))
                    for i in range(NT):
                        v = probs[u % 2][:, :, K_AT[i]:K_AT[i] + P]
                        last = g.affine_select(out=v, in_=v, compare_op=ALU.is_ge, fill=0.0, base=0,
                                               pattern=[[0, HQ], [1, P]], channel_multiplier=-1)
                    last.then_inc(sem("masked"), 1)

            def run(k, p):
                if there(k + 2):
                    b = k + 2
                    rstd(0, b)
                    pool.wait_ge(sem("z_made"), b + 1)
                    pool.wait_ge(sem("x_in_f"), 32 * (b + 1))
                    g.tensor_tensor(f_h[:], f_z[:], bcast(f_mod[:, 1:2, :], [P, NT, D]), ALU.mult
                                    ).then_inc(sem("h_half"), 1)
                    pool.wait_ge(sem("h_half"), b + 1)
                    g.tensor_tensor(f_h[:], f_h[:], bcast(f_mod[:, 0:1, :], [P, NT, D]), ALU.add
                                    ).then_inc(sem("h_made"), 1)
                    wait_apart(pool, "pool", "h_made", b + 1)
                    keep(f_h[:].rearrange("p i d -> p (i d)"), b).then_inc(sem("h_kept"), 1)
                mask(k, p, 0)
                if there(k + 1):
                    b, pp = k + 1, 1 - p
                    pool.wait_ge(sem("v_out"), b + 1)
                    wait_apart(pool, "pool", "pv_mm", QUADS * (b - 1))
                    g.tensor_copy(v_aug[pp][:, :, :, 0:HD], f_v[:].rearrange("p i (h d) -> p i h d", h=HEADS)
                                  ).then_inc(sem("v_put"), 1)
                if there(k + 2):
                    rstd(1, k + 2)
                mask(k, p, 1)
                if there(k - 1):
                    b = k - 1
                    rstd(2, b)
                mask(k, p, 2)
                if there(k - 1):
                    pool.wait_ge(sem("z2_made"), b + 1)
                    pool.wait_ge(sem("x1_back"), 32 * (b + 1))
                    g.tensor_tensor(b_x2[:], b_x2[:], bcast(b_gate[:].rearrange("p (o d) -> p o d", o=1), [P, NT, D]),
                                    ALU.mult).then_inc(sem("gated"), 1)
                    pool.wait_ge(sem("gated"), b + 1)
                    g.tensor_tensor(b_x1[:], b_x1[:], b_x2[:], ALU.add).then_inc(sem("base_made"), 1)
                mask(k, p, 3)
                if there(k + 2):
                    b = k + 2
                    wait(pool, "terms_out", 96 * b)
                    wait_apart(pool, "pool", "k_out", b + 1)
                    g.tensor_copy(f_parts[:, :, 0, :], f_fp[:]).then_inc(sem("split"), 1)
                    pool.wait_ge(sem("split"), 4 * b + 1)
                    g.tensor_tensor(f_fp[:], f_fp[:], f_parts[:, :, 0, :], ALU.subtract).then_inc(sem("split"), 1)
                    wait_apart(pool, "pool", "split", 4 * b + 2)
                    g.tensor_copy(f_parts[:, :, 1, :], f_fp[:]).then_inc(sem("split"), 1)
                    pool.wait_ge(sem("split"), 4 * b + 3)
                    g.tensor_tensor(f_parts[:, :, 2, :], f_fp[:], f_parts[:, :, 1, :], ALU.subtract
                                    ).then_inc(sem("split"), 1)
                    pool.wait_ge(sem("split"), 4 * b + 4)
                    pool.sem_inc(sem("parts_made"), 1)
                if there(k - 1):
                    wait_apart(pool, "pool", "z2T_made", k)
                    keep(b_z2T[:], k - 1).then_inc(sem("z2_kept"), 1)

            iterations(run)(pool)

        @block.tensor
        def _(pe):
            t = nc.tensor
            pe.wait_ge(sem("consts"), 1)
            pe.wait_ge(sem("weights_in"), 16 * 15)
            for i in range(3):
                t.transpose(S_ps[:, i * D:(i + 1) * D], w_in[:, i, :], ident[:])
            t.transpose(M_ps[:, 0:B], c_in[0:B, :], ident[0:B, 0:B]).then_inc(sem("setup_tr"), 1)
            pe.wait_ge(sem("silu_made"), 1)
            for i in range(3):
                t.matmul(T_ps[:, i * B:(i + 1) * B], wmod_in[:, i * D:(i + 1) * D], silu_c, start=True, stop=True)
            t.matmul(O_ps[0:B, 0:3 * D], silu_c, wmod_in[:, 3 * D:6 * D], start=True, stop=True
                     ).then_inc(sem("mod_mm"), 1)

            pe.wait_ge(sem("setup_done"), 1)

            def spiking(b, p):
                R_ps = (S_ps, T_ps)[p]
                pe.wait_ge(sem("xhat_a"), b + 1)
                if not (isinstance(b, int) and b == 0):
                    pe.wait_ge(sem("hT_a"), b)
                for i in range(NT):
                    last = t.transpose(M_ps[:, i * P:(i + 1) * P], a_xhat[p][:, i, :], ident[:])
                last.then_inc(sem("xT_a"), 1)
                pe.wait_ge(sem("hT_a"), b + 1)
                wait(pe, "ek_a", b - 1)
                wait(pe, "kv_a", b - 1)
                for i in range(3):
                    last = t.matmul(R_ps[:, i * T:(i + 1) * T], wT[:, i, :], a_hT[p], start=True, stop=True)
                last.then_inc(sem("rkv_a"), 1)
            spiking(0, 0)
            spiking(1, 1)
            with pe.Fori(1, B // 2) as i:
                spiking(i * 2, 0)
                spiking(i * 2 + 1, 1)

            def scores(k, p, q, j):
                b, u, pp = k + q // QUADS, q % QUADS, (p + q // QUADS) % 2
                if not there(b):
                    return
                h = HQ * u + j
                if h == 0:
                    pe.wait_ge(sem("stacks_in"), 32 * (b + 1))
                wait(pe, "blk_made", HEADS * b + h)
                for i in range(NT):
                    at = Q_AT[i]
                    t.matmul(S_ps[:, at:at + P * (i + 1)], q_stack[pp][0:SHIFT, h, P * i:P * (i + 1)],
                             k_stack[pp][0:SHIFT, h, 0:P * (i + 1)], start=True, stop=False)
                    last = t.matmul(S_ps[:, at + P * i:at + P * (i + 1)], ident_h[:], causal[:], start=False, stop=True)
                last.then_inc(sem("S_mm"), 1)

            def shifted(k, p, u, j):
                if not there(k):
                    return
                h = HQ * u + j
                if j == 0:
                    n = QUADS * k + u
                    pe.wait_ge(sem(f"shift_in{u % 2}"), (n - u % 2) * 16 + 32)
                wait(pe, "exp_made", HEADS * k + h)
                for i in range(NT):
                    last = t.matmul(T_ps[:, K_AT[i]:K_AT[i] + T - P * i], k_stack[p][0:SHIFT + 2, h, P * i:P * (i + 1)],
                                    q_stack[p][0:SHIFT + 2, h, P * i:T], start=True, stop=True)
                last.then_inc(sem("T_mm"), 1)

            def values(k, p, q):
                b, u, pp = k + q // QUADS, q % QUADS, (p + q // QUADS) % 2
                if not there(b):
                    return
                n = QUADS * k + q
                if u == 0:
                    pe.wait_ge(sem("v_put"), b + 1)
                pe.wait_ge(sem("masked"), n + 1)
                wait(pe, "o_out", n)
                for i in range(NT):
                    for j in range(HQ):
                        last = t.matmul(O_ps[32 * j:32 * j + HD + 1, P * i:T], v_aug[pp][:, i, HQ * u + j, :],
                                        probs[u % 2][:, j, K_AT[i]:K_AT[i] + T - P * i],
                                        start=(i == 0), stop=(i == NT - 1))
                last.then_inc(sem("pv_mm"), 1)

            def transposes(kind, k, u, ready, count, src, done, n=NT):
                if job_index(next(j for j in JOBS if j[0] == kind and j[1] == u), k) is None:
                    return
                pe.wait_ge(sem(ready), count)
                wait_M_free(pe, kind, u, k)
                for i in range(n):
                    last = t.transpose(M_ps[:, i * P:(i + 1) * P], src(i), ident[:])
                last.then_inc(sem(done), 1)

            def run(k, p):
                for u in range(QUADS):
                    for j in range(HQ):
                        scores(k, p, u + 2, j)
                        shifted(k, p, u, j)
                        if j == 0:
                            n = QUADS * k + u - 2
                            transposes("o", k, u, "o_out", n + 1, lambda i: o_sb[:, i * P:(i + 1) * P], "o_tr")
                        if j == 1 and job_index(("max", u, u + 1), k) is not None:
                            n = QUADS * k + u + 1
                            pe.wait_ge(sem("max_made"), n + 1)
                            wait_M_free(pe, "max", u, k)
                            t.transpose(M_ps[0:HQ * NT, 0:P], rowmax[(u + 1) % 2][:].rearrange("p h i -> p (h i)"),
                                        ident[:]).then_inc(sem("max_tr"), 1)
                        if (u, j) == (0, 2):
                            transposes("spk", k, u, "spk_made", k + 3, lambda i: f_spk[:, i * P:(i + 1) * P], "spk_tr")
                        if (u, j) == (0, 3) and there(k - 2):
                            pe.wait_ge(sem("z2T_made"), k - 1)
                            wait_M_free(pe, "route", u, k)
                            for i in range(NT):
                                last = t.matmul(M_ps[:, i * E:(i + 1) * E], b_z2T[:, i * P:(i + 1) * P], wrout[:],
                                                start=True, stop=True)
                            last.then_inc(sem("route_mm"), 1)
                        if (u, j) == (1, 2):
                            transposes("y", k, u, "y_made", QUADS * k, lambda i: b_y[:, i, :], "y_tr")
                        if (u, j) == (1, 3) and there(k - 1):
                            pe.wait_ge(sem("yT_made"), k)
                            for i in range(NT):
                                last = t.matmul(M_ps[:, i * P:(i + 1) * P], b_yT[:, i * P:(i + 1) * P], wproj[:],
                                                start=True, stop=True)
                            last.then_inc(sem("proj_mm"), 1)
                        if (u, j) == (2, 2):
                            transposes("z1", k, u, "z1_made", k + 3, lambda i: f_z[:, i, :], "z1_tr")
                        if (u, j) in ((2, 3), (3, 2)) and there(k + 2):
                            i = u - 2
                            pe.wait_ge(sem("z1T_made"), k + 3)
                            wait_M_free(pe, "qk"[i], u, k)
                            t.matmul(M_ps[:, :], wqkv[:, i * D:(i + 1) * D], f_z1T[:], start=True, stop=True
                                     ).then_inc(sem("qk"[i] + "_mm"), 1)
                        if (u, j) == (3, 3):
                            if there(k + 2):
                                wait_M_free(pe, "v", u, k)
                                for i in range(NT):
                                    last = t.matmul(M_ps[:, i * P:(i + 1) * P], f_z1T[:, i * P:(i + 1) * P],
                                                    wqkv[:, 2 * D:3 * D], start=True, stop=True)
                                last.then_inc(sem("v_mm"), 1)
                            transposes("z2", k, u, "z2_made", k, lambda i: b_z2[:, i, :], "z2_tr")
                    values(k, p, u - 1)

            iterations(run)(pe)

            pe.wait_ge(sem("w12_in"), 32)
            pe.wait_ge(sem("w1_scaled"), 1)
            pe.wait_ge(sem("z2_kept"), B)
            pe.sem_inc(sem("down_mm"), 2)
            with pe.Fori(0, B) as b:
                for e in range(E):
                    H_ps, Y_ps, n = (S_ps, T_ps)[e % 2], (O_ps, M_ps)[e % 2], b * E + e
                    pe.wait_ge(sem("gelu_made"), n + 1)
                    for f in range(FH):
                        last = t.matmul(H_ps[:, f * T:(f + 1) * T], w1_sb[:, (e * FH + f) * P:(e * FH + f + 1) * P],
                                        row_all[:, ds(b), :].rearrange("p o t -> p (o t)"), start=True, stop=True)
                    last.then_inc(sem("up_mm"), 1)
                    pe.wait_ge(sem("gelu_made"), n + 3)
                    pe.wait_ge(sem("acc_made"), n + 1)
                    for i in range(NT):
                        for f in range(FH):
                            last = t.matmul(Y_ps[:, i * P:(i + 1) * P], hid[e % 2][:, f, i * P:(i + 1) * P],
                                            w2_sb[:, e * FH + f, :], start=(f == 0), stop=(f == FH - 1))
                    last.then_inc(sem("down_mm"), 1)

        @block.scalar
        def _(act):
            a = nc.scalar
            act.wait_ge(sem("setup_tr"), 1)
            a.activation(silu_t[:, 0, :], M_ps[:, 0:B], ACT.Exp, scale=-1.0).then_inc(sem("silu_exp"), 1)
            act.wait_ge(sem("weights_in"), 16 * 15)
            a.activation(cols[:, 3:5], cols[:, 3:5], ACT.Exp).then_inc(sem("decay_exp"), 1)
            act.wait_ge(sem("setup_done"), 1)

            def spiking(b, p):
                R_ps = (S_ps, T_ps)[p]
                act.wait_ge(sem("xT_a"), b + 1)
                wait(act, "rkv_a", b - 1)
                col = lambda i: mod_cm[:, i, ds(b)]
                a.activation(a_hT[p], M_ps[:, :], ACT.Identity, bias=col(0), scale=col(1)).then_inc(sem("hT_a"), 1)
                act.wait_ge(sem("rkv_a"), b + 1)
                wait(act, "inp_a", b - 1)
                a.activation(a_er[p], R_ps[:, 0:T], ACT.Exp, bias=BR, scale=-1.0)
                a.activation(a_ek[p], R_ps[:, T:2 * T], ACT.Exp, bias=BK).then_inc(sem("ek_a"), 1)
            spiking(0, 0)
            spiking(1, 1)
            with act.Fori(1, B // 2) as i:
                spiking(i * 2, 0)
                spiking(i * 2 + 1, 1)

            def run(k, p):
                for u in range(QUADS):
                    for j in range(HQ):
                        if there(k):
                            h = HQ * u + j
                            if j == 0:
                                wait(act, "pv_mm", QUADS * k + u - 1)
                            act.wait_ge(sem("T_mm"), HEADS * k + h + 1)
                            a.activation(probs[u % 2][:, j, :], T_ps[:, 0:SCORES], ACT.Exp).then_inc(sem("exp_made"), 1)
                        n = QUADS * k + u + 1
                        if j == 1 and job_index(("max", u, u + 1), k) is not None:
                            act.wait_ge(sem("max_tr"), n + 1)
                            v = (u + 1) % 2
                            wait(act, f"shift_in{v}", (n - v) * 16)
                            a.mul(shift[v][:, 0, :], M_ps[0:HQ * NT, 0:P], -1.0).then_inc(sem("shift_hi"), 1)
                        if (u, j) == (1, 2) and there(k - 1):
                            act.wait_ge(sem("y_tr"), k)
                            wait(act, "proj_mm", k - 1)
                            a.copy(b_yT[:], M_ps[:, :]).then_inc(sem("yT_made"), 1)
                        if (u, j) == (2, 2) and there(k + 2):
                            act.wait_ge(sem("z1_tr"), k + 3)
                            wait(act, "v_mm", k + 2)
                            a.copy(f_z1T[:], M_ps[:, :]).then_inc(sem("z1T_made"), 1)
                        if (u, j) in ((2, 3), (3, 2)) and there(k + 2):
                            i = u - 2
                            act.wait_ge(sem("qk"[i] + "_mm"), k + 3)
                            wait(act, "parts_made", k + 2)
                            a.copy(f_fp[:, i, :], M_ps[:, :]).then_inc(sem("qk"[i] + "_out"), 1)
                        if (u, j) == (3, 3):
                            if there(k + 2):
                                act.wait_ge(sem("v_mm"), k + 3)
                                wait(act, "v_put", k + 2)
                                a.copy(f_v[:].rearrange("p i d -> p (i d)"), M_ps[:, :]).then_inc(sem("v_out"), 1)
                            if there(k - 1):
                                act.wait_ge(sem("z2_tr"), k)
                                wait(act, "route_mm", k - 1)
                                wait(act, "z2_kept", k - 1)
                                a.copy(b_z2T[:], M_ps[:, :]).then_inc(sem("z2T_made"), 1)
                    n = QUADS * k + u - 1
                    if job_index(("o", 0, u - 1), k) is not None:
                        act.wait_ge(sem("pv_mm"), n + 1)
                        wait(act, "o_tr", n)
                        a.copy(o_sb[:], O_ps[:, :]).then_inc(sem("o_out"), 1)

            iterations(run)(act)

            act.wait_ge(sem("margin_made"), 1)
            a.activation(r_e2, r_d, ACT.Exp).then_inc(sem("gates_exp"), 1)
            act.sem_inc(sem("gelu_made"), 2)
            with act.Fori(0, B) as b:
                for e in range(E):
                    H_ps, n = (S_ps, T_ps)[e % 2], b * E + e
                    act.wait_ge(sem("up_mm"), n + 1)
                    act.wait_ge(sem("down_mm"), n + 1)
                    a.activation(hid[e % 2].rearrange("p f t -> p (f t)"), H_ps[:, 0:FH * T], ACT.Gelu
                                 ).then_inc(sem("gelu_made"), 1)

        @block.vector
        def _(dve):
            v = nc.vector
            n_setup = [0]

            def link(ins):
                n_setup[0] += 1
                ins.then_inc(sem("setup_dve"), 1)
                dve.wait_ge(sem("setup_dve"), n_setup[0])

            v.memset(O_ps[:, :], 0.0)
            dve.wait_ge(sem("setup_tr"), 1)
            v.tensor_copy(wT[:].rearrange("p a d -> p (a d)"), S_ps[:, 0:3 * D])
            dve.wait_ge(sem("silu_exp"), 1)
            link(v.tensor_scalar_add(silu_t[:, 1, :], silu_t[:, 0, :], 1.0))
            link(v.reciprocal(silu_t[:, 0, :], silu_t[:, 1, :]))
            v.tensor_tensor(silu_c, M_ps[:, 0:B], silu_t[:, 0, :], ALU.mult).then_inc(sem("silu_made"), 1)
            dve.wait_ge(sem("mod_mm"), 1)

            def gate(dst, src, t1, t2):
                link(v.tensor_scalar(t1, src, 0.0, 2.0, ALU.is_ge, ALU.mult))
                link(v.scalar_tensor_tensor(t2, t1, -1.0, src, ALU.add, ALU.mult))
                link(v.tensor_scalar(t2, t2, GATE_MIN, None, ALU.max))
                link(v.scalar_tensor_tensor(dst, t1, -1.0, t2, ALU.add, ALU.mult))
            v.tensor_copy(mod_cm[:, 0, :], T_ps[:, 0:B])
            v.tensor_scalar_add(mod_cm[:, 1, :], T_ps[:, B:2 * B], 1.0)
            gate(mod_cm[:, 2, :], T_ps[:, 2 * B:3 * B], gate_t[:, 0, :], gate_t[:, 1, :])
            v.tensor_copy(row_t[0:B, 0, :], O_ps[0:B, 0:D])
            v.tensor_scalar_add(row_t[0:B, 1, :], O_ps[0:B, D:2 * D], 1.0)
            gate(row_t[0:B, 2, :], O_ps[0:B, 2 * D:3 * D], row_g[0:B, 0, :], row_g[0:B, 1, :])
            dve.sem_inc(sem("rows_made"), 1)
            dve.wait_ge(sem("decay_exp"), 1)
            v.tensor_scalar_mul(BR, BR, -1.0)
            link(v.tensor_scalar(wqkv[:, 0:D], wqkv[:, 0:D], LN1, 1.0 / math.sqrt(HD), ALU.mult, ALU.mult))
            v.tensor_scalar(wqkv[:, D:3 * D], wqkv[:, D:3 * D], LN1, None, ALU.mult)
            link(v.tensor_scalar(wrout[:], wrout[:], LN2, None, ALU.mult))
            v.memset(O_ps[:, :], 0.0).then_inc(sem("setup_done"), 1)

            def stats(x_t, st, mv, var, name, n, count):
                for i in range(NT):
                    last = v.bn_stats(st[:, i, :], x_t[:, i, :])
                last.then_inc(sem(name + "_c"), 1)
                wait_apart(dve, "dve", name + "_c", 2 * n + 1)
                for i in range(NT):
                    last = v.bn_aggr(mv[:, i, :], st[:, i, :])
                last.then_inc(sem(name + "_c"), 1)
                dve.wait_ge(sem(name + "_c"), 2 * n + 2)
                v.tensor_scalar_add(var, mv[:, :, 1], LN_EPS).then_inc(sem(name), 1)

            def normalise(dst, x_t, mv, rstd):
                for i in range(NT):
                    last = v.tensor_scalar(dst[:, i, :], x_t[:, i, :], mv[:, i, 0:1], rstd[:, i:i + 1],
                                           ALU.subtract, ALU.mult)
                return last

            def stats_a(b, p):
                half_b = b // 2 if isinstance(b, int) else None
                dve.wait_ge(sem(f"x_in{p}"), (b - p) * 8 + 16)
                wait(dve, "rstd_a", b - 1)
                stats(a_x[p], a_stats[p], a_mv[p], a_var[p], "var_a", b, None)

            def xhat_a(b, p):
                dve.wait_ge(sem("rstd_a"), b + 1)
                wait(dve, "xT_a", b - 1)
                normalise(a_xhat[p], a_x[p], a_mv[p], a_rstd[p]).then_inc(sem("xhat_a"), 1)

            def spiking(b, p, more=True):
                R_ps = (S_ps, T_ps)[p]
                if more:
                    stats_a(b + 1, 1 - p)
                dve.wait_ge(sem("ek_a"), b + 1)
                v.scalar_tensor_tensor(a_kv, R_ps[:, 2 * T:3 * T], BV, a_ek[p], ALU.add, ALU.mult
                                       ).then_inc(sem("kv_a"), 1)
                v.tensor_tensor_scan(a_sb, bcast(TD, [P, T]), a_ek[p], 0.0, ALU.mult, ALU.add
                                     ).then_inc(sem("wkv_a"), 1)
                v.tensor_scalar_add(a_er1, a_er[p], 1.0)
                dve.wait_ge(sem("kv_a"), b + 1)
                v.tensor_tensor_scan(a_sa, bcast(TD, [P, T]), a_kv, 0.0, ALU.mult, ALU.add).then_inc(sem("wkv_a"), 1)
                if more:
                    xhat_a(b + 1, 1 - p)
                dve.wait_ge(sem("wkv_a"), 5 * b + 1)
                v.scalar_tensor_tensor(a_den0, a_ek[p], GD, a_sb, ALU.mult, ALU.add).then_inc(sem("wkv_a"), 1)
                dve.wait_ge(sem("wkv_a"), 5 * b + 2)
                v.scalar_tensor_tensor(a_num, a_kv, GD, a_sa, ALU.mult, ALU.add)
                dve.wait_ge(sem("wkv_a"), 5 * b + 3)
                v.scalar_tensor_tensor(a_den, a_den0, WKV_EPS, a_er1, ALU.add, ALU.mult).then_inc(sem("wkv_a"), 1)
                dve.wait_ge(sem("wkv_a"), 5 * b + 4)
                v.reciprocal(a_rec, a_den).then_inc(sem("wkv_a"), 1)
                dve.wait_ge(sem("wkv_a"), 5 * b + 5)
                v.scalar_tensor_tensor(row_all[:, ds(b), :].rearrange("p o t -> p (o t)"), a_num, 1.0 / THRESH, a_rec,
                                       ALU.mult, ALU.mult).then_inc(sem("inp_a"), 1)

            stats_a(0, 0)
            xhat_a(0, 0)
            spiking(0, 0)
            spiking(1, 1)
            with dve.Fori(1, B // 2 - 1) as i:
                spiking(i * 2, 0)
                spiking(i * 2 + 1, 1)
            spiking(B - 2, 0)
            spiking(B - 1, 1, more=False)

            dve.wait_ge(sem("inp_a"), B)
            v.memset(m_out[:, :, U - 1], 0.0).then_inc(sem("mem"), 1)
            with dve.Fori(0, T // U) as turn:
                done = turn * (2 * U + 2)
                wait_apart(dve, "dve", "mem", done + 1)
                v.tensor_copy(m_in, row_all[:, :, bass.ds(turn * U, U)]).then_inc(sem("mem"), 1)
                dve.wait_ge(sem("mem"), done + 2)
                for j in range(U):
                    prev = m_out[:, :, (j - 1) % U]
                    v.scalar_tensor_tensor(m_tmp, prev, 1.0, m_in[:, :, j], ALU.is_gt, ALU.subtract
                                           ).then_inc(sem("mem"), 1)
                    dve.wait_ge(sem("mem"), done + 2 * j + 3)
                    v.scalar_tensor_tensor(m_out[:, :, j], prev, BETA, m_tmp, ALU.mult, ALU.subtract
                                           ).then_inc(sem("mem"), 1)
                    if j < U - 1:
                        dve.wait_ge(sem("mem"), done + 2 * j + 4)
                wait_apart(dve, "dve", "mem", done + 2 * U + 2)
                v.tensor_copy(row_all[:, :, bass.ds(turn * U, U)], m_out).then_inc(sem("mem"), 1)
            dve.wait_ge(sem("mem"), 1 + (T // U) * (2 * U + 2))

            def row(b):
                return row_all[:, ds(b), :].rearrange("p o t -> p (o t)")

            def run(k, p):
                if there(k + 2):
                    wait(dve, "spk_tr", k + 2)
                    v.tensor_scalar(f_spk[:], row(k + 2), 1.0, mod_cm[:, 2, ds(k + 2)], ALU.is_gt, ALU.mult
                                    ).then_inc(sem("spk_made"), 1)
                for u in range(QUADS):
                    s_b, s_u = k + (u + 2) // QUADS, (u + 2) % QUADS
                    for j in range(HQ):
                        if there(s_b):
                            dve.wait_ge(sem("S_mm"), HEADS * s_b + HQ * s_u + j + 1)
                            v.tensor_reduce(blkmax[u % 2][:, j, :],
                                            S_ps[:, 0:SCORES].rearrange("p (n t) -> p n t", n=NBLK), AX.X, ALU.max
                                            ).then_inc(sem("blk_made"), 1)
                        if j == 1:
                            if job_index(("o", u, u - 2), k) is not None:
                                n = QUADS * k + u - 2
                                h0 = HQ * ((u - 2) % QUADS)
                                dve.wait_ge(sem("o_tr"), n + 1)
                                heads = M_ps[:, :].rearrange("p (i h w) -> p i h w", i=NT, h=HQ)
                                v.reciprocal(o_rec[:], heads[:, :, :, HD]).then_inc(sem("o_rec"), 1)
                                dve.wait_ge(sem("o_rec"), n + 1)
                                if u == 2:
                                    wait(dve, "y_tr", k)
                                v.tensor_tensor(b_y[:, :, h0 * HD:(h0 + HQ) * HD].rearrange("p i (h d) -> p i h d", h=HQ),
                                                heads[:, :, :, 0:HD],
                                                bcast(o_rec[:].rearrange("p i (h o) -> p i h o", o=1), [P, NT, HQ, HD]),
                                                ALU.mult).then_inc(sem("y_made"), 1)
                            if job_index(("max", u, u + 1), k) is not None:
                                n = QUADS * k + u + 1
                                w = (u + 1) % 2
                                dve.wait_ge(sem("shift_hi"), n + 1)
                                v.scalar_tensor_tensor(shift[w][:, 1, :], M_ps[0:HQ * NT, 0:P], -1.0, shift[w][:, 0, :],
                                                       ALU.mult, ALU.subtract).then_inc(sem("shift_made"), 1)
                        if (u, j) == (0, 2) and there(k + 2):
                            b = k + 2
                            dve.wait_ge(sem("spk_tr"), b + 1)
                            dve.wait_ge(sem("x_in_f"), 32 * (b + 1))
                            wait(dve, "x1_saved", 16 * b)
                            v.tensor_tensor(f_x1[:], f_x[:], M_tiles, ALU.add).then_inc(sem("x1_made"), 1)
                            dve.wait_ge(sem("x1_made"), b + 1)
                            stats(f_x1, ln_stats[0], ln_mv[0], ln_var[0][:], "var0", b, None)
                        if (u, j) == (0, 3):
                            if there(k - 2):
                                wait_apart(dve, "dve", "route_mm", k - 1)
                                v.tensor_copy(logits_all[:, ds(k - 2), :, :].rearrange("p o i e -> p (o i e)"),
                                              M_ps[:, 0:NT * E]).then_inc(sem("logits_made"), 1)
                            if there(k + 2):
                                dve.wait_ge(sem("rstd0"), k + 3)
                                wait(dve, "z1_tr", k + 2)
                                normalise(f_z, f_x1, ln_mv[0], ln_rstd[0]).then_inc(sem("z_made"), 1)
                        if (u, j) == (1, 2) and there(k + 2):
                            dve.wait_ge(sem("h_made"), k + 3)
                            stats(f_h, ln_stats[1], ln_mv[1], ln_var[1][:], "var1", k + 2, None)
                        if (u, j) == (1, 3) and there(k + 2):
                            dve.wait_ge(sem("rstd1"), k + 3)
                            normalise(f_z, f_h, ln_mv[1], ln_rstd[1]).then_inc(sem("z1_made"), 1)
                        if (u, j) == (2, 0) and there(k - 1):
                            b = k - 1
                            dve.wait_ge(sem("proj_mm"), b + 1)
                            dve.wait_ge(sem("h_kept"), b + 1)
                            wait(dve, "base_made", b)
                            v.tensor_tensor(b_x2[:].rearrange("p i d -> p (i d)"), row(b), M_ps[:, :], ALU.add
                                            ).then_inc(sem("x2_made"), 1)
                            dve.wait_ge(sem("x2_made"), b + 1)
                            stats(b_x2, ln_stats[2], ln_mv[2], ln_var[2][:], "var2", b, None)
                        if (u, j) == (2, 2) and there(k - 1):
                            dve.wait_ge(sem("rstd2"), k)
                            wait(dve, "z2_tr", k - 1)
                            normalise(b_z2, b_x2, ln_mv[2], ln_rstd[2]).then_inc(sem("z2_made"), 1)
                    if there(s_b):
                        n = QUADS * s_b + s_u
                        dve.wait_ge(sem("blk_made"), HQ * n + HQ)
                        wait(dve, "max_tr", n - 1)
                        bm, rm = blkmax[u % 2], rowmax[u % 2]
                        v.tensor_reduce(rm[:, :, 3], bm[:, :, 0:4], AX.X, ALU.max)
                        v.tensor_reduce(rm[:, :, 2], bm[:, :, 4:7], AX.X, ALU.max)
                        v.tensor_copy(rm[:, :, 0], bm[:, :, 7])
                        v.tensor_reduce(rm[:, :, 1], bm[:, :, 8:10], AX.X, ALU.max).then_inc(sem("max_made"), 1)

            iterations(run)(dve)

            n_route = [0]

            def chain(ins):
                n_route[0] += 1
                ins.then_inc(sem("routing"), 1)
                dve.wait_ge(sem("routing"), n_route[0])

            dve.wait_ge(sem("z2_kept"), B)
            dve.wait_ge(sem("logits_made"), B)
            lg = logits_all[:].rearrange("p b i e -> p (b i) e")

            def wide(col):
                return bcast(col.rearrange("p (n o) -> p n o", o=1), [P, NL, E])
            for e in range(E):
                last = v.memset(place[:, e:e + 1], float(E - e))
            chain(last)
            places = bcast(place.rearrange("p (o e) -> p o e", o=1), [P, NL, E])

            def first_max(src, mx, first, onehot):
                chain(v.tensor_reduce(mx, src, AX.X, ALU.max))
                chain(v.tensor_tensor(r_eq, src, wide(mx), ALU.is_equal))
                chain(v.tensor_tensor(r_k, r_eq, places, ALU.mult))
                chain(v.tensor_reduce(first, r_k, AX.X, ALU.max))
                chain(v.tensor_tensor(onehot, places, wide(first), ALU.is_equal))
            first_max(lg, r_m1, r_f1, r_o1)
            chain(v.scalar_tensor_tensor(r_l2, r_o1, MASKED, lg, ALU.mult, ALU.add))
            first_max(r_l2, r_m2, r_f2, r_o2)
            v.tensor_tensor(r_d, r_m2, r_m1, ALU.subtract).then_inc(sem("margin_made"), 1)
            dve.wait_ge(sem("gates_exp"), 1)
            chain(v.tensor_scalar_add(r_s, r_e2, 1.0))
            chain(v.reciprocal(r_r1, r_s))
            chain(v.tensor_tensor(r_r2, r_r1, r_e2, ALU.mult))
            chain(v.tensor_tensor(r_eq, r_o1, wide(r_r1), ALU.mult))
            chain(v.tensor_tensor(r_k, r_o2, wide(r_r2), ALU.mult))
            chain(v.tensor_tensor(rw, r_eq, r_k, ALU.add))

            dve.wait_ge(sem("w12_in"), 32)
            v.tensor_scalar(w1_sb, w1_sb, LN2, None, ALU.mult).then_inc(sem("w1_scaled"), 1)
            dve.sem_inc(sem("acc_made"), 2)
            with dve.Fori(0, B) as b:
                v.tensor_copy(rw_b, rw[:, bass.ds(b * NT, NT), :]).then_inc(sem("rw_b"), 1)
                dve.wait_ge(sem("rw_b"), b + 1)
                for e in range(E):
                    Y_ps, n = (O_ps, M_ps)[e % 2], b * E + e
                    dve.wait_ge(sem("down_mm"), n + 3)
                    if e:
                        dve.wait_ge(sem("acc_made"), n + 2)
                    for i in range(NT):
                        y, w = Y_ps[:, i * P:(i + 1) * P], rw_b[:, i, e:e + 1]
                        if e == 0:
                            last = v.tensor_scalar(acc[:, i, :], y, w, None, ALU.mult)
                        else:
                            last = v.scalar_tensor_tensor(acc[:, i, :], y, w, acc[:, i, :], ALU.mult, ALU.add)
                    last.then_inc(sem("acc_made"), 1)
                dve.wait_ge(sem("acc_made"), b * E + E + 2)
                dve.wait_ge(sem("base_in"), b * 32 + 32)
                v.tensor_tensor(acc, acc, bcast(gate_c.rearrange("p (o d) -> p o d", o=1), [P, NT, D]), ALU.mult
                                ).then_inc(sem("gated_c"), 1)
                dve.wait_ge(sem("gated_c"), b + 1)
                v.tensor_tensor(base_c, base_c, acc, ALU.add).then_inc(sem("out_made"), 1)


_INS = ['x', 'W_r', 'b_r', 'W_k', 'b_k', 'W_v', 'b_v', 'W_td', 'b_td', 'global_decay']
_FFN = ['ln1_w', 'c_attn_w', 'c_proj_w', 'ln2_w', 'router_w', 'w1', 'w2']
_NAMES = ['L0_attn_' + n for n in _INS] + ['L0_ffn_' + n for n in _FFN] + ['L0_c', 'L0_wmod']


def kernel(**inputs):
    import numpy as _np
    import concourse.bacc as _bacc
    from concourse import mybir as _mybir
    from concourse.bass_utils import run_bass_kernel_spmd as _run

    nc = _bacc.Bacc("TRN2", target_bir_lowering=False, num_devices=1)
    arrays, args = {}, []
    for name in _NAMES:
        a = _np.ascontiguousarray(inputs[name])
        arrays[f"in_{name}_dram"] = a
        args.append(nc.dram_tensor(f"in_{name}_dram", a.shape, _mybir.dt.from_np(a.dtype), kind="ExternalInput").ap())
    shape = inputs['L0_attn_x'].shape
    out = nc.dram_tensor("out_0_dram", shape, _mybir.dt.float32, kind="ExternalOutput").ap()
    adaln_spiking_moe_layer(nc, *args, out)
    r = _run(nc, [arrays], core_ids=[0])
    return r.results[0]["out_0_dram"]
```

```python
import math

import concourse.bass as bass
from concourse import mybir
from contextlib import ExitStack

FP32 = mybir.dt.float32
I32 = mybir.dt.int32
BF16 = mybir.dt.bfloat16
ALU = mybir.AluOpType
ACT = mybir.ActivationFunctionType
AX = mybir.AxisListType

THRESH = 0.05
BETA = 0.3
WKV_EPS = 1e-6
LN_EPS = 1e-5
GATE_MIN = 0.25
MASKED = -3.0e38


def adaln_spiking_moe_layer(nc, x, W_r, b_r, W_k, b_k, W_v, b_v, W_td, b_td, global_decay, ln1_w, c_attn_w,
                            c_proj_w, ln2_w, router_w, w1, w2, c, wmod, out):
    B, T, D = x.shape
    P = 128
    NT = T // P
    HEADS, HD = 16, 8
    QUADS = 4
    HQ = HEADS // QUADS
    E = router_w.shape[1]
    F = w1.shape[1] // E
    FH = F // P
    SCORES = P * NT * (NT + 1) // 2
    NBLK = NT * (NT + 1) // 2
    TERMS = 6
    SPLIT = 3
    PROD = TERMS * HD
    SHIFT = 96
    U = 32
    Q_AT = {3: 0, 2: 512, 0: 896, 1: 1024}
    K_AT = {0: 0, 1: 512, 3: 896, 2: 1024}


    TOK = B * T
    LISTS = 2 * E
    TS = 2 * P
    NS = TS // P
    CAP = TOK + TS
    ROW = 2 * D + 4
    NUM = 2 * D
    HALF = TOK // TS + E
    TILES = 2 * HALF
    TURN = 8
    AHEAD = 2
    SPARE = LISTS + AHEAD
    FILL = E
    assert out.shape[0] == TOK + (FILL + SPARE) * TS

    lists = nc.dram_tensor("lists", [LISTS * CAP + SPARE * TS, ROW], FP32).ap()
    mod_rows = nc.dram_tensor("mod_rows", [B, 3, D], FP32).ap()
    mid = nc.dram_tensor("mid", [B, P, NT, D], FP32).ap()
    q_terms = [nc.dram_tensor(f"q_terms{i}", [D, TERMS, T], BF16).ap() for i in range(2)]
    k_terms = [nc.dram_tensor(f"k_terms{i}", [D, TERMS, T], BF16).ap() for i in range(2)]
    x_v = x.rearrange("b (i p) d -> b p i d", p=P)
    out_v = out[0:TOK, :].rearrange("(b i p) d -> b p i d", p=P, i=NT)

    ctx = ExitStack()
    with ctx:
        def sb(name, shape, dt=FP32):
            return ctx.enter_context(nc.sbuf_tensor(name, shape, dt))

        def pb(name, shape):
            return ctx.enter_context(nc.psum_tensor(name, shape, FP32))

        sems = {}

        def sem(name):
            if name not in sems:
                sems[name] = ctx.enter_context(nc.semaphore(name))
            return sems[name]

        def wait(eng, name, value):
            if not isinstance(value, int) or value > 0:
                eng.wait_ge(sem(name), value)

        def wait_apart(eng, who, name, value):
            wait(eng, name, value)
            if not isinstance(value, int):
                eng.sem_inc(sem(f"{who}_passed"), 1)

        def ds(b):
            return slice(b, b + 1) if isinstance(b, int) else bass.ds(b, 1)

        def dram(ap, b):
            return ap[ds(b)].rearrange("o p i d -> (o p) i d")

        row_all = sb("row_all", [P, B, T])
        ident = sb("ident", [P, P])
        ident_h = sb("ident_h", [P, P], BF16)
        causal = sb("causal", [P, P], BF16)
        half = sb("half", [P, NT])
        wT = sb("wT", [P, 3, D])
        wqkv = sb("wqkv", [P, 3 * D])
        wproj = sb("wproj", [P, D])
        wrout = sb("wrout", [P, E])
        cols = sb("cols", [P, 8])
        BR, BK, BV, TD, GD, LN1, LN2 = (cols[:, i:i + 1] for i in range(7))
        mod_cm = sb("mod_cm", [P, 3, B])

        ARENA = 26 * 1024
        arena = sb("arena", [P, ARENA])

        def carver():
            at = [0]

            def take(n, dt=FP32):
                words = n if dt == FP32 else n // 2
                v = arena[:, at[0]:at[0] + words]
                at[0] += words
                assert at[0] <= ARENA, at[0]
                return v if dt == FP32 else v.bitcast(dt)
            return take

        take = carver()
        c_in = take(D)
        wmod_in = take(6 * D)
        w_in = take(3 * D).rearrange("p (a d) -> p a d", a=3)
        silu_c = take(B)
        silu_t = take(2 * B).rearrange("p (a b) -> p a b", a=2)
        gate_t = take(2 * B).rearrange("p (a b) -> p a b", a=2)
        row_t = take(3 * D).rearrange("p (a d) -> p a d", a=3)
        row_g = take(2 * D).rearrange("p (a d) -> p a d", a=2)

        def two(n):
            return [take(n) for _ in range(2)]

        a_x = [v.rearrange("p (i d) -> p i d", i=NT) for v in two(T)]
        a_stats = [v.rearrange("p (i s) -> p i s", i=NT) for v in two(NT * 6)]
        a_mv = [v.rearrange("p (i s) -> p i s", i=NT) for v in two(NT * 2)]
        a_var = two(NT)
        a_rstd = two(NT)
        a_xhat = [v.rearrange("p (i d) -> p i d", i=NT) for v in two(T)]
        a_hT = two(T)
        a_ek = two(T)
        a_er = two(T)
        a_er1, a_kv, a_sa, a_sb, a_num, a_den0, a_den, a_rec = (take(T) for _ in range(8))

        take = carver()
        q_stack = [take(HEADS * T, BF16).rearrange("p (h t) -> p h t", h=HEADS) for _ in range(2)]
        k_stack = [take(HEADS * T, BF16).rearrange("p (h t) -> p h t", h=HEADS) for _ in range(2)]
        probs = [take(HQ * SCORES).rearrange("p (h s) -> p h s", h=HQ) for _ in range(2)]

        take = carver()
        w_all = take(E * 2 * FH * P).rearrange("p (e w) -> p e w", e=E)
        w_tile = [take(2 * FH * P) for _ in range(4)]
        x_tile = [take(NS * ROW).rearrange("p (i w) -> p i w", i=NS) for _ in range(TURN)]
        xT_tile = [take(TS) for _ in range(2)]
        hid = [take(FH * TS).rearrange("p (f t) -> p f t", f=FH) for _ in range(2)]
        res = [take(TS).rearrange("p (i d) -> p i d", i=NS) for _ in range(TURN)]
        NTAB = TILES + AHEAD
        t_ge, t_lt, t_in, t_at, t_row = (take(NTAB * LISTS).rearrange("p (t l) -> p t l", l=LISTS) for _ in range(5))
        t_no, t_first, t_rows, t_sum, t_free, t_spare = (take(NTAB) for _ in range(6))
        n_gt = take(LISTS * (TOK // TS)).rearrange("p (l j) -> p l j", l=LISTS)
        n_cnt, n_tiles, n_exc, n_end, n_first, n_exp, l_cap = (take(LISTS) for _ in range(7))
        n_used = take(4)
        fill_rows = take(FILL * NS * ROW).rearrange("p (n w) -> p n w", w=ROW)

        v_aug = [sb(f"v_aug{i}", [P, NT, HEADS, HD + 1]) for i in range(2)]

        def buf(name):
            return sb(name, [P, NT, D])

        f_x, f_x1, f_z, f_h, b_y, b_x2, b_x1 = (buf(n) for n in (
            "f_x", "f_x1", "f_z", "f_h", "b_y", "b_x2", "b_x1"))
        f_spk = sb("f_spk", [P, T])
        f_z1T = f_spk
        f_fp = sb("f_fp", [P, 2, T])
        f_parts = sb("f_parts", [P, 2, SPLIT, T], BF16)
        f_v = sb("f_v", [P, NT, D])
        f_mod = sb("f_mod", [P, 2, D])
        b_gate = [sb(f"b_gate{i}", [P, D]) for i in range(2)]
        rows = [[sb(f"rows{i}{c}", [P, NT, ROW]) for c in range(2)] for i in range(2)]
        place = sb("place", [P, E])
        r_lg = sb("r_lg", [P, NT, E])
        r_l2 = sb("r_l2", [P, NT, E])
        r_eq = sb("r_eq", [P, NT, E])
        r_k = sb("r_k", [P, NT, E])
        r_m = sb("r_m", [P, 2, NT])
        r_f = sb("r_f", [P, NT])
        r_d = sb("r_d", [P, NT])
        r_e2 = sb("r_e2", [P, NT])
        r_s = sb("r_s", [P, NT])
        r_w = sb("r_w", [P, 2, NT])
        r_one = sb("r_one", [P, NT, 2, E])
        r_oneh = sb("r_oneh", [P, NT, 2 * E], BF16)
        r_pos = sb("r_pos", [P, NT, 2 * E])
        r_hit = sb("r_hit", [P, NT, 2 * E])
        r_row = sb("r_row", [P, NT, 2])
        r_slot = sb("r_slot", [P, NT, 2], I32)
        r_next = sb("r_next", [P, 2 * E])
        before = sb("before", [P, P], BF16)
        ones_h = sb("ones_h", [P, P], BF16)
        zero_row = sb("zero_row", [P, NUM])[:]
        spare_no = sb("spare_no", [P, SPARE * NS, 4], I32)
        two_T = sb("two_T", [P, NT], I32)
        tile_no = sb("tile_no", [1, NTAB], I32)
        tab = sb("tab", [1, 2 * NTAB + LISTS], I32)
        b_yT = sb("b_yT", [P, T])
        b_z2T = b_yT
        ln_stats = [sb(f"ln_stats{i}", [P, NT, 6]) for i in range(3)]
        ln_mv = [sb(f"ln_mv{i}", [P, NT, 2]) for i in range(3)]
        ln_var = [sb(f"ln_var{i}", [P, NT]) for i in range(3)]
        ln_rstd = [sb(f"ln_rstd{i}", [P, NT]) for i in range(3)]
        blkmax = [sb(f"blkmax{i}", [P, HQ, NBLK]) for i in range(2)]
        rowmax = [sb(f"rowmax{i}", [P, HQ, NT]) for i in range(2)]
        shift = [sb(f"shift{i}", [HQ * NT, 2, P], BF16) for i in range(2)]
        o_sb = sb("o_sb", [P, T])
        o_rec = sb("o_rec", [P, NT, HQ])
        m_in = f_fp[:, 0, 0:B * U].rearrange("p (b u) -> p b u", b=B)
        m_out = f_fp[:, 1, 0:B * U].rearrange("p (b u) -> p b u", b=B)
        m_tmp = b_gate[0][:, 0:B]

        S_ps = pb("S_ps", [P, 3 * 512])
        T_ps = pb("T_ps", [P, 3 * 512])
        O_ps = pb("O_ps", [P, 512])
        M_ps = pb("M_ps", [P, 512])
        M_tiles = M_ps[:, :].rearrange("p (i d) -> p i d", i=NT)

        def bcast(ap, shape):
            return ap.broadcast_to(shape)

        JOBS = [("o", 0, -2), ("max", 0, 1), ("spk", 0, 2), ("route", 0, -2),
                ("o", 1, -1), ("max", 1, 2), ("y", 1, -1), ("proj", 1, -1),
                ("rank", 2, -2), ("o", 2, 0), ("max", 2, 3), ("z1", 2, 2), ("q", 2, 2),
                ("o", 3, 1), ("max", 3, 4), ("k", 3, 2), ("v", 3, 2), ("z2", 3, -1)]
        READER = {"o": "y_made", "max": "shift_made", "spk": "x1_made", "route": "logits_made", "y": "yT_made",
                  "proj": "x2_made", "z1": "z1T_made", "q": "q_out", "k": "k_out", "v": "v_out", "z2": "z2T_made", "rank": "pos_made"}
        PER_QUAD = ("o", "max")

        def job_index(job, k):
            kind, _, lag = job
            n = QUADS * k + lag if kind in PER_QUAD else k + lag
            last = QUADS * B if kind in PER_QUAD else B
            return n if not isinstance(k, int) or 0 <= n < last else None

        def wait_M_free(eng, kind, u, k):
            at = next(i for i, j in enumerate(JOBS) if j[0] == kind and j[1] == u)
            back = 0
            while True:
                at -= 1
                if at < 0:
                    at, back = len(JOBS) - 1, back + 1
                if back > 2:
                    return
                n = job_index(JOBS[at], k - back)
                if n is not None:
                    wait(eng, READER[JOBS[at][0]], n + 1)
                    return

        def there(b):
            return not isinstance(b, int) or 0 <= b < B

        def iterations(run):
            def program(eng):
                for k in range(-2, 4):
                    run(k, k % 2)
                with eng.Fori(2, B // 2 - 1) as i:
                    run(i * 2, 0)
                    run(i * 2 + 1, 1)
                for k in range(B - 2, B + 2):
                    run(k, k % 2)
            return program

        def fill_up(eng, choice):
            eng.wait_ge(sem("fill_set"), 1)
            eng.wait_ge(sem("tab_made"), 1)
            for e in range(E):
                i = choice * E + e
                end = eng.value_load(tab[0:1, 2 * NTAB + i:2 * NTAB + i + 1], min_val=i * CAP, max_val=i * CAP + TOK)
                eng.dma_start(lists[bass.ds(end, TS), :].rearrange("(i p) w -> p i w", p=P),
                              fill_rows[:, e * NS:(e + 1) * NS, :]).then_inc(sem("filled"), 16)

        block = ctx.enter_context(nc.Block())

        @block.sync
        def _(sp):
            for dst, src in ((c_in[0:B, :], c), (wmod_in, wmod), (w_in[:, 0], W_r), (w_in[:, 1], W_k), (w_in[:, 2], W_v),
                             (wqkv[:], c_attn_w), (wproj[:], c_proj_w), (wrout[:], router_w)):
                sp.dma_start(dst, src).then_inc(sem("weights_in"), 16)
            for i, v in enumerate((b_r, b_k, b_v, b_td, global_decay, ln1_w, ln2_w)):
                sp.dma_start(cols[:, i:i + 1], v.rearrange("(p o) -> p o", o=1)).then_inc(sem("weights_in"), 16)
            sp.wait_ge(sem("rows_made"), 1)
            sp.dma_start(mod_rows, row_t[0:B]).then_inc(sem("rows_saved"), 16)
            sp.wait_ge(sem("rows_saved"), 16)
            sp.wait_ge(sem("spare_set"), 2)
            sp.dma_start(out[TOK:TOK + (FILL + SPARE) * TS, :].rearrange("(n p i) d -> p n (i d)", p=P, i=NS),
                         bcast(zero_row.rearrange("p (o w) -> p o w", o=1), [P, FILL + SPARE, TS])
                         ).then_inc(sem("spare_saved"), 16)
            free = lists[LISTS * CAP:LISTS * CAP + SPARE * TS, :].rearrange("(n p) w -> p n w", p=P)
            sp.dma_start(free[:, :, 0:NUM], bcast(zero_row.rearrange("p (o w) -> p o w", o=1), [P, SPARE * NS, NUM])
                         ).then_inc(sem("spare_saved"), 16)
            sp.dma_start(free[:, :, NUM:ROW].bitcast(I32), spare_no[:]
                         ).then_inc(sem("spare_saved"), 16)

            def load_x(b, p):
                wait_apart(sp, "sp", "xhat_a", b - 1)
                sp.dma_start(a_x[p], dram(x_v, b)).then_inc(sem(f"x_in{p}"), 16)
            load_x(0, 0)
            load_x(1, 1)
            with sp.Fori(1, B // 2) as i:
                load_x(i * 2, 0)
                load_x(i * 2 + 1, 1)

            def shift_rows(k, p, q):
                n = QUADS * k + q
                b, u, pp = k + q // QUADS, q % QUADS, (p + q // QUADS) % 2
                if there(b):
                    wait_apart(sp, "sp", "shift_made", n + 1)
                    for r in range(2):
                        dst = q_stack[pp][SHIFT + r:SHIFT + r + 1, HQ * u:HQ * (u + 1), :]
                        sp.dma_start(dst.rearrange("o h (i t) -> o (h i) t", i=NT),
                                     shift[u % 2][:, r, :]).then_inc(sem(f"shift_in{u % 2}"), 16)

            def run(k, p):
                if there(k + 2):
                    load_front(k + 2)
                shift_rows(k, p, 1)
                if there(k + 1):
                    b, pp = k + 1, 1 - p
                    wait_apart(sp, "sp", "parts_made", b + 1)
                    wait_apart(sp, "sp", "stacks_in", 32 * (b - 1))
                    q1, q2, q3 = (f_parts[:, 0, i:i + 1, :] for i in range(3))
                    sp.dma_start(q_terms[pp][:, 0:3], bcast(q1, [D, 3, T])).then_inc(sem("terms_out"), 16)
                    sp.dma_start(q_terms[pp][:, 3:5], bcast(q2, [D, 2, T])).then_inc(sem("terms_out"), 16)
                    sp.dma_start(q_terms[pp][:, 5:6], q3).then_inc(sem("terms_out"), 16)
                    sp.dma_start(k_terms[pp][:, 0:3], f_parts[:, 1, 0:3]).then_inc(sem("terms_out"), 16)
                    sp.dma_start(k_terms[pp][:, 3:5], f_parts[:, 1, 0:2]).then_inc(sem("terms_out"), 16)
                    sp.dma_start(k_terms[pp][:, 5:6], f_parts[:, 1, 0:1]).then_inc(sem("terms_out"), 16)
                    wait_apart(sp, "sp", "terms_out", 96 * (b + 1))
                    wait_apart(sp, "sp", "T_mm", HEADS * (b - 1))
                    if isinstance(b, int) and b < 2:
                        sp.wait_ge(sem("pads_set"), 1)
                    for stack, terms in ((q_stack[pp], q_terms[pp]), (k_stack[pp], k_terms[pp])):
                        sp.dma_start(stack[0:PROD], terms.rearrange("(h d) s t -> (d s) h t", d=HD)
                                     ).then_inc(sem("stacks_in"), 16)
                if there(k + 2):
                    wait_apart(sp, "sp", "x1_made", k + 3)
                    sp.dma_start(dram(mid, k + 2), f_x1[:]).then_inc(sem("x1_saved"), 16)
                shift_rows(k, p, 2)
                if there(k - 1):
                    b = k - 1
                    wait_apart(sp, "sp", "base_out", 16 * b)
                    wait_apart(sp, "sp", "x1_saved", 16 * (b + 1))
                    wait_apart(sp, "sp", "rows_gated", b - 1)
                    sp.dma_start(b_x1[:], dram(mid, b)).then_inc(sem("x1_back"), 16)
                    sp.dma_start(b_gate[1 - p][:], bcast(mod_rows[ds(b), 2, :], [P, D])).then_inc(sem("x1_back"), 16)
                shift_rows(k, p, 3)
                shift_rows(k, p, 4)
                if there(k - 1):
                    wait_apart(sp, "sp", "base_made", k)
                    sp.dma_start(dram(out_v, k - 1), b_x1[:]).then_inc(sem("base_out"), 16)

            def load_front(b):
                wait_apart(sp, "sp", "x1_made", b)
                sp.dma_start(f_x[:], dram(x_v, b)).then_inc(sem("x_in_f"), 16)
                wait_apart(sp, "sp", "h_made", b)
                sp.dma_start(f_mod[:], bcast(mod_rows[ds(b), 0:2, :], [P, 2, D])).then_inc(sem("x_in_f"), 16)

            iterations(run)(sp)
            sp.wait_ge(sem("base_out"), 16 * B)

            sp.wait_ge(sem("pv_mm"), QUADS * B)
            sp.wait_ge(sem("T_mm"), HEADS * B)
            sp.dma_start(w_all[:, :, 0:F], w1.rearrange("c (e f) -> c e f", e=E)).then_inc(sem("w12_in"), 16)
            for f in range(FH):
                sp.dma_start(w_all[:, :, F + f * D:F + (f + 1) * D],
                             w2.rearrange("(e f p) d -> f p e d", p=P, f=FH)[f]).then_inc(sem("w12_in"), 16)
            sp.wait_ge(sem("listed"), 16 * 2 * NT * B)
            fill_up(sp, 0)
            sp.wait_ge(sem("filled"), 16 * LISTS)
            sp.wait_ge(sem("spare_saved"), 48)

            def load_tile(t, r):
                row = sp.value_load(tab[0:1, ds(t)], min_val=0, max_val=LISTS * CAP + (SPARE - 1) * TS)
                if not (isinstance(t, int) and t < TURN):
                    wait_apart(sp, "sp", f"res_saved{r}", 16 * NS * (t // TURN if isinstance(t, int) else t_turn[0]))
                sp.dma_start(x_tile[r], lists[bass.ds(row, TS), :].rearrange("(i p) w -> p i w", p=P)
                             ).then_inc(sem(f"x_tile_in{r}"), 16)
            t_turn = [None]
            for r in range(TURN):
                load_tile(r, r)
            with sp.Fori(1, TILES // TURN) as i:
                t_turn[0] = i
                for r in range(TURN):
                    load_tile(i * TURN + r, r)
            for t in range(TILES, NTAB):
                load_tile(t, t % TURN)

        @block.gpsimd
        def _(pool):
            g = nc.gpsimd
            g.memset(ident[:], 0.0).then_inc(sem("id0"), 1)
            g.memset(half[:], -0.5).then_inc(sem("half_set"), 1)
            g.memset(m_tmp, 0.0)
            g.memset(causal[:], 0.0).then_inc(sem("id0"), 1)
            pool.wait_ge(sem("id0"), 2)
            g.affine_select(out=ident[:], in_=ident[:], compare_op=ALU.not_equal, fill=1.0, base=0,
                            pattern=[[-1, P]], channel_multiplier=1).then_inc(sem("id1"), 1)
            g.affine_select(out=causal[:], in_=causal[:], compare_op=ALU.is_ge, fill=MASKED, base=0,
                            pattern=[[-1, P]], channel_multiplier=1).then_inc(sem("id1"), 1)
            pool.wait_ge(sem("id1"), 2)
            g.tensor_copy(ident_h[:], ident[:]).then_inc(sem("consts"), 1)
            g.memset(ones_h[:], 1.0).then_inc(sem("tri0"), 1)
            pool.wait_ge(sem("tri0"), 1)
            g.affine_select(out=before[:], in_=ones_h[:], compare_op=ALU.is_gt, fill=0.0, base=0,
                            pattern=[[1, P]], channel_multiplier=-1)
            g.iota(spare_no[:], [[P, SPARE * NS], [0, 4]], base=TOK + FILL * TS, channel_multiplier=1
                   ).then_inc(sem("spare_set"), 1)
            g.memset(zero_row, 0.0).then_inc(sem("spare_set"), 1)
            for i in range(2):
                for c in range(2):
                    g.memset(rows[i][c][:, :, NUM:ROW], 0.0).then_inc(sem("row_no"), 1)
            pool.wait_ge(sem("row_no"), 4)
            for i in range(2):
                for c in range(2):
                    g.iota(rows[i][c][:, :, NUM].bitcast(I32), [[P, NT]], base=(i - 2) * T, channel_multiplier=1)
            g.iota(two_T[:], [[0, NT]], base=2 * T, channel_multiplier=0).then_inc(sem("row_no"), 1)
            for v in v_aug:
                g.memset(v[:, :, :, HD:HD + 1], 1.0).then_inc(sem("ones_set"), 1)
            g.iota(tile_no[:], [[1, NTAB]], base=0, channel_multiplier=0).then_inc(sem("tiles_counted"), 1)

            pool.wait_ge(sem("half_set"), 1)

            def rstd_a(b, p):
                pool.wait_ge(sem("var_a"), b + 1)
                g.tensor_tensor(a_rstd[p], a_var[p], half[:], ALU.pow).then_inc(sem("rstd_a"), 1)
            with pool.Fori(0, B // 2) as i:
                rstd_a(i * 2, 0)
                rstd_a(i * 2 + 1, 1)

            pool.wait_ge(sem("inp_a"), B)
            for t in q_stack + k_stack:
                g.memset(t[0:SHIFT].bitcast(FP32), 0.0)
            for t in k_stack:
                last = g.memset(t[SHIFT:SHIFT + 2], 1.0)
            last.then_inc(sem("pads_set"), 1)
            pool.wait_ge(sem("pads_set"), 1)

            def rstd(i, b):
                pool.wait_ge(sem(f"var{i}"), b + 1)
                g.tensor_tensor(ln_rstd[i][:], ln_var[i][:], half[:], ALU.pow).then_inc(sem(f"rstd{i}"), 1)

            def mask(k, p, u):
                if there(k):
                    wait_apart(pool, "pool", "exp_made", HEADS * k + HQ * (u + 1))
                    for i in range(NT):
                        v = probs[u % 2][:, :, K_AT[i]:K_AT[i] + P]
                        last = g.affine_select(out=v, in_=v, compare_op=ALU.is_ge, fill=0.0, base=0,
                                               pattern=[[0, HQ], [1, P]], channel_multiplier=-1)
                    last.then_inc(sem("masked"), 1)

            def dispatch(k, p, c):
                if there(k - 3):
                    b = k - 3
                    if c == 0:
                        pool.wait_ge(sem("numbered"), 2 * b + 2)
                        pool.wait_ge(sem("slot_made"), b + 1)
                        wait_apart(pool, "pool", "rows_gated", b + 1)
                    for i in range(NT):
                        g.indirect_dma_start(lists[:, :], bass.IndirectOffsetOnAxis(ap=r_slot[:, i, c:c + 1], axis=0),
                                             rows[1 - p][c][:, i, :], None).then_inc(sem("listed"), 16)

            def run(k, p):
                if there(k + 2):
                    b = k + 2
                    rstd(0, b)
                    pool.wait_ge(sem("z_made"), b + 1)
                    pool.wait_ge(sem("x_in_f"), 32 * (b + 1))
                    wait(pool, "h_kept", b)
                    g.tensor_tensor(f_h[:], f_z[:], bcast(f_mod[:, 1:2, :], [P, NT, D]), ALU.mult
                                    ).then_inc(sem("h_half"), 1)
                    pool.wait_ge(sem("h_half"), b + 1)
                    g.tensor_tensor(f_h[:], f_h[:], bcast(f_mod[:, 0:1, :], [P, NT, D]), ALU.add
                                    ).then_inc(sem("h_made"), 1)
                if there(k + 1):
                    b = k + 1
                    pool.wait_ge(sem("split"), 3 * b + 3)
                    g.tensor_tensor(f_parts[:, :, 2, :], f_fp[:], f_parts[:, :, 1, :], ALU.subtract
                                    ).then_inc(sem("parts_made"), 1)
                mask(k, p, 0)
                dispatch(k, p, 0)
                if there(k + 2):
                    rstd(1, k + 2)
                mask(k, p, 1)
                dispatch(k, p, 1)
                if there(k - 1):
                    b = k - 1
                    rstd(2, b)
                mask(k, p, 2)
                if there(k - 1):
                    pool.wait_ge(sem("z2_made"), b + 1)
                    pool.wait_ge(sem("x1_back"), 32 * (b + 1))
                    g.tensor_tensor(b_x2[:], b_x2[:], bcast(b_gate[1 - p][:].rearrange("p (o d) -> p o d", o=1), [P, NT, D]),
                                    ALU.mult).then_inc(sem("gated"), 1)
                    pool.wait_ge(sem("gated"), b + 1)
                    g.tensor_tensor(b_x1[:], b_x1[:], b_x2[:], ALU.add).then_inc(sem("base_made"), 1)
                mask(k, p, 3)
                if there(k + 2):
                    b = k + 2
                    pool.wait_ge(sem("split"), 3 * b + 1)
                    g.tensor_tensor(f_fp[:], f_fp[:], f_parts[:, :, 0, :], ALU.subtract).then_inc(sem("split"), 1)
                if there(k - 2):
                    b = k - 2
                    pool.wait_ge(sem("z2_copied"), b + 1)
                    for c in range(2):
                        n = rows[p][c][:, :, NUM].bitcast(I32)
                        g.tensor_tensor(n, n, two_T[:], ALU.add).then_inc(sem("numbered"), 1)

            iterations(run)(pool)
            for c in range(2):
                dispatch(B + 2, B % 2, c)

            pool.wait_ge(sem("pv_mm"), QUADS * B)
            pool.wait_ge(sem("T_mm"), HEADS * B)
            g.memset(fill_rows, 0.0).then_inc(sem("fill_zero"), 1)
            pool.wait_ge(sem("fill_zero"), 1)
            g.iota(fill_rows[:, :, NUM].bitcast(I32), [[P, FILL * NS]], base=TOK, channel_multiplier=1
                   ).then_inc(sem("fill_set"), 1)

            pool.wait_ge(sem("base_out"), 16 * B)
            pool.wait_ge(sem("spare_saved"), 48)

            def add_tiles(first, turns):
                with pool.Fori(first, first + turns) as i:
                    for r in range(TURN):
                        wait_apart(pool, "pool", "res_made", i * TURN + r + 3)
                        for s in range(NS):
                            g.indirect_dma_start(out[:, :], bass.IndirectOffsetOnAxis(
                                ap=x_tile[r][:, s, NUM:NUM + 1].bitcast(I32), axis=0), res[r][:, s, :], None,
                                compute_op=ALU.add).then_inc(sem(f"res_saved{r}"), 16)
                for r in range(TURN):
                    pool.wait_ge(sem(f"res_saved{r}"), 16 * NS * (first + turns))
            add_tiles(0, HALF // TURN)
            add_tiles(HALF // TURN, HALF // TURN)

        @block.tensor
        def _(pe):
            t = nc.tensor
            pe.wait_ge(sem("consts"), 1)
            pe.wait_ge(sem("weights_in"), 16 * 15)
            for i in range(3):
                t.transpose(S_ps[:, i * D:(i + 1) * D], w_in[:, i, :], ident[:])
            t.transpose(M_ps[:, 0:B], c_in[0:B, :], ident[0:B, 0:B]).then_inc(sem("setup_tr"), 1)
            pe.wait_ge(sem("silu_made"), 1)
            for i in range(3):
                t.matmul(T_ps[:, i * B:(i + 1) * B], wmod_in[:, i * D:(i + 1) * D], silu_c, start=True, stop=True)
            t.matmul(O_ps[0:B, 0:3 * D], silu_c, wmod_in[:, 3 * D:6 * D], start=True, stop=True
                     ).then_inc(sem("mod_mm"), 1)

            pe.wait_ge(sem("setup_done"), 1)

            def spiking(b, p):
                R_ps = (S_ps, T_ps)[p]
                pe.wait_ge(sem("xhat_a"), b + 1)
                if not (isinstance(b, int) and b == 0):
                    pe.wait_ge(sem("hT_a"), b)
                for i in range(NT):
                    last = t.transpose(M_ps[:, i * P:(i + 1) * P], a_xhat[p][:, i, :], ident[:])
                last.then_inc(sem("xT_a"), 1)
                pe.wait_ge(sem("hT_a"), b + 1)
                wait(pe, "ek_a", b - 1)
                wait(pe, "kv_a", b - 1)
                for i in range(3):
                    last = t.matmul(R_ps[:, i * T:(i + 1) * T], wT[:, i, :], a_hT[p], start=True, stop=True)
                last.then_inc(sem("rkv_a"), 1)
            spiking(0, 0)
            spiking(1, 1)
            with pe.Fori(1, B // 2) as i:
                spiking(i * 2, 0)
                spiking(i * 2 + 1, 1)

            def scores(k, p, q, j):
                b, u, pp = k + q // QUADS, q % QUADS, (p + q // QUADS) % 2
                if not there(b):
                    return
                h = HQ * u + j
                if h == 0:
                    pe.wait_ge(sem("stacks_in"), 32 * (b + 1))
                wait(pe, "blk_made", HEADS * b + h)
                for i in range(NT):
                    at = Q_AT[i]
                    t.matmul(S_ps[:, at:at + P * (i + 1)], q_stack[pp][0:SHIFT, h, P * i:P * (i + 1)],
                             k_stack[pp][0:SHIFT, h, 0:P * (i + 1)], start=True, stop=False)
                    last = t.matmul(S_ps[:, at + P * i:at + P * (i + 1)], ident_h[:], causal[:], start=False, stop=True)
                last.then_inc(sem("S_mm"), 1)

            def shifted(k, p, u, j):
                if not there(k):
                    return
                h = HQ * u + j
                if j == 0:
                    n = QUADS * k + u
                    pe.wait_ge(sem(f"shift_in{u % 2}"), (n - u % 2) * 16 + 32)
                wait(pe, "exp_made", HEADS * k + h)
                for i in range(NT):
                    last = t.matmul(T_ps[:, K_AT[i]:K_AT[i] + T - P * i], k_stack[p][0:SHIFT + 2, h, P * i:P * (i + 1)],
                                    q_stack[p][0:SHIFT + 2, h, P * i:T], start=True, stop=True)
                last.then_inc(sem("T_mm"), 1)

            def values(k, p, q):
                b, u, pp = k + q // QUADS, q % QUADS, (p + q // QUADS) % 2
                if not there(b):
                    return
                n = QUADS * k + q
                if u == 0:
                    pe.wait_ge(sem("v_put"), b + 1)
                pe.wait_ge(sem("masked"), n + 1)
                wait(pe, "o_out", n)
                for i in range(NT):
                    for j in range(HQ):
                        last = t.matmul(O_ps[32 * j:32 * j + HD + 1, P * i:T], v_aug[pp][:, i, HQ * u + j, :],
                                        probs[u % 2][:, j, K_AT[i]:K_AT[i] + T - P * i],
                                        start=(i == 0), stop=(i == NT - 1))
                last.then_inc(sem("pv_mm"), 1)

            def transposes(kind, k, u, ready, count, src, done, n=NT):
                if job_index(next(j for j in JOBS if j[0] == kind and j[1] == u), k) is None:
                    return
                pe.wait_ge(sem(ready), count)
                wait_M_free(pe, kind, u, k)
                for i in range(n):
                    last = t.transpose(M_ps[:, i * P:(i + 1) * P], src(i), ident[:])
                last.then_inc(sem(done), 1)

            def run(k, p):
                for u in range(QUADS):
                    for j in range(HQ):
                        scores(k, p, u + 2, j)
                        shifted(k, p, u, j)
                        if (u, j) == (2, 0) and there(k - 2):
                            pe.wait_ge(sem("ones_made"), k - 1)
                            wait_M_free(pe, "rank", u, k)
                            for i in range(NT):
                                for a in range(i):
                                    t.matmul(M_ps[:, i * LISTS:(i + 1) * LISTS], ones_h[:], r_oneh[:, a, :],
                                             start=(a == 0), stop=False)
                                t.matmul(M_ps[:, i * LISTS:(i + 1) * LISTS], before[:], r_oneh[:, i, :],
                                         start=(i == 0), stop=True)
                            for i in range(NT):
                                last = t.matmul(M_ps[:, NT * LISTS:(NT + 1) * LISTS], ones_h[:], r_oneh[:, i, :],
                                                start=(i == 0), stop=(i == NT - 1))
                            last.then_inc(sem("rank_mm"), 1)
                        if j == 0:
                            n = QUADS * k + u - 2
                            transposes("o", k, u, "o_out", n + 1, lambda i: o_sb[:, i * P:(i + 1) * P], "o_tr")
                        if j == 1 and job_index(("max", u, u + 1), k) is not None:
                            n = QUADS * k + u + 1
                            pe.wait_ge(sem("max_made"), n + 1)
                            wait_M_free(pe, "max", u, k)
                            t.transpose(M_ps[0:HQ * NT, 0:P], rowmax[(u + 1) % 2][:].rearrange("p h i -> p (h i)"),
                                        ident[:]).then_inc(sem("max_tr"), 1)
                        if (u, j) == (0, 2):
                            transposes("spk", k, u, "spk_made", k + 3, lambda i: f_spk[:, i * P:(i + 1) * P], "spk_tr")
                        if (u, j) == (0, 3) and there(k - 2):
                            pe.wait_ge(sem("z2T_made"), k - 1)
                            wait_M_free(pe, "route", u, k)
                            for i in range(NT):
                                last = t.matmul(M_ps[:, i * E:(i + 1) * E], b_z2T[:, i * P:(i + 1) * P], wrout[:],
                                                start=True, stop=True)
                            last.then_inc(sem("route_mm"), 1)
                        if (u, j) == (1, 2):
                            transposes("y", k, u, "y_made", QUADS * k, lambda i: b_y[:, i, :], "y_tr")
                        if (u, j) == (1, 3) and there(k - 1):
                            pe.wait_ge(sem("yT_made"), k)
                            for i in range(NT):
                                last = t.matmul(M_ps[:, i * P:(i + 1) * P], b_yT[:, i * P:(i + 1) * P], wproj[:],
                                                start=True, stop=True)
                            last.then_inc(sem("proj_mm"), 1)
                        if (u, j) == (2, 2):
                            transposes("z1", k, u, "z1_made", k + 3, lambda i: f_z[:, i, :], "z1_tr")
                        if (u, j) in ((2, 3), (3, 2)) and there(k + 2):
                            i = u - 2
                            pe.wait_ge(sem("z1T_made"), k + 3)
                            wait_M_free(pe, "qk"[i], u, k)
                            t.matmul(M_ps[:, :], wqkv[:, i * D:(i + 1) * D], f_z1T[:], start=True, stop=True
                                     ).then_inc(sem("qk"[i] + "_mm"), 1)
                        if (u, j) == (3, 3):
                            if there(k + 2):
                                wait_M_free(pe, "v", u, k)
                                for i in range(NT):
                                    last = t.matmul(M_ps[:, i * P:(i + 1) * P], f_z1T[:, i * P:(i + 1) * P],
                                                    wqkv[:, 2 * D:3 * D], start=True, stop=True)
                                last.then_inc(sem("v_mm"), 1)
                            transposes("z2", k, u, "z2_made", k, lambda i: rows[1 - p][0][:, i, 0:D], "z2_tr")
                    values(k, p, u - 1)

            iterations(run)(pe)

            pe.wait_ge(sem("exp_made"), HEADS * B)
            pe.wait_ge(sem("blk_made"), HEADS * B)

            def R(r):
                return (S_ps, T_ps)[r % 2]

            def turn_over(n, r):
                pe.wait_ge(sem(f"x_tile_in{r % TURN}"), 16 * n_use(n, r))
                pe.wait_ge(sem("xT_made"), n + 1)
                for s in range(NS):
                    last = t.transpose(R(r)[:, s * P:(s + 1) * P], x_tile[r % TURN][:, s, 0:D], ident[:])
                last.then_inc(sem("x_tr"), 1)

            def n_use(n, r):
                return n // TURN + 1 if isinstance(n, int) else turn[0] + (1 if r < TURN else 2)

            def up(n, r):
                pe.wait_ge(sem("xT_made"), n + 3)
                pe.wait_ge(sem("w_made"), n + 1)
                pe.wait_ge(sem("gelu_made"), n + 1)
                for f in range(FH):
                    last = t.matmul(R(r)[:, 512 + f * TS:512 + (f + 1) * TS], w_tile[r % 4][:, f * P:(f + 1) * P],
                                    xT_tile[r % 2], start=True, stop=True)
                last.then_inc(sem("up_mm"), 1)

            def down(n, r):
                pe.wait_ge(sem("gelu_made"), n + 3)
                pe.wait_ge(sem("res_made"), n + 1)
                for s in range(NS):
                    for f in range(FH):
                        last = t.matmul(R(r)[:, 1024 + s * P:1024 + (s + 1) * P], hid[r % 2][:, f, s * P:(s + 1) * P],
                                        w_tile[r % 4][:, F + f * D:F + (f + 1) * D], start=(f == 0), stop=(f == FH - 1))
                last.then_inc(sem("down_mm"), 1)
            turn = [None]
            pe.sem_inc(sem("up_mm"), 2)
            pe.sem_inc(sem("down_mm"), 2)
            turn_over(0, 0)
            turn_over(1, 1)
            up(0, 0)
            with pe.Fori(0, TILES // TURN) as i:
                turn[0] = i
                for r in range(TURN):
                    turn_over(i * TURN + (r + 2), r + 2)
                    up(i * TURN + (r + 1), r + 1)
                    down(i * TURN + r, r)

        @block.scalar
        def _(act):
            a = nc.scalar
            act.wait_ge(sem("setup_tr"), 1)
            a.activation(silu_t[:, 0, :], M_ps[:, 0:B], ACT.Exp, scale=-1.0).then_inc(sem("silu_exp"), 1)
            act.wait_ge(sem("weights_in"), 16 * 15)
            a.activation(cols[:, 3:5], cols[:, 3:5], ACT.Exp).then_inc(sem("decay_exp"), 1)
            act.wait_ge(sem("setup_done"), 1)

            def spiking(b, p):
                R_ps = (S_ps, T_ps)[p]
                act.wait_ge(sem("xT_a"), b + 1)
                wait(act, "rkv_a", b - 1)
                col = lambda i: mod_cm[:, i, ds(b)]
                a.activation(a_hT[p], M_ps[:, :], ACT.Identity, bias=col(0), scale=col(1)).then_inc(sem("hT_a"), 1)
                act.wait_ge(sem("rkv_a"), b + 1)
                wait(act, "inp_a", b - 1)
                a.activation(a_er[p], R_ps[:, 0:T], ACT.Exp, bias=BR, scale=-1.0)
                a.activation(a_ek[p], R_ps[:, T:2 * T], ACT.Exp, bias=BK).then_inc(sem("ek_a"), 1)
            spiking(0, 0)
            spiking(1, 1)
            with act.Fori(1, B // 2) as i:
                spiking(i * 2, 0)
                spiking(i * 2 + 1, 1)

            def run(k, p):
                for u in range(QUADS):
                    for j in range(HQ):
                        if there(k):
                            h = HQ * u + j
                            if j == 0:
                                wait(act, "pv_mm", QUADS * k + u - 1)
                            act.wait_ge(sem("T_mm"), HEADS * k + h + 1)
                            a.activation(probs[u % 2][:, j, :], T_ps[:, 0:SCORES], ACT.Exp).then_inc(sem("exp_made"), 1)
                        n = QUADS * k + u + 1
                        if j == 1 and job_index(("max", u, u + 1), k) is not None:
                            act.wait_ge(sem("max_tr"), n + 1)
                            v = (u + 1) % 2
                            wait(act, f"shift_in{v}", (n - v) * 16)
                            a.mul(shift[v][:, 0, :], M_ps[0:HQ * NT, 0:P], -1.0).then_inc(sem("shift_hi"), 1)
                        if (u, j) == (0, 1) and there(k + 1):
                            wait_apart(act, "act", "split", 3 * (k + 1) + 2)
                            a.copy(f_parts[:, :, 1, :], f_fp[:]).then_inc(sem("split"), 1)
                        if (u, j) == (1, 1) and there(k + 1):
                            wait(act, "pv_mm", QUADS * k)
                            wait_apart(act, "act", "v_out", k + 2)
                            a.copy(v_aug[1 - p][:, :, :, 0:HD], f_v[:].rearrange("p i (h d) -> p i h d", h=HEADS)
                                   ).then_inc(sem("v_put"), 1)
                        if (u, j) == (2, 0) and there(k + 2):
                            wait_apart(act, "act", "h_made", k + 3)
                            a.copy(row_all[:, ds(k + 2), :].rearrange("p o t -> p (o t)"),
                                   f_h[:].rearrange("p i d -> p (i d)")).then_inc(sem("h_kept"), 1)
                        if (u, j) == (2, 1) and there(k - 2):
                            wait_apart(act, "act", "margin_made", k - 1)
                            wait_apart(act, "act", "weights_made", k - 2)
                            a.activation(r_e2[:], r_d[:], ACT.Exp).then_inc(sem("gates_exp"), 1)
                        if (u, j) == (3, 1) and there(k - 1):
                            wait_apart(act, "act", "z2_made", k)
                            a.copy(rows[1 - p][1][:, :, 0:D], rows[1 - p][0][:, :, 0:D]).then_inc(sem("z2_copied"), 1)
                        if (u, j) == (1, 2) and there(k - 1):
                            wait_apart(act, "act", "route_mm", k - 1)
                            act.wait_ge(sem("y_tr"), k)
                            wait(act, "proj_mm", k - 1)
                            a.copy(b_yT[:], M_ps[:, :]).then_inc(sem("yT_made"), 1)
                        if (u, j) == (2, 2) and there(k + 2):
                            wait_apart(act, "act", "spk_tr", k + 3)
                            act.wait_ge(sem("z1_tr"), k + 3)
                            wait(act, "v_mm", k + 2)
                            a.copy(f_z1T[:], M_ps[:, :]).then_inc(sem("z1T_made"), 1)
                        if (u, j) in ((2, 3), (3, 2)) and there(k + 2):
                            i = u - 2
                            act.wait_ge(sem("qk"[i] + "_mm"), k + 3)
                            wait(act, "parts_made", k + 2)
                            a.copy(f_fp[:, i, :], M_ps[:, :]).then_inc(sem("qk"[i] + "_out"), 1)
                        if (u, j) == (3, 3):
                            if there(k + 2):
                                act.wait_ge(sem("v_mm"), k + 3)
                                wait(act, "v_put", k + 2)
                                a.copy(f_v[:].rearrange("p i d -> p (i d)"), M_ps[:, :]).then_inc(sem("v_out"), 1)
                            if there(k - 1):
                                wait_apart(act, "act", "proj_mm", k)
                                act.wait_ge(sem("z2_tr"), k)
                                wait(act, "route_mm", k - 1)
                                a.copy(b_z2T[:], M_ps[:, :]).then_inc(sem("z2T_made"), 1)
                            if there(k + 2):
                                wait_apart(act, "act", "k_out", k + 3)
                                wait_apart(act, "act", "terms_out", 96 * (k + 2))
                                a.copy(f_parts[:, :, 0, :], f_fp[:]).then_inc(sem("split"), 1)
                    n = QUADS * k + u - 1
                    if job_index(("o", 0, u - 1), k) is not None:
                        act.wait_ge(sem("pv_mm"), n + 1)
                        wait(act, "o_tr", n)
                        a.copy(o_sb[:], O_ps[:, :]).then_inc(sem("o_out"), 1)

            iterations(run)(act)

            act.wait_ge(sem("listed"), 16 * 2 * NT * B)
            fill_up(act, 1)
            act.wait_ge(sem("pv_mm"), QUADS * B)

            def turned(n, r):
                act.wait_ge(sem("x_tr"), n + 1)
                act.wait_ge(sem("up_mm"), n + 1)
                a.activation(xT_tile[r % 2], (S_ps, T_ps)[r % 2][:, 0:TS], ACT.Identity, scale=LN2
                             ).then_inc(sem("xT_made"), 1)

            def gelu(n, r):
                act.wait_ge(sem("up_mm"), n + 3)
                act.wait_ge(sem("down_mm"), n + 1)
                a.activation(hid[r % 2].rearrange("p f t -> p (f t)"), (S_ps, T_ps)[r % 2][:, 512:512 + FH * TS], ACT.Gelu
                             ).then_inc(sem("gelu_made"), 1)
            act.sem_inc(sem("xT_made"), 2)
            act.sem_inc(sem("gelu_made"), 2)
            turned(0, 0)
            turned(1, 1)
            gelu(0, 0)
            with act.Fori(0, TILES // TURN) as i:
                for r in range(TURN):
                    turned(i * TURN + (r + 2), r)
                    gelu(i * TURN + (r + 1), r + 1)

        @block.vector
        def _(dve):
            v = nc.vector
            n_setup = [0]

            def link(ins):
                n_setup[0] += 1
                ins.then_inc(sem("setup_dve"), 1)
                dve.wait_ge(sem("setup_dve"), n_setup[0])

            v.memset(O_ps[:, :], 0.0)
            dve.wait_ge(sem("setup_tr"), 1)
            v.tensor_copy(wT[:].rearrange("p a d -> p (a d)"), S_ps[:, 0:3 * D])
            dve.wait_ge(sem("silu_exp"), 1)
            link(v.tensor_scalar_add(silu_t[:, 1, :], silu_t[:, 0, :], 1.0))
            link(v.reciprocal(silu_t[:, 0, :], silu_t[:, 1, :]))
            v.tensor_tensor(silu_c, M_ps[:, 0:B], silu_t[:, 0, :], ALU.mult).then_inc(sem("silu_made"), 1)
            dve.wait_ge(sem("mod_mm"), 1)

            def gate(dst, src, t1, t2):
                link(v.tensor_scalar(t1, src, 0.0, 2.0, ALU.is_ge, ALU.mult))
                link(v.scalar_tensor_tensor(t2, t1, -1.0, src, ALU.add, ALU.mult))
                link(v.tensor_scalar(t2, t2, GATE_MIN, None, ALU.max))
                link(v.scalar_tensor_tensor(dst, t1, -1.0, t2, ALU.add, ALU.mult))
            v.tensor_copy(mod_cm[:, 0, :], T_ps[:, 0:B])
            v.tensor_scalar_add(mod_cm[:, 1, :], T_ps[:, B:2 * B], 1.0)
            gate(mod_cm[:, 2, :], T_ps[:, 2 * B:3 * B], gate_t[:, 0, :], gate_t[:, 1, :])
            v.tensor_copy(row_t[0:B, 0, :], O_ps[0:B, 0:D])
            v.tensor_scalar_add(row_t[0:B, 1, :], O_ps[0:B, D:2 * D], 1.0)
            gate(row_t[0:B, 2, :], O_ps[0:B, 2 * D:3 * D], row_g[0:B, 0, :], row_g[0:B, 1, :])
            dve.sem_inc(sem("rows_made"), 1)
            dve.wait_ge(sem("decay_exp"), 1)
            v.tensor_scalar_mul(BR, BR, -1.0)
            link(v.tensor_scalar(wqkv[:, 0:D], wqkv[:, 0:D], LN1, 1.0 / math.sqrt(HD), ALU.mult, ALU.mult))
            v.tensor_scalar(wqkv[:, D:3 * D], wqkv[:, D:3 * D], LN1, None, ALU.mult)
            link(v.tensor_scalar(wrout[:], wrout[:], LN2, None, ALU.mult))
            for e in range(E):
                v.memset(place[:, e:e + 1], float(E - e))
            for i in range(LISTS):
                last = v.memset(r_next[:, i:i + 1], float(i * CAP))
            last.then_inc(sem("places_set"), 1)
            v.memset(O_ps[:, :], 0.0).then_inc(sem("setup_done"), 1)

            def stats(x_t, st, mv, var, name, n, count):
                for i in range(NT):
                    last = v.bn_stats(st[:, i, :], x_t[:, i, :])
                last.then_inc(sem(name + "_c"), 1)
                wait_apart(dve, "dve", name + "_c", 2 * n + 1)
                for i in range(NT):
                    last = v.bn_aggr(mv[:, i, :], st[:, i, :])
                last.then_inc(sem(name + "_c"), 1)
                dve.wait_ge(sem(name + "_c"), 2 * n + 2)
                v.tensor_scalar_add(var, mv[:, :, 1], LN_EPS).then_inc(sem(name), 1)

            def normalise(dst, x_t, mv, rstd):
                for i in range(NT):
                    last = v.tensor_scalar(dst[:, i, 0:D], x_t[:, i, :], mv[:, i, 0:1], rstd[:, i:i + 1],
                                           ALU.subtract, ALU.mult)
                return last

            def stats_a(b, p):
                half_b = b // 2 if isinstance(b, int) else None
                dve.wait_ge(sem(f"x_in{p}"), (b - p) * 8 + 16)
                wait(dve, "rstd_a", b - 1)
                stats(a_x[p], a_stats[p], a_mv[p], a_var[p], "var_a", b, None)

            def xhat_a(b, p):
                dve.wait_ge(sem("rstd_a"), b + 1)
                wait(dve, "xT_a", b - 1)
                normalise(a_xhat[p], a_x[p], a_mv[p], a_rstd[p]).then_inc(sem("xhat_a"), 1)

            def spiking(b, p, more=True):
                R_ps = (S_ps, T_ps)[p]
                if more:
                    stats_a(b + 1, 1 - p)
                dve.wait_ge(sem("ek_a"), b + 1)
                v.scalar_tensor_tensor(a_kv, R_ps[:, 2 * T:3 * T], BV, a_ek[p], ALU.add, ALU.mult
                                       ).then_inc(sem("kv_a"), 1)
                v.tensor_tensor_scan(a_sb, bcast(TD, [P, T]), a_ek[p], 0.0, ALU.mult, ALU.add
                                     ).then_inc(sem("wkv_a"), 1)
                v.tensor_scalar_add(a_er1, a_er[p], 1.0)
                dve.wait_ge(sem("kv_a"), b + 1)
                v.tensor_tensor_scan(a_sa, bcast(TD, [P, T]), a_kv, 0.0, ALU.mult, ALU.add).then_inc(sem("wkv_a"), 1)
                if more:
                    xhat_a(b + 1, 1 - p)
                dve.wait_ge(sem("wkv_a"), 5 * b + 1)
                v.scalar_tensor_tensor(a_den0, a_ek[p], GD, a_sb, ALU.mult, ALU.add).then_inc(sem("wkv_a"), 1)
                dve.wait_ge(sem("wkv_a"), 5 * b + 2)
                v.scalar_tensor_tensor(a_num, a_kv, GD, a_sa, ALU.mult, ALU.add)
                dve.wait_ge(sem("wkv_a"), 5 * b + 3)
                v.scalar_tensor_tensor(a_den, a_den0, WKV_EPS, a_er1, ALU.add, ALU.mult).then_inc(sem("wkv_a"), 1)
                dve.wait_ge(sem("wkv_a"), 5 * b + 4)
                v.reciprocal(a_rec, a_den).then_inc(sem("wkv_a"), 1)
                dve.wait_ge(sem("wkv_a"), 5 * b + 5)
                v.scalar_tensor_tensor(row_all[:, ds(b), :].rearrange("p o t -> p (o t)"), a_num, 1.0 / THRESH, a_rec,
                                       ALU.mult, ALU.mult).then_inc(sem("inp_a"), 1)

            stats_a(0, 0)
            xhat_a(0, 0)
            spiking(0, 0)
            spiking(1, 1)
            with dve.Fori(1, B // 2 - 1) as i:
                spiking(i * 2, 0)
                spiking(i * 2 + 1, 1)
            spiking(B - 2, 0)
            spiking(B - 1, 1, more=False)

            dve.wait_ge(sem("inp_a"), B)
            v.memset(m_out[:, :, U - 1], 0.0).then_inc(sem("mem"), 1)
            with dve.Fori(0, T // U) as turn:
                done = turn * (2 * U + 2)
                wait_apart(dve, "dve", "mem", done + 1)
                v.tensor_copy(m_in, row_all[:, :, bass.ds(turn * U, U)]).then_inc(sem("mem"), 1)
                dve.wait_ge(sem("mem"), done + 2)
                for j in range(U):
                    prev = m_out[:, :, (j - 1) % U]
                    v.scalar_tensor_tensor(m_tmp, prev, 1.0, m_in[:, :, j], ALU.is_gt, ALU.subtract
                                           ).then_inc(sem("mem"), 1)
                    dve.wait_ge(sem("mem"), done + 2 * j + 3)
                    v.scalar_tensor_tensor(m_out[:, :, j], prev, BETA, m_tmp, ALU.mult, ALU.subtract
                                           ).then_inc(sem("mem"), 1)
                    if j < U - 1:
                        dve.wait_ge(sem("mem"), done + 2 * j + 4)
                wait_apart(dve, "dve", "mem", done + 2 * U + 2)
                v.tensor_copy(row_all[:, :, bass.ds(turn * U, U)], m_out).then_inc(sem("mem"), 1)
            dve.wait_ge(sem("mem"), 1 + (T // U) * (2 * U + 2))

            def row(b):
                return row_all[:, ds(b), :].rearrange("p o t -> p (o t)")

            places = bcast(place[:].rearrange("p (o e) -> p o e", o=1), [P, NT, E])

            def wide(col):
                return bcast(col.rearrange("p (n o) -> p n o", o=1), [P, NT, E])
            FIRST, SECOND = r_m[:, 0, :], r_m[:, 1, :]
            ROUTE = {
                (0, 3): [lambda: v.tensor_reduce(FIRST, r_lg[:], AX.X, ALU.max)],
                (1, 0): [lambda: v.tensor_tensor(r_eq[:], r_lg[:], wide(FIRST), ALU.is_equal),
                         lambda: v.tensor_tensor(r_k[:], r_eq[:], places, ALU.mult)],
                (1, 1): [lambda: v.tensor_reduce(r_f[:], r_k[:], AX.X, ALU.max),
                         lambda: v.tensor_tensor(r_one[:, :, 0, :], places, wide(r_f[:]), ALU.is_equal)],
                (1, 2): [lambda: v.scalar_tensor_tensor(r_l2[:], r_one[:, :, 0, :], MASKED, r_lg[:], ALU.mult, ALU.add),
                         lambda: v.tensor_reduce(SECOND, r_l2[:], AX.X, ALU.max)],
                (1, 3): [lambda: v.tensor_tensor(r_eq[:], r_l2[:], wide(SECOND), ALU.is_equal),
                         lambda: v.tensor_tensor(r_k[:], r_eq[:], places, ALU.mult),
                         lambda: v.tensor_reduce(r_f[:], r_k[:], AX.X, ALU.max)],
            }
            BEFORE = {(u, j): sum(len(s) for at, s in ROUTE.items() if at < (u, j)) for u in range(QUADS)
                      for j in range(HQ)}
            STEPS = sum(len(s) for s in ROUTE.values())

            def route_steps(k, at):
                if at in ROUTE and there(k - 2):
                    n = STEPS * (k - 2) + BEFORE[at]
                    for s, step in enumerate(ROUTE[at]):
                        wait_apart(dve, "dve", "routing", n + s)
                        step().then_inc(sem("routing"), 1)

            def run(k, p):
                if there(k + 2):
                    wait_apart(dve, "dve", "v_mm", k + 2)
                    v.tensor_scalar(f_spk[:], row(k + 2), 1.0, mod_cm[:, 2, ds(k + 2)], ALU.is_gt, ALU.mult
                                    ).then_inc(sem("spk_made"), 1)
                for u in range(QUADS):
                    s_b, s_u = k + (u + 2) // QUADS, (u + 2) % QUADS
                    for j in range(HQ):
                        if (u, j) == (2, 0) and there(k - 2):
                            wait_apart(dve, "dve", "routing", STEPS * (k - 1))
                            v.tensor_tensor(r_one[:, :, 1, :], places, wide(r_f[:]), ALU.is_equal
                                            ).then_inc(sem("second_made"), 1)
                            wait_apart(dve, "dve", "second_made", k - 1)
                            wait_apart(dve, "dve", "rank_mm", k - 2)
                            v.tensor_copy(r_oneh[:], r_one[:].rearrange("p i c e -> p i (c e)")
                                          ).then_inc(sem("ones_made"), 1)
                            wait_apart(dve, "dve", "gates_exp", k - 2)
                            v.tensor_tensor(r_d[:], SECOND, FIRST, ALU.subtract).then_inc(sem("margin_made"), 1)
                        if there(s_b):
                            dve.wait_ge(sem("S_mm"), HEADS * s_b + HQ * s_u + j + 1)
                            v.tensor_reduce(blkmax[u % 2][:, j, :],
                                            S_ps[:, 0:SCORES].rearrange("p (n t) -> p n t", n=NBLK), AX.X, ALU.max
                                            ).then_inc(sem("blk_made"), 1)
                        if j == 1:
                            if job_index(("o", u, u - 2), k) is not None:
                                n = QUADS * k + u - 2
                                h0 = HQ * ((u - 2) % QUADS)
                                dve.wait_ge(sem("o_tr"), n + 1)
                                heads = M_ps[:, :].rearrange("p (i h w) -> p i h w", i=NT, h=HQ)
                                v.reciprocal(o_rec[:], heads[:, :, :, HD]).then_inc(sem("o_rec"), 1)
                                dve.wait_ge(sem("o_rec"), n + 1)
                                if u == 2:
                                    wait(dve, "y_tr", k)
                                v.tensor_tensor(b_y[:, :, h0 * HD:(h0 + HQ) * HD].rearrange("p i (h d) -> p i h d", h=HQ),
                                                heads[:, :, :, 0:HD],
                                                bcast(o_rec[:].rearrange("p i (h o) -> p i h o", o=1), [P, NT, HQ, HD]),
                                                ALU.mult).then_inc(sem("y_made"), 1)
                            if job_index(("max", u, u + 1), k) is not None:
                                n = QUADS * k + u + 1
                                w = (u + 1) % 2
                                dve.wait_ge(sem("shift_hi"), n + 1)
                                v.scalar_tensor_tensor(shift[w][:, 1, :], M_ps[0:HQ * NT, 0:P], -1.0, shift[w][:, 0, :],
                                                       ALU.mult, ALU.subtract).then_inc(sem("shift_made"), 1)
                        if (u, j) == (0, 2) and there(k + 2):
                            b = k + 2
                            dve.wait_ge(sem("spk_tr"), b + 1)
                            dve.wait_ge(sem("x_in_f"), 32 * (b + 1))
                            wait(dve, "x1_saved", 16 * b)
                            v.tensor_tensor(f_x1[:], f_x[:], M_tiles, ALU.add).then_inc(sem("x1_made"), 1)
                            dve.wait_ge(sem("x1_made"), b + 1)
                            stats(f_x1, ln_stats[0], ln_mv[0], ln_var[0][:], "var0", b, None)
                        if (u, j) == (0, 3):
                            if there(k - 2):
                                wait_apart(dve, "dve", "route_mm", k - 1)
                                v.tensor_copy(r_lg[:].rearrange("p i e -> p (i e)"),
                                              M_ps[:, 0:NT * E]).then_inc(sem("logits_made"), 1)
                                wait_apart(dve, "dve", "logits_made", k - 1)
                            if there(k + 2):
                                dve.wait_ge(sem("rstd0"), k + 3)
                                wait(dve, "z1_tr", k + 2)
                                normalise(f_z, f_x1, ln_mv[0], ln_rstd[0]).then_inc(sem("z_made"), 1)
                        if (u, j) == (1, 2) and there(k + 2):
                            dve.wait_ge(sem("h_made"), k + 3)
                            stats(f_h, ln_stats[1], ln_mv[1], ln_var[1][:], "var1", k + 2, None)
                        if (u, j) == (1, 3) and there(k + 2):
                            dve.wait_ge(sem("rstd1"), k + 3)
                            normalise(f_z, f_h, ln_mv[1], ln_rstd[1]).then_inc(sem("z1_made"), 1)
                        if (u, j) == (2, 0) and there(k - 1):
                            b = k - 1
                            dve.wait_ge(sem("proj_mm"), b + 1)
                            dve.wait_ge(sem("h_kept"), b + 1)
                            wait(dve, "base_made", b)
                            v.tensor_tensor(b_x2[:].rearrange("p i d -> p (i d)"), row(b), M_ps[:, :], ALU.add
                                            ).then_inc(sem("x2_made"), 1)
                            dve.wait_ge(sem("x2_made"), b + 1)
                            stats(b_x2, ln_stats[2], ln_mv[2], ln_var[2][:], "var2", b, None)
                        if (u, j) == (2, 0) and there(k - 2):
                            dve.wait_ge(sem("rank_mm"), k - 1)
                            if isinstance(k, int) and k > 2 or not isinstance(k, int):
                                wait_apart(dve, "dve", "pos_made", k - 2)
                            v.tensor_tensor(r_pos[:], M_ps[:, 0:NT * LISTS].rearrange("p (i l) -> p i l", i=NT),
                                            bcast(r_next[:].rearrange("p (o l) -> p o l", o=1), [P, NT, LISTS]),
                                            ALU.add).then_inc(sem("ranked"), 1)
                            wait_apart(dve, "dve", "ranked", k - 1)
                            v.tensor_tensor(r_next[:], r_next[:], M_ps[:, NT * LISTS:(NT + 1) * LISTS], ALU.add
                                            ).then_inc(sem("pos_made"), 1)
                        if (u, j) == (2, 1) and there(k - 2):
                            dve.wait_ge(sem("ranked"), k - 1)
                            v.tensor_tensor(r_hit[:], r_one[:].rearrange("p i c e -> p i (c e)"), r_pos[:], ALU.mult
                                            ).then_inc(sem("hit_made"), 1)
                            dve.wait_ge(sem("gates_exp"), k - 1)
                            v.tensor_scalar_add(r_s[:], r_e2[:], 1.0).then_inc(sem("sum_made"), 1)
                        if (u, j) == (2, 2) and there(k - 2):
                            wait_apart(dve, "dve", "hit_made", k - 1)
                            v.tensor_reduce(r_row[:].rearrange("p i c -> p (i c)"),
                                            r_hit[:].rearrange("p i (c e) -> p (i c) e", c=2), AX.X, ALU.add
                                            ).then_inc(sem("slot_found"), 1)
                            wait_apart(dve, "dve", "sum_made", k - 1)
                            v.reciprocal(r_w[:, 0, :], r_s[:]).then_inc(sem("weight0"), 1)
                        if (u, j) == (2, 3) and there(k - 2):
                            wait_apart(dve, "dve", "slot_found", k - 1)
                            wait_apart(dve, "dve", "listed", 16 * 2 * NT * (k - 2))
                            v.tensor_copy(r_slot[:], r_row[:]).then_inc(sem("slot_made"), 1)
                            dve.wait_ge(sem("weight0"), k - 1)
                            v.tensor_tensor(r_w[:, 1, :], r_w[:, 0, :], r_e2[:], ALU.mult).then_inc(sem("weights_made"), 1)
                        if u == 3 and j < 2 and there(k - 2):
                            if j == 0:
                                dve.wait_ge(sem("weights_made"), k - 1)
                                dve.wait_ge(sem("x1_back"), 32 * (k - 1))
                            for i in range(NT):
                                last = v.tensor_scalar(rows[p][j][:, i, D:2 * D], b_gate[p][:], r_w[:, j, i:i + 1], None,
                                                       ALU.mult)
                            if j == 1:
                                last.then_inc(sem("rows_gated"), 1)
                        if (u, j) == (2, 2) and there(k - 1):
                            dve.wait_ge(sem("rstd2"), k)
                            wait(dve, "z2_tr", k - 1)
                            wait_apart(dve, "dve", "listed", 16 * 2 * NT * (k - 2))
                            normalise(rows[1 - p][0], b_x2, ln_mv[2], ln_rstd[2]).then_inc(sem("z2_made"), 1)
                        route_steps(k, (u, j))
                    if there(s_b):
                        n = QUADS * s_b + s_u
                        dve.wait_ge(sem("blk_made"), HQ * n + HQ)
                        wait(dve, "max_tr", n - 1)
                        bm, rm = blkmax[u % 2], rowmax[u % 2]
                        v.tensor_reduce(rm[:, :, 3], bm[:, :, 0:4], AX.X, ALU.max)
                        v.tensor_reduce(rm[:, :, 2], bm[:, :, 4:7], AX.X, ALU.max)
                        v.tensor_copy(rm[:, :, 0], bm[:, :, 7])
                        v.tensor_reduce(rm[:, :, 1], bm[:, :, 8:10], AX.X, ALU.max).then_inc(sem("max_made"), 1)

            iterations(run)(dve)

            n_table = [0]

            def chain(ins):
                n_table[0] += 1
                ins.then_inc(sem("table"), 1)
                dve.wait_ge(sem("table"), n_table[0])

            def one(ap):
                return ap[0:1]

            def by_tile(ap):
                return bcast(one(ap).rearrange("p (t o) -> p t o", o=1), [1, NTAB, LISTS])

            def by_list(ap, n=NTAB):
                return bcast(one(ap).rearrange("p (o l) -> p o l", o=1), [1, n, LISTS])
            dve.wait_ge(sem("pv_mm"), QUADS * B)
            dve.wait_ge(sem("T_mm"), HEADS * B)
            dve.wait_ge(sem("pos_made"), B)
            dve.wait_ge(sem("tiles_counted"), 1)
            STEP = TOK // TS
            choices = lambda ap: one(ap).rearrange("p (c e) -> p c e", c=2)
            v.tensor_copy(one(t_no), tile_no[:])
            for e in range(E):
                v.memset(choices(n_exp)[:, :, e], float(e))
            for i in range(LISTS):
                v.memset(l_cap[0:1, i:i + 1], float(i * CAP))
            v.memset(n_exc[0:1, 0:1], 0.0)
            chain(v.memset(n_exc[0:1, E:E + 1], float(HALF)))
            chain(v.tensor_tensor(one(n_cnt), r_next[0:1], one(l_cap), ALU.subtract))
            v.tensor_scalar(one(t_first), one(t_no), float(TS), None, ALU.mult)
            chain(v.tensor_scalar(one(n_cnt), one(n_cnt), 1.0 / TS, None, ALU.mult))
            chain(v.tensor_tensor(one(n_gt), bcast(one(n_cnt).rearrange("p (l o) -> p l o", o=1), [1, LISTS, STEP]),
                                  bcast(t_no[0:1, 0:STEP].rearrange("p (o j) -> p o j", o=1), [1, LISTS, STEP]),
                                  ALU.is_gt))
            chain(v.tensor_reduce(one(n_tiles), one(n_gt), AX.X, ALU.add))
            for e in range(1, E):
                chain(v.tensor_tensor(choices(n_exc)[:, :, e], choices(n_exc)[:, :, e - 1], choices(n_tiles)[:, :, e - 1],
                                      ALU.add))
            chain(v.tensor_tensor(one(n_end), one(n_exc), one(n_tiles), ALU.add))
            v.tensor_scalar(n_used[0:1, 0:1], n_end[0:1, E - 1:E], float(-TS), float(LISTS * CAP), ALU.mult, ALU.add)
            v.tensor_scalar(n_used[0:1, 1:2], n_end[0:1, LISTS - 1:LISTS], float(-TS), float(LISTS * CAP + E * TS),
                            ALU.mult, ALU.add)
            v.scalar_tensor_tensor(one(n_first), one(n_exc), float(-TS), one(l_cap), ALU.mult, ALU.add)
            v.tensor_tensor(one(t_ge), by_tile(t_no), by_list(n_exc), ALU.is_ge)
            chain(v.tensor_tensor(one(t_lt), by_tile(t_no), by_list(n_end), ALU.is_lt))
            chain(v.tensor_tensor(one(t_in), one(t_ge), one(t_lt), ALU.mult))
            chain(v.tensor_tensor(one(t_at), by_tile(t_first), by_list(n_first), ALU.add))
            chain(v.tensor_tensor(one(t_row), one(t_in), one(t_at), ALU.mult))
            v.tensor_reduce(one(t_rows), one(t_row), AX.X, ALU.add)
            v.tensor_reduce(one(t_sum), one(t_in), AX.X, ALU.add)
            v.tensor_scalar(t_spare[0:1, 0:HALF], t_first[0:1, 0:HALF], n_used[0:1, 0:1], None, ALU.add)
            v.tensor_scalar(t_spare[0:1, HALF:NTAB], t_first[0:1, HALF:NTAB], n_used[0:1, 1:2], None, ALU.add)
            chain(v.tensor_tensor(one(t_ge), one(t_in), by_list(n_exp), ALU.mult))
            chain(v.tensor_scalar(one(t_free), one(t_sum), -1.0, 1.0, ALU.mult, ALU.add))
            chain(v.tensor_tensor(one(t_spare), one(t_spare), one(t_free), ALU.mult))
            chain(v.tensor_tensor(one(t_rows), one(t_rows), one(t_spare), ALU.add))
            chain(v.tensor_reduce(one(t_sum), one(t_ge), AX.X, ALU.add))
            v.tensor_copy(tab[0:1, 0:NTAB], one(t_rows))
            v.tensor_copy(tab[0:1, NTAB:2 * NTAB], one(t_sum))
            v.tensor_copy(tab[0:1, 2 * NTAB:], r_next[0:1]).then_inc(sem("tab_made"), 1)
            dve.wait_ge(sem("tab_made"), 1)

            dve.wait_ge(sem("w12_in"), 48)

            def weights(n, r):
                e = dve.value_load(tab[0:1, ds(n + NTAB)], min_val=0, max_val=E - 1)
                if not isinstance(n, int):
                    dve.wait_ge(sem("down_mm"), n - 1)
                v.tensor_scalar(w_tile[r % 4], w_all[:, bass.ds(e, 1), :].rearrange("p o w -> p (o w)"), 1.0, None,
                                ALU.mult).then_inc(sem("w_made"), 1)
            dve.sem_inc(sem("res_made"), 2)
            weights(0, 0)
            weights(1, 1)
            with dve.Fori(0, TILES // TURN) as i:
                for r in range(TURN):
                    weights(i * TURN + (r + 2), r + 2)
                    dve.wait_ge(sem("down_mm"), i * TURN + (r + 3))
                    v.tensor_tensor(res[r], (S_ps, T_ps)[r % 2][:, 1024:1024 + TS].rearrange("p (s d) -> p s d", s=NS),
                                    x_tile[r][:, :, D:2 * D], ALU.mult).then_inc(sem("res_made"), 1)


_INS = ['x', 'W_r', 'b_r', 'W_k', 'b_k', 'W_v', 'b_v', 'W_td', 'b_td', 'global_decay']
_FFN = ['ln1_w', 'c_attn_w', 'c_proj_w', 'ln2_w', 'router_w', 'w1', 'w2']
_NAMES = ['L0_attn_' + n for n in _INS] + ['L0_ffn_' + n for n in _FFN] + ['L0_c', 'L0_wmod']


def kernel(**inputs):
    import numpy as _np
    import concourse.bacc as _bacc
    from concourse import mybir as _mybir
    from concourse.bass_utils import run_bass_kernel_spmd as _run

    nc = _bacc.Bacc("TRN2", target_bir_lowering=False, num_devices=1)
    arrays, args = {}, []
    for name in _NAMES:
        a = _np.ascontiguousarray(inputs[name])
        arrays[f"in_{name}_dram"] = a
        args.append(nc.dram_tensor(f"in_{name}_dram", a.shape, _mybir.dt.from_np(a.dtype), kind="ExternalInput").ap())
    shape = inputs['L0_attn_x'].shape
    experts, tile = 8, 256
    tokens = shape[0] * shape[1]
    out = nc.dram_tensor("out_0_dram", (tokens + (3 * experts + 2) * tile, shape[2]), _mybir.dt.float32, kind="ExternalOutput").ap()
    adaln_spiking_moe_layer(nc, *args, out)
    r = _run(nc, [arrays], core_ids=[0])
    return r.results[0]["out_0_dram"][:tokens].reshape(shape)
```

```python
import math

import concourse.bass as bass
from concourse import mybir
from contextlib import ExitStack

FP32 = mybir.dt.float32
I32 = mybir.dt.int32
BF16 = mybir.dt.bfloat16
ALU = mybir.AluOpType
ACT = mybir.ActivationFunctionType
AX = mybir.AxisListType

THRESH = 0.05
BETA = 0.3
WKV_EPS = 1e-6
LN_EPS = 1e-5
GATE_MIN = 0.25
MASKED = -3.0e38


def adaln_spiking_moe_layer(nc, x, W_r, b_r, W_k, b_k, W_v, b_v, W_td, b_td, global_decay, ln1_w, c_attn_w,
                            c_proj_w, ln2_w, router_w, w1, w2, c, wmod, out):
    B, T, D = x.shape
    P = 128
    NT = T // P
    HEADS, HD = 16, 8
    QUADS = 4
    HQ = HEADS // QUADS
    E = router_w.shape[1]
    F = w1.shape[1] // E
    FH = F // P
    SCORES = P * NT * (NT + 1) // 2
    NBLK = NT * (NT + 1) // 2
    TERMS = 6
    SPLIT = 3
    PROD = TERMS * HD
    SHIFT = 96
    G = B // NT
    U = P // G
    Q_AT = {3: 0, 2: 512, 0: 896, 1: 1024}
    K_AT = {0: 0, 1: 512, 3: 896, 2: 1024}


    TOK = B * T
    LISTS = 2 * E
    TS = 2 * P
    NS = TS // P
    CAP = TOK + TS
    ROW = 2 * D + 4
    NUM = 2 * D
    HALF = TOK // TS + E
    TILES = 2 * HALF
    TURN = 8
    AHEAD = 2
    SPARE = LISTS + AHEAD
    FILL = E
    assert out.shape[0] == TOK + (FILL + SPARE) * TS

    lists = nc.dram_tensor("lists", [LISTS * CAP + SPARE * TS, ROW], FP32).ap()
    mod_rows = nc.dram_tensor("mod_rows", [B, 3, D], FP32).ap()
    mid = nc.dram_tensor("mid", [B, P, NT, D], FP32).ap()
    q_terms = [nc.dram_tensor(f"q_terms{i}", [D, TERMS, T], BF16).ap() for i in range(2)]
    k_terms = [nc.dram_tensor(f"k_terms{i}", [D, TERMS, T], BF16).ap() for i in range(2)]
    x_v = x.rearrange("b (i p) d -> b p i d", p=P)
    x_tiles = x.rearrange("b (i p) d -> i p b d", p=P)
    out_v = out[0:TOK, :].rearrange("(b i p) d -> b p i d", p=P, i=NT)

    ctx = ExitStack()
    with ctx:
        def sb(name, shape, dt=FP32):
            return ctx.enter_context(nc.sbuf_tensor(name, shape, dt))

        def pb(name, shape):
            return ctx.enter_context(nc.psum_tensor(name, shape, FP32))

        sems = {}

        def sem(name):
            if name not in sems:
                sems[name] = ctx.enter_context(nc.semaphore(name))
            return sems[name]

        def wait(eng, name, value):
            if not isinstance(value, int) or value > 0:
                eng.wait_ge(sem(name), value)

        def wait_apart(eng, who, name, value):
            wait(eng, name, value)
            if not isinstance(value, int):
                eng.sem_inc(sem(f"{who}_passed"), 1)

        def ds(b):
            return slice(b, b + 1) if isinstance(b, int) else bass.ds(b, 1)

        def dram(ap, b):
            return ap[ds(b)].rearrange("o p i d -> (o p) i d")

        row_all = sb("row_all", [P, B, T])
        ident = sb("ident", [P, P])
        ident_h = sb("ident_h", [P, P], BF16)
        causal = sb("causal", [P, P], BF16)
        half = sb("half", [P, NT])
        wT = sb("wT", [P, 3, D])
        wqkv = sb("wqkv", [P, 3 * D])
        wproj = sb("wproj", [P, D])
        wrout = sb("wrout", [P, E])
        cols = sb("cols", [P, 8])
        BR, BK, BV, TD, GD, LN1, LN2 = (cols[:, i:i + 1] for i in range(7))
        mod_cm = sb("mod_cm", [P, 3, B])

        ARENA = 26 * 1024
        arena = sb("arena", [P, ARENA])

        def carver():
            at = [0]

            def take(n, dt=FP32):
                words = n if dt == FP32 else n // 2
                v = arena[:, at[0]:at[0] + words]
                at[0] += words
                assert at[0] <= ARENA, at[0]
                return v if dt == FP32 else v.bitcast(dt)
            return take

        take = carver()
        c_in = take(D)
        wmod_in = take(6 * D)
        w_in = take(3 * D).rearrange("p (a d) -> p a d", a=3)
        silu_c = take(B)
        silu_t = take(2 * B).rearrange("p (a b) -> p a b", a=2)
        gate_t = take(2 * B).rearrange("p (a b) -> p a b", a=2)
        row_t = take(3 * D).rearrange("p (a d) -> p a d", a=3)
        row_g = take(2 * D).rearrange("p (a d) -> p a d", a=2)

        def two(n):
            return [take(n) for _ in range(2)]

        a_x = [v.rearrange("p (i d) -> p i d", i=NT) for v in two(T)]
        a_stats = [v.rearrange("p (i s) -> p i s", i=NT) for v in two(NT * 6)]
        a_mv = [v.rearrange("p (i s) -> p i s", i=NT) for v in two(NT * 2)]
        a_var = two(NT)
        a_rstd = two(NT)
        a_xhat = [v.rearrange("p (i d) -> p i d", i=NT) for v in two(T)]
        a_hT = two(T)
        a_ek = two(T)
        a_er = two(T)
        a_er1, a_kv, a_sa, a_sb, a_num, a_den0, a_den, a_rec = (take(T) for _ in range(8))

        take = carver()
        q_stack = [take(HEADS * T, BF16).rearrange("p (h t) -> p h t", h=HEADS) for _ in range(2)]
        k_stack = [take(HEADS * T, BF16).rearrange("p (h t) -> p h t", h=HEADS) for _ in range(2)]
        probs = [take(HQ * SCORES).rearrange("p (h s) -> p h s", h=HQ) for _ in range(2)]

        take = carver()
        w_all = take(E * 2 * FH * P).rearrange("p (e w) -> p e w", e=E)
        w_tile = [take(2 * FH * P) for _ in range(4)]
        x_tile = [take(NS * ROW).rearrange("p (i w) -> p i w", i=NS) for _ in range(TURN)]
        xT_tile = [take(TS) for _ in range(2)]
        hid = [take(FH * TS).rearrange("p (f t) -> p f t", f=FH) for _ in range(2)]
        res = [take(TS).rearrange("p (i d) -> p i d", i=NS) for _ in range(TURN)]
        NTAB = TILES + AHEAD
        t_ge, t_lt, t_in, t_at, t_row = (take(NTAB * LISTS).rearrange("p (t l) -> p t l", l=LISTS) for _ in range(5))
        t_no, t_first, t_rows, t_sum, t_free, t_spare = (take(NTAB) for _ in range(6))
        n_gt = take(LISTS * (TOK // TS)).rearrange("p (l j) -> p l j", l=LISTS)
        n_cnt, n_tiles, n_exc, n_end, n_first, n_exp, l_cap = (take(LISTS) for _ in range(7))
        n_used = take(4)
        fill_rows = take(FILL * NS * ROW).rearrange("p (n w) -> p n w", w=ROW)

        v_aug = [sb(f"v_aug{i}", [P, NT, HEADS, HD + 1]) for i in range(2)]

        def buf(name):
            return sb(name, [P, NT, D])

        f_x, f_x1, f_z, f_h, b_y, b_x2, b_x1 = (buf(n) for n in (
            "f_x", "f_x1", "f_z", "f_h", "b_y", "b_x2", "b_x1"))
        f_spk = sb("f_spk", [P, T])
        f_z1T = f_spk
        f_fp = sb("f_fp", [P, 2, T])
        f_parts = sb("f_parts", [P, 2, SPLIT, T], BF16)
        f_v = sb("f_v", [P, NT, D])
        f_mod = sb("f_mod", [P, 2, D])
        b_gate = [sb(f"b_gate{i}", [P, D]) for i in range(2)]
        rows = [[sb(f"rows{i}{c}", [P, NT, ROW]) for c in range(2)] for i in range(2)]
        place = sb("place", [P, E])
        r_lg = sb("r_lg", [P, NT, E])
        r_l2 = sb("r_l2", [P, NT, E])
        r_eq = sb("r_eq", [P, NT, E])
        r_k = sb("r_k", [P, NT, E])
        r_m = sb("r_m", [P, 2, NT])
        r_f = sb("r_f", [P, NT])
        r_d = sb("r_d", [P, NT])
        r_e2 = sb("r_e2", [P, NT])
        r_s = sb("r_s", [P, NT])
        r_w = sb("r_w", [P, 2, NT])
        r_one = sb("r_one", [P, NT, 2, E])
        r_oneh = sb("r_oneh", [P, NT, 2 * E], BF16)
        r_pos = sb("r_pos", [P, NT, 2 * E])
        r_hit = sb("r_hit", [P, NT, 2 * E])
        r_row = sb("r_row", [P, NT, 2])
        r_slot = sb("r_slot", [P, NT, 2], I32)
        r_next = sb("r_next", [P, 2 * E])
        before = sb("before", [P, P], BF16)
        ones_h = sb("ones_h", [P, P], BF16)
        zero_row = sb("zero_row", [P, NUM])[:]
        spare_no = sb("spare_no", [P, SPARE * NS, 4], I32)
        two_T = sb("two_T", [P, NT], I32)
        tile_no = sb("tile_no", [1, NTAB], I32)
        tab = sb("tab", [1, 2 * NTAB + LISTS], I32)
        b_yT = sb("b_yT", [P, T])
        b_z2T = b_yT
        ln_stats = [sb(f"ln_stats{i}", [P, NT, 6]) for i in range(3)]
        ln_mv = [sb(f"ln_mv{i}", [P, NT, 2]) for i in range(3)]
        ln_var = [sb(f"ln_var{i}", [P, NT]) for i in range(3)]
        ln_rstd = [sb(f"ln_rstd{i}", [P, NT]) for i in range(3)]
        blkmax = [sb(f"blkmax{i}", [P, HQ, NBLK]) for i in range(2)]
        rowmax = [sb(f"rowmax{i}", [P, HQ, NT]) for i in range(2)]
        shift = [sb(f"shift{i}", [HQ * NT, 2, P], BF16) for i in range(2)]
        o_sb = sb("o_sb", [P, T])
        max_T = [sb(f"max_T{i}", [HQ * NT, P]) for i in range(2)]
        o_rec = sb("o_rec", [P, NT, HQ])
        m_in = f_fp[:, 0, 0:B * U].rearrange("p (b u) -> p b u", b=B)
        m_out = f_fp[:, 1, 0:B * U].rearrange("p (b u) -> p b u", b=B)
        m_tmp = b_gate[0][:, 0:B]
        state = b_gate[1][:, 0:2 * B].rearrange("p (a b) -> p a b", a=2)

        S_ps = pb("S_ps", [P, 3 * 512])
        T_ps = pb("T_ps", [P, 3 * 512])
        O_ps = pb("O_ps", [P, 512])
        M_ps = pb("M_ps", [P, 512])
        max_ps, logits_ps, ranks_ps = M_ps[0:HQ * NT, 0:P], M_ps[:, 0:NT * E], M_ps[:, 0:(NT + 1) * LISTS]
        M_tiles = M_ps[:, :].rearrange("p (i d) -> p i d", i=NT)

        def bcast(ap, shape):
            return ap.broadcast_to(shape)

        JOBS = [("route", 0, -2), ("max", 0, 1), ("o", 0, -2), ("spk", 0, 2),
                ("max", 1, 2), ("o", 1, -1), ("y", 1, -1),
                ("proj", 2, -1), ("max", 2, 3), ("o", 2, 0), ("rank", 2, -2), ("z1", 2, 2),
                ("q", 3, 2), ("max", 3, 4), ("o", 3, 1), ("k", 3, 2), ("v", 3, 2), ("z2", 3, -1)]
        READER = {"o": "y_made", "max": "max_out", "spk": "x1_made", "route": "logits_made", "y": "yT_made",
                  "proj": "x2_made", "z1": "z1T_made", "q": "q_out", "k": "k_out", "v": "v_out", "z2": "z2T_made",
                  "rank": "pos_made"}
        PER_QUAD = ("o", "max")

        def job_index(job, k):
            kind, _, lag = job
            n = QUADS * k + lag if kind in PER_QUAD else k + lag
            last = QUADS * B if kind in PER_QUAD else B
            return n if not isinstance(k, int) or 0 <= n < last else None

        def wait_M_free(eng, kind, u, k):
            at = next(i for i, j in enumerate(JOBS) if j[0] == kind and j[1] == u)
            back = 0
            while True:
                at -= 1
                if at < 0:
                    at, back = len(JOBS) - 1, back + 1
                if back > 2:
                    return
                n = job_index(JOBS[at], k - back)
                if n is not None:
                    wait(eng, READER[JOBS[at][0]], n + 1)
                    return

        STEPS = 12

        def there(b):
            return not isinstance(b, int) or 0 <= b < B

        def iterations(run):
            def program(eng):
                for k in range(-2, 4):
                    run(k, k % 2)
                with eng.Fori(2, B // 2 - 1) as i:
                    run(i * 2, 0)
                    run(i * 2 + 1, 1)
                for k in range(B - 2, B + 2):
                    run(k, k % 2)
            return program

        def fill_up(eng, choice):
            eng.wait_ge(sem("fill_set"), 1)
            eng.wait_ge(sem("tab_made"), 1)
            for e in range(E):
                i = choice * E + e
                end = eng.value_load(tab[0:1, 2 * NTAB + i:2 * NTAB + i + 1], min_val=i * CAP, max_val=i * CAP + TOK)
                eng.dma_start(lists[bass.ds(end, TS), :].rearrange("(i p) w -> p i w", p=P),
                              fill_rows[:, e * NS:(e + 1) * NS, :]).then_inc(sem(f"filled{choice}"), 16)

        block = ctx.enter_context(nc.Block())

        @block.sync
        def _(sp):
            for dst, src in ((c_in[0:B, :], c), (wmod_in, wmod), (w_in[:, 0], W_r), (w_in[:, 1], W_k), (w_in[:, 2], W_v),
                             (wqkv[:], c_attn_w), (wproj[:], c_proj_w), (wrout[:], router_w)):
                sp.dma_start(dst, src).then_inc(sem("weights_in"), 16)
            for i, v in enumerate((b_r, b_k, b_v, b_td, global_decay, ln1_w, ln2_w)):
                sp.dma_start(cols[:, i:i + 1], v.rearrange("(p o) -> p o", o=1)).then_inc(sem("weights_in"), 16)
            def load_x(i, g):
                c = i * G + g
                wait_apart(sp, "sp", "xhat_a", c - 1)
                sp.dma_start(a_x[g % 2], x_tiles[ds(i), :, g * NT:(g + 1) * NT, :].rearrange("o p b d -> (o p) b d")
                             ).then_inc(sem(f"x_in{g % 2}"), 16)
            load_x(0, 0)
            load_x(0, 1)
            sp.wait_ge(sem("rows_made"), 1)
            sp.dma_start(mod_rows, row_t[0:B]).then_inc(sem("rows_saved"), 16)
            for g in range(2, G):
                load_x(0, g)
            with sp.Fori(1, NT) as i:
                for g in range(G):
                    load_x(i, g)
            sp.wait_ge(sem("rows_saved"), 16)

            sp.wait_ge(sem("spare_set"), 2)
            sp.dma_start(out[TOK:TOK + (FILL + SPARE) * TS, :].rearrange("(n p i) d -> p n (i d)", p=P, i=NS),
                         bcast(zero_row.rearrange("p (o w) -> p o w", o=1), [P, FILL + SPARE, TS])
                         ).then_inc(sem("spare_saved"), 16)
            free = lists[LISTS * CAP:LISTS * CAP + SPARE * TS, :].rearrange("(n p) w -> p n w", p=P)
            sp.dma_start(free[:, :, 0:NUM], bcast(zero_row.rearrange("p (o w) -> p o w", o=1), [P, SPARE * NS, NUM])
                         ).then_inc(sem("spare_saved"), 16)
            sp.dma_start(free[:, :, NUM:ROW].bitcast(I32), spare_no[:]
                         ).then_inc(sem("spare_saved"), 16)

            def shift_rows(k, p, q):
                n = QUADS * k + q
                b, u, pp = k + q // QUADS, q % QUADS, (p + q // QUADS) % 2
                if there(b):
                    wait_apart(sp, "sp", "shift_made", n + 1)
                    for r in range(2):
                        dst = q_stack[pp][SHIFT + r:SHIFT + r + 1, HQ * u:HQ * (u + 1), :]
                        sp.dma_start(dst.rearrange("o h (i t) -> o (h i) t", i=NT),
                                     shift[u % 2][:, r, :]).then_inc(sem(f"shift_in{u % 2}"), 16)

            def run(k, p):
                if there(k + 2):
                    load_front(k + 2)
                shift_rows(k, p, 1)
                if there(k + 1):
                    b, pp = k + 1, 1 - p
                    wait_apart(sp, "sp", "parts_made", b + 1)
                    wait_apart(sp, "sp", "stacks_in", 32 * (b - 1))
                    q1, q2, q3 = (f_parts[:, 0, i:i + 1, :] for i in range(3))
                    sp.dma_start(q_terms[pp][:, 0:3], bcast(q1, [D, 3, T])).then_inc(sem("terms_out"), 16)
                    sp.dma_start(q_terms[pp][:, 3:5], bcast(q2, [D, 2, T])).then_inc(sem("terms_out"), 16)
                    sp.dma_start(q_terms[pp][:, 5:6], q3).then_inc(sem("terms_out"), 16)
                    sp.dma_start(k_terms[pp][:, 0:3], f_parts[:, 1, 0:3]).then_inc(sem("terms_out"), 16)
                    sp.dma_start(k_terms[pp][:, 3:5], f_parts[:, 1, 0:2]).then_inc(sem("terms_out"), 16)
                    sp.dma_start(k_terms[pp][:, 5:6], f_parts[:, 1, 0:1]).then_inc(sem("terms_out"), 16)
                    wait_apart(sp, "sp", "terms_out", 96 * (b + 1))
                    wait_apart(sp, "sp", "T_mm", HEADS * (b - 1))
                    if isinstance(b, int) and b < 2:
                        sp.wait_ge(sem("pads_set"), 1)
                    for stack, terms in ((q_stack[pp], q_terms[pp]), (k_stack[pp], k_terms[pp])):
                        sp.dma_start(stack[0:PROD], terms.rearrange("(h d) s t -> (d s) h t", d=HD)
                                     ).then_inc(sem("stacks_in"), 16)
                if there(k + 2):
                    wait_apart(sp, "sp", "x1_made", k + 3)
                    sp.dma_start(dram(mid, k + 2), f_x1[:]).then_inc(sem("x1_saved"), 16)
                shift_rows(k, p, 2)
                if there(k - 1):
                    b = k - 1
                    wait_apart(sp, "sp", "base_out", 16 * b)
                    wait_apart(sp, "sp", "x1_saved", 16 * (b + 1))
                    wait_apart(sp, "sp", "rows_gated", b - 1)
                    sp.dma_start(b_x1[:], dram(mid, b)).then_inc(sem("x1_back"), 16)
                    sp.dma_start(b_gate[1 - p][:], bcast(mod_rows[ds(b), 2, :], [P, D])).then_inc(sem("x1_back"), 16)
                shift_rows(k, p, 3)
                shift_rows(k, p, 4)
                if there(k - 1):
                    wait_apart(sp, "sp", "base_made", k)
                    sp.dma_start(dram(out_v, k - 1), b_x1[:]).then_inc(sem("base_out"), 16)

            def load_front(b):
                wait_apart(sp, "sp", "x1_made", b)
                sp.dma_start(f_x[:], dram(x_v, b)).then_inc(sem("x_in_f"), 16)
                wait_apart(sp, "sp", "h_made", b)
                sp.dma_start(f_mod[:], bcast(mod_rows[ds(b), 0:2, :], [P, 2, D])).then_inc(sem("x_in_f"), 16)

            iterations(run)(sp)
            sp.wait_ge(sem("base_out"), 16 * B)

            sp.wait_ge(sem("pv_mm"), QUADS * B)
            sp.wait_ge(sem("T_mm"), HEADS * B)
            sp.dma_start(w_all[:, :, 0:F], w1.rearrange("c (e f) -> c e f", e=E)).then_inc(sem("w12_in"), 16)
            for f in range(FH):
                sp.dma_start(w_all[:, :, F + f * D:F + (f + 1) * D],
                             w2.rearrange("(e f p) d -> f p e d", p=P, f=FH)[f]).then_inc(sem("w12_in"), 16)
            fill_up(sp, 0)
            sp.wait_ge(sem("listed"), 16 * 2 * NT * B)
            sp.wait_ge(sem("filled0"), 16 * E)
            sp.wait_ge(sem("spare_saved"), 48)

            def load_tile(t, r):
                row = sp.value_load(tab[0:1, ds(t)], min_val=0, max_val=LISTS * CAP + (SPARE - 1) * TS)
                if not (isinstance(t, int) and t < TURN):
                    wait_apart(sp, "sp", f"res_saved{r}", 16 * NS * (t // TURN if isinstance(t, int) else t_turn[0]))
                sp.dma_start(x_tile[r], lists[bass.ds(row, TS), :].rearrange("(i p) w -> p i w", p=P)
                             ).then_inc(sem(f"x_tile_in{r}"), 16)
            t_turn = [None]
            for r in range(TURN):
                load_tile(r, r)
            for first, last in ((1, HALF // TURN), (HALF // TURN, TILES // TURN)):
                if first > 1:
                    sp.wait_ge(sem("filled1"), 16 * E)
                with sp.Fori(first, last) as i:
                    t_turn[0] = i
                    for r in range(TURN):
                        load_tile(i * TURN + r, r)
            for t in range(TILES, NTAB):
                load_tile(t, t % TURN)

        @block.gpsimd
        def _(pool):
            g = nc.gpsimd
            g.memset(ident[:], 0.0).then_inc(sem("id0"), 1)
            g.memset(half[:], -0.5).then_inc(sem("half_set"), 1)
            g.memset(m_tmp, 0.0)
            g.memset(causal[:], 0.0).then_inc(sem("id0"), 1)
            pool.wait_ge(sem("id0"), 2)
            g.affine_select(out=ident[:], in_=ident[:], compare_op=ALU.not_equal, fill=1.0, base=0,
                            pattern=[[-1, P]], channel_multiplier=1).then_inc(sem("id1"), 1)
            g.affine_select(out=causal[:], in_=causal[:], compare_op=ALU.is_ge, fill=MASKED, base=0,
                            pattern=[[-1, P]], channel_multiplier=1).then_inc(sem("id1"), 1)
            pool.wait_ge(sem("id1"), 2)
            g.tensor_copy(ident_h[:], ident[:]).then_inc(sem("consts"), 1)
            g.memset(ones_h[:], 1.0).then_inc(sem("tri0"), 1)
            pool.wait_ge(sem("tri0"), 1)
            g.affine_select(out=before[:], in_=ones_h[:], compare_op=ALU.is_gt, fill=0.0, base=0,
                            pattern=[[1, P]], channel_multiplier=-1)
            g.iota(spare_no[:], [[P, SPARE * NS], [0, 4]], base=TOK + FILL * TS, channel_multiplier=1
                   ).then_inc(sem("spare_set"), 1)
            g.memset(zero_row, 0.0).then_inc(sem("spare_set"), 1)
            for i in range(2):
                for c in range(2):
                    g.memset(rows[i][c][:, :, NUM:ROW], 0.0).then_inc(sem("row_no"), 1)
            pool.wait_ge(sem("row_no"), 4)
            for i in range(2):
                for c in range(2):
                    g.iota(rows[i][c][:, :, NUM].bitcast(I32), [[P, NT]], base=(i - 2) * T, channel_multiplier=1)
            g.iota(two_T[:], [[0, NT]], base=2 * T, channel_multiplier=0).then_inc(sem("row_no"), 1)
            for v in v_aug:
                g.memset(v[:, :, :, HD:HD + 1], 1.0).then_inc(sem("ones_set"), 1)
            g.iota(tile_no[:], [[1, NTAB]], base=0, channel_multiplier=0).then_inc(sem("tiles_counted"), 1)

            pool.wait_ge(sem("half_set"), 1)

            def rstd_a(b, p):
                pool.wait_ge(sem("var_a"), b + 1)
                g.tensor_tensor(a_rstd[p], a_var[p], half[:], ALU.pow).then_inc(sem("rstd_a"), 1)
            with pool.Fori(0, B // 2) as i:
                rstd_a(i * 2, 0)
                rstd_a(i * 2 + 1, 1)

            pool.wait_ge(sem("inp_a"), B)
            for t in q_stack + k_stack:
                g.memset(t[0:SHIFT].bitcast(FP32), 0.0)
            for t in k_stack:
                last = g.memset(t[SHIFT:SHIFT + 2], 1.0)
            last.then_inc(sem("pads_set"), 1)
            pool.wait_ge(sem("pads_set"), 1)

            def rstd(i, b):
                pool.wait_ge(sem(f"var{i}"), b + 1)
                g.tensor_tensor(ln_rstd[i][:], ln_var[i][:], half[:], ALU.pow).then_inc(sem(f"rstd{i}"), 1)

            def mask(k, p, u):
                if there(k):
                    wait_apart(pool, "pool", "exp_made", HEADS * k + HQ * (u + 1))
                    for i in range(NT):
                        v = probs[u % 2][:, :, K_AT[i]:K_AT[i] + P]
                        last = g.affine_select(out=v, in_=v, compare_op=ALU.is_ge, fill=0.0, base=0,
                                               pattern=[[0, HQ], [1, P]], channel_multiplier=-1)
                    last.then_inc(sem("masked"), 1)

            def dispatch(k, p, c):
                if there(k - 3):
                    b = k - 3
                    if c == 0:
                        pool.wait_ge(sem("numbered"), 2 * b + 2)
                        pool.wait_ge(sem("slot_made"), b + 1)
                        wait_apart(pool, "pool", "rows_gated", b + 1)
                    for i in range(NT):
                        g.indirect_dma_start(lists[:, :], bass.IndirectOffsetOnAxis(ap=r_slot[:, i, c:c + 1], axis=0),
                                             rows[1 - p][c][:, i, :], None).then_inc(sem("listed"), 16)

            def run(k, p):
                if there(k + 1):
                    b = k + 1
                    pool.wait_ge(sem("split"), 3 * b + 3)
                    g.tensor_tensor(f_parts[:, :, 2, :], f_fp[:], f_parts[:, :, 1, :], ALU.subtract
                                    ).then_inc(sem("parts_made"), 1)
                if there(k + 2):
                    b = k + 2
                    rstd(0, b)
                    pool.wait_ge(sem("z_made"), b + 1)
                    pool.wait_ge(sem("x_in_f"), 32 * (b + 1))
                    wait(pool, "h_kept", b)
                    g.tensor_tensor(f_h[:], f_z[:], bcast(f_mod[:, 1:2, :], [P, NT, D]), ALU.mult
                                    ).then_inc(sem("h_half"), 1)
                    pool.wait_ge(sem("h_half"), b + 1)
                    g.tensor_tensor(f_h[:], f_h[:], bcast(f_mod[:, 0:1, :], [P, NT, D]), ALU.add
                                    ).then_inc(sem("h_made"), 1)
                mask(k, p, 0)
                dispatch(k, p, 0)
                if there(k + 2):
                    rstd(1, k + 2)
                mask(k, p, 1)
                dispatch(k, p, 1)
                if there(k - 1):
                    b = k - 1
                    rstd(2, b)
                mask(k, p, 2)
                if there(k - 1):
                    pool.wait_ge(sem("z2_made"), b + 1)
                    pool.wait_ge(sem("x1_back"), 32 * (b + 1))
                    g.tensor_tensor(b_x2[:], b_x2[:], bcast(b_gate[1 - p][:].rearrange("p (o d) -> p o d", o=1), [P, NT, D]),
                                    ALU.mult).then_inc(sem("gated"), 1)
                    pool.wait_ge(sem("gated"), b + 1)
                    g.tensor_tensor(b_x1[:], b_x1[:], b_x2[:], ALU.add).then_inc(sem("base_made"), 1)
                mask(k, p, 3)
                if there(k + 2):
                    b = k + 2
                    pool.wait_ge(sem("split"), 3 * b + 1)
                    g.tensor_tensor(f_fp[:], f_fp[:], f_parts[:, :, 0, :], ALU.subtract).then_inc(sem("split"), 1)
                if there(k - 2):
                    b = k - 2
                    pool.wait_ge(sem("z2_copied"), b + 1)
                    for c in range(2):
                        n = rows[p][c][:, :, NUM].bitcast(I32)
                        g.tensor_tensor(n, n, two_T[:], ALU.add).then_inc(sem("numbered"), 1)

            iterations(run)(pool)
            for c in range(2):
                dispatch(B + 2, B % 2, c)

            pool.wait_ge(sem("pv_mm"), QUADS * B)
            pool.wait_ge(sem("T_mm"), HEADS * B)
            g.memset(fill_rows, 0.0).then_inc(sem("fill_zero"), 1)
            pool.wait_ge(sem("fill_zero"), 1)
            g.iota(fill_rows[:, :, NUM].bitcast(I32), [[P, FILL * NS]], base=TOK, channel_multiplier=1
                   ).then_inc(sem("fill_set"), 1)

            pool.wait_ge(sem("base_out"), 16 * B)
            pool.wait_ge(sem("spare_saved"), 48)

            def add_tiles(first, turns):
                with pool.Fori(first, first + turns) as i:
                    for r in range(TURN):
                        wait_apart(pool, "pool", "res_made", i * TURN + r + 3)
                        for s in range(NS):
                            g.indirect_dma_start(out[:, :], bass.IndirectOffsetOnAxis(
                                ap=x_tile[r][:, s, NUM:NUM + 1].bitcast(I32), axis=0), res[r][:, s, :], None,
                                compute_op=ALU.add).then_inc(sem(f"res_saved{r}"), 16)
                for r in range(TURN):
                    pool.wait_ge(sem(f"res_saved{r}"), 16 * NS * (first + turns))
            add_tiles(0, HALF // TURN)
            add_tiles(HALF // TURN, HALF // TURN)

        @block.tensor
        def _(pe):
            t = nc.tensor
            pe.wait_ge(sem("consts"), 1)
            pe.wait_ge(sem("weights_in"), 16 * 15)
            for i in range(3):
                t.transpose(S_ps[:, i * D:(i + 1) * D], w_in[:, i, :], ident[:])
            t.transpose(M_ps[:, 0:B], c_in[0:B, :], ident[0:B, 0:B]).then_inc(sem("setup_tr"), 1)
            pe.wait_ge(sem("silu_made"), 1)
            for i in range(3):
                t.matmul(T_ps[:, i * B:(i + 1) * B], wmod_in[:, i * D:(i + 1) * D], silu_c, start=True, stop=True)
            t.matmul(O_ps[0:B, 0:3 * D], silu_c, wmod_in[:, 3 * D:6 * D], start=True, stop=True
                     ).then_inc(sem("mod_mm"), 1)

            pe.wait_ge(sem("setup_done"), 1)

            def spiking(b, p):
                R_ps = (S_ps, T_ps)[p]
                pe.wait_ge(sem("xhat_a"), b + 1)
                if not (isinstance(b, int) and b == 0):
                    pe.wait_ge(sem("hT_a"), b)
                for i in range(NT):
                    last = t.transpose(M_ps[:, i * P:(i + 1) * P], a_xhat[p][:, i, :], ident[:])
                last.then_inc(sem("xT_a"), 1)
                pe.wait_ge(sem("hT_a"), b + 1)
                wait(pe, "ek_a", b - 1)
                wait(pe, "kv_a", b - 1)
                for i in range(3):
                    last = t.matmul(R_ps[:, i * T:(i + 1) * T], wT[:, i, :], a_hT[p], start=True, stop=True)
                last.then_inc(sem("rkv_a"), 1)
            spiking(0, 0)
            spiking(1, 1)
            with pe.Fori(1, B // 2) as i:
                spiking(i * 2, 0)
                spiking(i * 2 + 1, 1)

            def scores(k, p, q, j, part):
                b, u, pp = k + q // QUADS, q % QUADS, (p + q // QUADS) % 2
                if not there(b):
                    return
                h = HQ * u + j
                if h == 0 and part == 0:
                    pe.wait_ge(sem("stacks_in"), 32 * (b + 1))
                wait(pe, ("blk_a_made", "blk_made")[part], HEADS * b + h)
                for i in ((3,), (2, 0, 1))[part]:
                    at = Q_AT[i]
                    t.matmul(S_ps[:, at:at + P * (i + 1)], q_stack[pp][0:SHIFT, h, P * i:P * (i + 1)],
                             k_stack[pp][0:SHIFT, h, 0:P * (i + 1)], start=True, stop=False)
                    last = t.matmul(S_ps[:, at + P * i:at + P * (i + 1)], ident_h[:], causal[:], start=False, stop=True)
                last.then_inc(sem(("S_a_mm", "S_mm")[part]), 1)

            def shifted(k, p, u, j, part):
                if not there(k):
                    return
                h = HQ * u + j
                if j == 0 and part == 0:
                    n = QUADS * k + u
                    pe.wait_ge(sem(f"shift_in{u % 2}"), (n - u % 2) * 16 + 32)
                wait(pe, ("exp_a_made", "exp_made")[part], HEADS * k + h)
                for i in ((0,), (1, 3, 2))[part]:
                    last = t.matmul(T_ps[:, K_AT[i]:K_AT[i] + T - P * i], k_stack[p][0:SHIFT + 2, h, P * i:P * (i + 1)],
                                    q_stack[p][0:SHIFT + 2, h, P * i:T], start=True, stop=True)
                last.then_inc(sem(("T_a_mm", "T_mm")[part]), 1)

            def values(k, p, q):
                b, u, pp = k + q // QUADS, q % QUADS, (p + q // QUADS) % 2
                if not there(b):
                    return
                n = QUADS * k + q
                if u == 0:
                    pe.wait_ge(sem("v_put"), b + 1)
                pe.wait_ge(sem("masked"), n + 1)
                wait(pe, "o_out", n)
                for i in range(NT):
                    for j in range(HQ):
                        last = t.matmul(O_ps[32 * j:32 * j + HD + 1, P * i:T], v_aug[pp][:, i, HQ * u + j, :],
                                        probs[u % 2][:, j, K_AT[i]:K_AT[i] + T - P * i],
                                        start=(i == 0), stop=(i == NT - 1))
                last.then_inc(sem("pv_mm"), 1)

            def transposes(kind, k, u, ready, count, src, done, n=NT):
                if job_index(next(j for j in JOBS if j[0] == kind and j[1] == u), k) is None:
                    return
                pe.wait_ge(sem(ready), count)
                wait_M_free(pe, kind, u, k)
                for i in range(n):
                    last = t.transpose(M_ps[:, i * P:(i + 1) * P], src(i), ident[:])
                last.then_inc(sem(done), 1)

            def run(k, p):
                for u in range(QUADS):
                    for j in range(HQ):
                        scores(k, p, u + 2, j, 0)
                        shifted(k, p, u, j, 0)
                        if j == 1 and job_index(("max", u, u + 1), k) is not None:
                            n = QUADS * k + u + 1
                            pe.wait_ge(sem("max_made"), n + 1)
                            wait_M_free(pe, "max", u, k)
                            t.transpose(max_ps, rowmax[(u + 1) % 2][:].rearrange("p h i -> p (h i)"),
                                        ident[:]).then_inc(sem("max_tr"), 1)
                        if (u, j) == (0, 3):
                            transposes("spk", k, u, "spk_made", k + 3, lambda i: f_spk[:, i * P:(i + 1) * P], "spk_tr")
                        if (u, j) == (1, 3):
                            transposes("y", k, u, "y_made", QUADS * k, lambda i: b_y[:, i, :], "y_tr")
                        if (u, j) == (2, 0) and there(k - 1):
                            pe.wait_ge(sem("yT_made"), k)
                            for i in range(NT):
                                last = t.matmul(M_ps[:, i * P:(i + 1) * P], b_yT[:, i * P:(i + 1) * P], wproj[:],
                                                start=True, stop=True)
                            last.then_inc(sem("proj_mm"), 1)
                        if (u, j) == (3, 3) and there(k + 2):
                            wait_M_free(pe, "v", u, k)
                            for i in range(NT):
                                last = t.matmul(M_ps[:, i * P:(i + 1) * P], f_z1T[:, i * P:(i + 1) * P],
                                                wqkv[:, 2 * D:3 * D], start=True, stop=True)
                            last.then_inc(sem("v_mm"), 1)
                        scores(k, p, u + 2, j, 1)
                        shifted(k, p, u, j, 1)
                        if (u, j) == (0, 0) and there(k - 2):
                            pe.wait_ge(sem("z2T_made"), k - 1)
                            wait_M_free(pe, "route", u, k)
                            for i in range(NT):
                                last = t.matmul(logits_ps[:, i * E:(i + 1) * E], b_z2T[:, i * P:(i + 1) * P], wrout[:],
                                                start=True, stop=True)
                            last.then_inc(sem("route_mm"), 1)
                        if j == 1:
                            n = QUADS * k + u - 2
                            transposes("o", k, u, "o_out", n + 1, lambda i: o_sb[:, i * P:(i + 1) * P], "o_tr")
                        if (u, j) == (2, 2) and there(k - 2):
                            pe.wait_ge(sem("routing"), STEPS * (k - 1))
                            wait_M_free(pe, "rank", u, k)
                            for i in range(NT):
                                for a in range(i):
                                    t.matmul(ranks_ps[:, i * LISTS:(i + 1) * LISTS], ones_h[:], r_oneh[:, a, :],
                                             start=(a == 0), stop=False)
                                t.matmul(ranks_ps[:, i * LISTS:(i + 1) * LISTS], before[:], r_oneh[:, i, :],
                                         start=(i == 0), stop=True)
                            for i in range(NT):
                                last = t.matmul(ranks_ps[:, NT * LISTS:(NT + 1) * LISTS], ones_h[:],
                                                r_oneh[:, i, :], start=(i == 0), stop=(i == NT - 1))
                            last.then_inc(sem("rank_mm"), 1)
                        if (u, j) == (2, 3):
                            transposes("z1", k, u, "z1_made", k + 3, lambda i: f_z[:, i, :], "z1_tr")
                        if (u, j) in ((3, 0), (3, 2)) and there(k + 2):
                            i = j // 2
                            pe.wait_ge(sem("z1T_made"), k + 3)
                            wait_M_free(pe, "qk"[i], u, k)
                            t.matmul(M_ps[:, :], wqkv[:, i * D:(i + 1) * D], f_z1T[:], start=True, stop=True
                                     ).then_inc(sem("qk"[i] + "_mm"), 1)
                        if (u, j) == (3, 3):
                            transposes("z2", k, u, "z2_made", k, lambda i: rows[1 - p][0][:, i, 0:D], "z2_tr")
                    values(k, p, u - 1)

            iterations(run)(pe)

            pe.wait_ge(sem("exp_made"), HEADS * B)
            pe.wait_ge(sem("blk_made"), HEADS * B)

            def R(r):
                return (S_ps, T_ps)[r % 2]

            def turn_over(n, r):
                pe.wait_ge(sem(f"x_tile_in{r % TURN}"), 16 * n_use(n, r))
                pe.wait_ge(sem("xT_made"), n + 1)
                for s in range(NS):
                    last = t.transpose(R(r)[:, s * P:(s + 1) * P], x_tile[r % TURN][:, s, 0:D], ident[:])
                last.then_inc(sem("x_tr"), 1)

            def n_use(n, r):
                return n // TURN + 1 if isinstance(n, int) else turn[0] + (1 if r < TURN else 2)

            def up(n, r):
                pe.wait_ge(sem("xT_made"), n + 3)
                pe.wait_ge(sem("w_made"), n + 1)
                pe.wait_ge(sem("gelu_made"), n + 1)
                for f in range(FH):
                    last = t.matmul(R(r)[:, 512 + f * TS:512 + (f + 1) * TS], w_tile[r % 4][:, f * P:(f + 1) * P],
                                    xT_tile[r % 2], start=True, stop=True)
                last.then_inc(sem("up_mm"), 1)

            def down(n, r):
                pe.wait_ge(sem("gelu_made"), n + 3)
                pe.wait_ge(sem("res_made"), n + 1)
                for s in range(NS):
                    for f in range(FH):
                        last = t.matmul(R(r)[:, 1024 + s * P:1024 + (s + 1) * P], hid[r % 2][:, f, s * P:(s + 1) * P],
                                        w_tile[r % 4][:, F + f * D:F + (f + 1) * D], start=(f == 0), stop=(f == FH - 1))
                last.then_inc(sem("down_mm"), 1)
            turn = [None]
            pe.sem_inc(sem("up_mm"), 2)
            pe.sem_inc(sem("down_mm"), 2)
            turn_over(0, 0)
            turn_over(1, 1)
            up(0, 0)
            with pe.Fori(0, TILES // TURN) as i:
                turn[0] = i
                for r in range(TURN):
                    turn_over(i * TURN + (r + 2), r + 2)
                    up(i * TURN + (r + 1), r + 1)
                    down(i * TURN + r, r)

        @block.scalar
        def _(act):
            a = nc.scalar
            act.wait_ge(sem("setup_tr"), 1)
            a.activation(silu_t[:, 0, :], M_ps[:, 0:B], ACT.Exp, scale=-1.0).then_inc(sem("silu_exp"), 1)
            act.wait_ge(sem("weights_in"), 16 * 15)
            a.activation(cols[:, 3:5], cols[:, 3:5], ACT.Exp).then_inc(sem("decay_exp"), 1)
            act.wait_ge(sem("setup_done"), 1)

            def spiking(i, g):
                c, p = i * G + g, g % 2
                R_ps = (S_ps, T_ps)[p]
                act.wait_ge(sem("xT_a"), c + 1)
                wait(act, "rkv_a", c - 1)
                for j in range(NT):
                    b = g * NT + j
                    last = a.activation(a_hT[p][:, j * P:(j + 1) * P], M_ps[:, j * P:(j + 1) * P], ACT.Identity,
                                        bias=mod_cm[:, 0, b:b + 1], scale=mod_cm[:, 1, b:b + 1])
                last.then_inc(sem("hT_a"), 1)
                act.wait_ge(sem("rkv_a"), c + 1)
                wait(act, "inp_a", c - 1)
                a.activation(a_er[p], R_ps[:, 0:T], ACT.Exp, bias=BR, scale=-1.0)
                a.activation(a_ek[p], R_ps[:, T:2 * T], ACT.Exp, bias=BK).then_inc(sem("ek_a"), 1)
            for g in range(G):
                spiking(0, g)
            with act.Fori(1, NT) as i:
                for g in range(G):
                    spiking(i, g)

            def run(k, p):
                for u in range(QUADS):
                    for j in range(HQ):
                        if there(k):
                            h = HQ * u + j
                            if j == 0:
                                wait(act, "pv_mm", QUADS * k + u - 1)
                            act.wait_ge(sem("T_a_mm"), HEADS * k + h + 1)
                            a.activation(probs[u % 2][:, j, 0:T], T_ps[:, 0:T], ACT.Exp).then_inc(sem("exp_a_made"), 1)
                        n = QUADS * k + u + 1
                        if j == 1 and job_index(("max", u, u + 1), k) is not None:
                            act.wait_ge(sem("max_tr"), n + 1)
                            v = (u + 1) % 2
                            wait(act, f"shift_in{v}", (n - v) * 16)
                            a.mul(shift[v][:, 0, :], max_ps, -1.0).then_inc(sem("shift_hi"), 1)
                            wait_apart(act, "act", "shift_made", n - 1)
                            a.copy(max_T[v][:], max_ps).then_inc(sem("max_out"), 1)
                        if (u, j) == (1, 3) and there(k - 1):
                            wait_apart(act, "act", "route_mm", k - 1)
                            act.wait_ge(sem("y_tr"), k)
                            wait(act, "proj_mm", k - 1)
                            a.copy(b_yT[:], M_ps[:, :]).then_inc(sem("yT_made"), 1)
                        if (u, j) == (3, 3) and there(k + 2):
                            act.wait_ge(sem("v_mm"), k + 3)
                            wait(act, "v_put", k + 2)
                            a.copy(f_v[:].rearrange("p i d -> p (i d)"), M_ps[:, :]).then_inc(sem("v_out"), 1)
                        if there(k):
                            act.wait_ge(sem("T_mm"), HEADS * k + h + 1)
                            a.activation(probs[u % 2][:, j, T:SCORES], T_ps[:, T:SCORES], ACT.Exp
                                         ).then_inc(sem("exp_made"), 1)
                        if (u, j) == (0, 1) and there(k + 1):
                            wait_apart(act, "act", "split", 3 * (k + 1) + 2)
                            a.copy(f_parts[:, :, 1, :], f_fp[:]).then_inc(sem("split"), 1)
                        if (u, j) == (1, 1) and there(k + 1):
                            wait(act, "pv_mm", QUADS * k)
                            wait_apart(act, "act", "v_out", k + 2)
                            a.copy(v_aug[1 - p][:, :, :, 0:HD], f_v[:].rearrange("p i (h d) -> p i h d", h=HEADS)
                                   ).then_inc(sem("v_put"), 1)
                        if (u, j) == (2, 0) and there(k + 2):
                            wait_apart(act, "act", "h_made", k + 3)
                            a.copy(row_all[:, ds(k + 2), :].rearrange("p o t -> p (o t)"),
                                   f_h[:].rearrange("p i d -> p (i d)")).then_inc(sem("h_kept"), 1)
                        if (u, j) == (2, 1) and there(k - 2):
                            wait_apart(act, "act", "margin_made", k - 1)
                            wait_apart(act, "act", "weights_made", k - 2)
                            a.activation(r_e2[:], r_d[:], ACT.Exp).then_inc(sem("gates_exp"), 1)
                        if (u, j) == (3, 1) and there(k - 1):
                            wait_apart(act, "act", "z2_made", k)
                            a.copy(rows[1 - p][1][:, :, 0:D], rows[1 - p][0][:, :, 0:D]).then_inc(sem("z2_copied"), 1)
                        if (u, j) == (2, 3) and there(k + 2):
                            wait_apart(act, "act", "spk_tr", k + 3)
                            act.wait_ge(sem("z1_tr"), k + 3)
                            wait(act, "v_mm", k + 2)
                            a.copy(f_z1T[:], M_ps[:, :]).then_inc(sem("z1T_made"), 1)
                        if (u, j) in ((3, 0), (3, 2)) and there(k + 2):
                            i = j // 2
                            act.wait_ge(sem("qk"[i] + "_mm"), k + 3)
                            wait(act, "parts_made", k + 2)
                            a.copy(f_fp[:, i, :], M_ps[:, :]).then_inc(sem("qk"[i] + "_out"), 1)
                        if (u, j) == (3, 3):
                            if there(k - 1):
                                wait_apart(act, "act", "proj_mm", k)
                                act.wait_ge(sem("z2_tr"), k)
                                wait(act, "route_mm", k - 1)
                                a.copy(b_z2T[:], M_ps[:, :]).then_inc(sem("z2T_made"), 1)
                            if there(k + 2):
                                wait_apart(act, "act", "k_out", k + 3)
                                wait_apart(act, "act", "terms_out", 96 * (k + 2))
                                a.copy(f_parts[:, :, 0, :], f_fp[:]).then_inc(sem("split"), 1)
                    n = QUADS * k + u - 1
                    if job_index(("o", 0, u - 1), k) is not None:
                        act.wait_ge(sem("pv_mm"), n + 1)
                        wait(act, "o_tr", n)
                        a.copy(o_sb[:], O_ps[:, :]).then_inc(sem("o_out"), 1)

            iterations(run)(act)

            fill_up(act, 1)
            act.wait_ge(sem("pv_mm"), QUADS * B)

            def turned(n, r):
                act.wait_ge(sem("x_tr"), n + 1)
                act.wait_ge(sem("up_mm"), n + 1)
                a.activation(xT_tile[r % 2], (S_ps, T_ps)[r % 2][:, 0:TS], ACT.Identity, scale=LN2
                             ).then_inc(sem("xT_made"), 1)

            def gelu(n, r):
                act.wait_ge(sem("up_mm"), n + 3)
                act.wait_ge(sem("down_mm"), n + 1)
                a.activation(hid[r % 2].rearrange("p f t -> p (f t)"), (S_ps, T_ps)[r % 2][:, 512:512 + FH * TS], ACT.Gelu
                             ).then_inc(sem("gelu_made"), 1)
            act.sem_inc(sem("xT_made"), 2)
            act.sem_inc(sem("gelu_made"), 2)
            turned(0, 0)
            turned(1, 1)
            gelu(0, 0)
            with act.Fori(0, TILES // TURN) as i:
                for r in range(TURN):
                    turned(i * TURN + (r + 2), r)
                    gelu(i * TURN + (r + 1), r + 1)

        @block.vector
        def _(dve):
            v = nc.vector
            n_setup = [0]

            def link(ins):
                n_setup[0] += 1
                ins.then_inc(sem("setup_dve"), 1)
                dve.wait_ge(sem("setup_dve"), n_setup[0])

            v.memset(O_ps[:, :], 0.0)
            dve.wait_ge(sem("setup_tr"), 1)
            v.tensor_copy(wT[:].rearrange("p a d -> p (a d)"), S_ps[:, 0:3 * D])
            dve.wait_ge(sem("silu_exp"), 1)
            link(v.tensor_scalar_add(silu_t[:, 1, :], silu_t[:, 0, :], 1.0))
            link(v.reciprocal(silu_t[:, 0, :], silu_t[:, 1, :]))
            v.tensor_tensor(silu_c, M_ps[:, 0:B], silu_t[:, 0, :], ALU.mult).then_inc(sem("silu_made"), 1)
            dve.wait_ge(sem("mod_mm"), 1)

            def gate(dst, src, t1, t2):
                link(v.tensor_scalar(t1, src, 0.0, 2.0, ALU.is_ge, ALU.mult))
                link(v.scalar_tensor_tensor(t2, t1, -1.0, src, ALU.add, ALU.mult))
                link(v.tensor_scalar(t2, t2, GATE_MIN, None, ALU.max))
                link(v.scalar_tensor_tensor(dst, t1, -1.0, t2, ALU.add, ALU.mult))
            v.tensor_copy(mod_cm[:, 0, :], T_ps[:, 0:B])
            v.tensor_scalar_add(mod_cm[:, 1, :], T_ps[:, B:2 * B], 1.0)
            gate(mod_cm[:, 2, :], T_ps[:, 2 * B:3 * B], gate_t[:, 0, :], gate_t[:, 1, :])
            v.tensor_copy(row_t[0:B, 0, :], O_ps[0:B, 0:D])
            v.tensor_scalar_add(row_t[0:B, 1, :], O_ps[0:B, D:2 * D], 1.0)
            gate(row_t[0:B, 2, :], O_ps[0:B, 2 * D:3 * D], row_g[0:B, 0, :], row_g[0:B, 1, :])
            dve.sem_inc(sem("rows_made"), 1)
            dve.wait_ge(sem("decay_exp"), 1)
            v.tensor_scalar_mul(BR, BR, -1.0)
            link(v.tensor_scalar(wqkv[:, 0:D], wqkv[:, 0:D], LN1, 1.0 / math.sqrt(HD), ALU.mult, ALU.mult))
            v.tensor_scalar(wqkv[:, D:3 * D], wqkv[:, D:3 * D], LN1, None, ALU.mult)
            link(v.tensor_scalar(wrout[:], wrout[:], LN2, None, ALU.mult))
            for e in range(E):
                v.memset(place[:, e:e + 1], float(E - e))
            for i in range(LISTS):
                last = v.memset(r_next[:, i:i + 1], float(i * CAP))
            last.then_inc(sem("places_set"), 1)
            v.memset(O_ps[:, :], 0.0).then_inc(sem("setup_done"), 1)

            def stats(x_t, st, mv, var, name, n, count):
                for i in range(NT):
                    last = v.bn_stats(st[:, i, :], x_t[:, i, :])
                last.then_inc(sem(name + "_c"), 1)
                wait_apart(dve, "dve", name + "_c", 2 * n + 1)
                for i in range(NT):
                    last = v.bn_aggr(mv[:, i, :], st[:, i, :])
                last.then_inc(sem(name + "_c"), 1)
                dve.wait_ge(sem(name + "_c"), 2 * n + 2)
                v.tensor_scalar_add(var, mv[:, :, 1], LN_EPS).then_inc(sem(name), 1)

            def normalise(dst, x_t, mv, rstd):
                for i in range(NT):
                    last = v.tensor_scalar(dst[:, i, 0:D], x_t[:, i, :], mv[:, i, 0:1], rstd[:, i:i + 1],
                                           ALU.subtract, ALU.mult)
                return last

            FRONT = 3 * NT + 1
            BACK = 3 * NT + 8

            def front_step(n, c, p):
                x_t, st, mv = a_x[p], a_stats[p], a_mv[p]
                if n < NT:
                    if isinstance(c, int) and c + 1 >= B:
                        return
                    if n == 0:
                        dve.wait_ge(sem("rstd_a"), c + 2)
                        wait(dve, "xT_a", c)
                    q = 1 - p
                    ins = v.tensor_scalar(a_xhat[q][:, n, :], a_x[q][:, n, :], a_mv[q][:, n, 0:1], a_rstd[q][:, n:n + 1],
                                          ALU.subtract, ALU.mult)
                    if n == NT - 1:
                        ins.then_inc(sem("xhat_a"), 1)
                elif not (isinstance(c, int) and c + 2 >= B):
                    b = c + 2
                    if n == NT:
                        dve.wait_ge(sem(f"x_in{p}"), (b - p) * 8 + 16)
                        wait(dve, "rstd_a", b - 1)
                    if n < 2 * NT:
                        ins = v.bn_stats(st[:, n - NT, :], x_t[:, n - NT, :])
                    elif n < 3 * NT:
                        if n == 2 * NT:
                            wait_apart(dve, "dve", "var_a_c", 2 * b + 1)
                        ins = v.bn_aggr(mv[:, n - 2 * NT, :], st[:, n - 2 * NT, :])
                    else:
                        dve.wait_ge(sem("var_a_c"), 2 * b + 2)
                        v.tensor_scalar_add(a_var[p], mv[:, :, 1], LN_EPS).then_inc(sem("var_a"), 1)
                    if n in (2 * NT - 1, 3 * NT - 1):
                        ins.then_inc(sem("var_a_c"), 1)

            def back_step(n, i, g):
                c, p = i * G + g, g % 2
                R_ps = (S_ps, T_ps)[p]
                first = isinstance(i, int) and i == 0

                def scan(dst, src, which, j):
                    at = slice(j * P, (j + 1) * P)
                    b = g * NT + j
                    return v.tensor_tensor_scan(dst[:, at], bcast(TD, [P, P]), src[:, at],
                                                0.0 if first else state[:, which, b:b + 1], ALU.mult, ALU.add)

                def keep(src, which):
                    return v.tensor_copy(state[:, which, g * NT:(g + 1) * NT],
                                         src.rearrange("p (j t) -> p j t", j=NT)[:, :, P - 1])
                if n == 0:
                    dve.wait_ge(sem("ek_a"), c + 1)
                    v.scalar_tensor_tensor(a_kv, R_ps[:, 2 * T:3 * T], BV, a_ek[p], ALU.add, ALU.mult
                                           ).then_inc(sem("kv_a"), 1)
                elif n <= NT:
                    ins = scan(a_sb, a_ek[p], 1, n - 1)
                    if n == NT:
                        ins.then_inc(sem("wkv_a"), 1)
                elif n == NT + 1:
                    v.tensor_scalar_add(a_er1, a_er[p], 1.0)
                elif n <= 2 * NT + 1:
                    if n == NT + 2:
                        dve.wait_ge(sem("kv_a"), c + 1)
                    ins = scan(a_sa, a_kv, 0, n - NT - 2)
                    if n == 2 * NT + 1:
                        ins.then_inc(sem("wkv_a"), 1)
                elif n == 2 * NT + 2:
                    wait_apart(dve, "dve", "wkv_a", 5 * c + 1)
                    keep(a_sb, 1)
                elif n == 2 * NT + 3:
                    v.scalar_tensor_tensor(a_den0, a_ek[p], GD, a_sb, ALU.mult, ALU.add).then_inc(sem("wkv_a"), 1)
                elif n == 2 * NT + 4:
                    wait_apart(dve, "dve", "wkv_a", 5 * c + 2)
                    keep(a_sa, 0)
                elif n == 2 * NT + 5:
                    v.scalar_tensor_tensor(a_num, a_kv, GD, a_sa, ALU.mult, ALU.add)
                elif n == 2 * NT + 6:
                    dve.wait_ge(sem("wkv_a"), 5 * c + 3)
                    v.scalar_tensor_tensor(a_den, a_den0, WKV_EPS, a_er1, ALU.add, ALU.mult).then_inc(sem("wkv_a"), 1)
                elif n < BACK - 1:
                    j = n - 2 * NT - 7
                    if j == 0:
                        dve.wait_ge(sem("wkv_a"), 5 * c + 4)
                    ins = v.reciprocal(a_rec[:, j * P:(j + 1) * P], a_den[:, j * P:(j + 1) * P])
                    if j == NT - 1:
                        ins.then_inc(sem("wkv_a"), 1)
                else:
                    dve.wait_ge(sem("wkv_a"), 5 * c + 5)
                    tile_at = slice(i * P, (i + 1) * P) if isinstance(i, int) else bass.ds(i * P, P)
                    v.scalar_tensor_tensor(row_all[:, g * NT:(g + 1) * NT, tile_at],
                                           a_num.rearrange("p (j t) -> p j t", j=NT), 1.0 / THRESH,
                                           a_rec.rearrange("p (j t) -> p j t", j=NT), ALU.mult, ALU.mult
                                           ).then_inc(sem("inp_a"), 1)

            def chunk_step(n, i, g):
                if n < FRONT:
                    front_step(n, i * G + g, g % 2)
                else:
                    back_step(n - FRONT, i, g)

            def chunk_steps(at, of, i, g):
                for n in range(at * (FRONT + BACK) // of, (at + 1) * (FRONT + BACK) // of):
                    chunk_step(n, i, g)

            def turn_steps(turn, i=None, g=None):
                done = turn * (2 * U + 2)
                at = slice(turn * U, (turn + 1) * U) if isinstance(turn, int) else bass.ds(turn * U, U)
                wait_apart(dve, "dve", "mem", done + 1)
                v.tensor_copy(m_in, row_all[:, :, at]).then_inc(sem("mem"), 1)
                dve.wait_ge(sem("mem"), done + 2)
                for j in range(U):
                    prev = m_out[:, :, (j - 1) % U]
                    v.scalar_tensor_tensor(m_tmp, prev, 1.0, m_in[:, :, j], ALU.is_gt, ALU.subtract
                                           ).then_inc(sem("mem"), 1)
                    if g is not None:
                        chunk_steps(2 * j, 2 * U, i, g)
                    dve.wait_ge(sem("mem"), done + 2 * j + 3)
                    v.scalar_tensor_tensor(m_out[:, :, j], prev, BETA, m_tmp, ALU.mult, ALU.subtract
                                           ).then_inc(sem("mem"), 1)
                    if g is not None:
                        chunk_steps(2 * j + 1, 2 * U, i, g)
                    if j < U - 1:
                        dve.wait_ge(sem("mem"), done + 2 * j + 4)
                wait_apart(dve, "dve", "mem", done + 2 * U + 2)
                v.tensor_copy(row_all[:, :, at], m_out).then_inc(sem("mem"), 1)

            for n in range(NT, FRONT):
                front_step(n, -2, 0)
            dve.wait_ge(sem("rstd_a"), 1)
            normalise(a_xhat[0], a_x[0], a_mv[0], a_rstd[0]).then_inc(sem("xhat_a"), 1)
            for n in range(NT, FRONT):
                front_step(n, -1, 1)
            for g in range(G):
                chunk_steps(0, 1, 0, g)
            v.memset(m_out[:, :, U - 1], 0.0).then_inc(sem("mem"), 1)
            with dve.Fori(1, NT - 1) as i:
                for g in range(G):
                    dve.wait_ge(sem("inp_a"), i * G)
                    turn_steps(i * G + (g - G), i, g)
            for g in range(G):
                dve.wait_ge(sem("inp_a"), (NT - 1) * G)
                turn_steps((NT - 2) * G + g, NT - 1, g)
            dve.wait_ge(sem("inp_a"), B)
            with dve.Fori((NT - 1) * G, NT * G) as turn:
                turn_steps(turn)
            dve.wait_ge(sem("mem"), 1 + NT * G * (2 * U + 2))

            def row(b):
                return row_all[:, ds(b), :].rearrange("p o t -> p (o t)")

            places = bcast(place[:].rearrange("p (o e) -> p o e", o=1), [P, NT, E])

            def wide(col):
                return bcast(col.rearrange("p (n o) -> p n o", o=1), [P, NT, E])
            FIRST, SECOND = r_m[:, 0, :], r_m[:, 1, :]
            ROUTE = [lambda: v.tensor_reduce(FIRST, r_lg[:], AX.X, ALU.max),
                     lambda: v.tensor_tensor(r_eq[:], r_lg[:], wide(FIRST), ALU.is_equal),
                     lambda: v.tensor_tensor(r_k[:], r_eq[:], places, ALU.mult),
                     lambda: v.tensor_reduce(r_f[:], r_k[:], AX.X, ALU.max),
                     lambda: v.tensor_tensor(r_one[:, :, 0, :], places, wide(r_f[:]), ALU.is_equal),
                     lambda: v.scalar_tensor_tensor(r_l2[:], r_one[:, :, 0, :], MASKED, r_lg[:], ALU.mult, ALU.add),
                     lambda: v.tensor_reduce(SECOND, r_l2[:], AX.X, ALU.max),
                     lambda: v.tensor_tensor(r_eq[:], r_l2[:], wide(SECOND), ALU.is_equal),
                     lambda: v.tensor_tensor(r_k[:], r_eq[:], places, ALU.mult),
                     lambda: v.tensor_reduce(r_f[:], r_k[:], AX.X, ALU.max),
                     lambda: v.tensor_tensor(r_one[:, :, 1, :], places, wide(r_f[:]), ALU.is_equal),
                     lambda: v.tensor_copy(r_oneh[:], r_one[:].rearrange("p i c e -> p i (c e)"))]
            assert len(ROUTE) == STEPS

            def route_step(k, at, part):
                step = 2 * (at[0] * HQ + at[1]) + part - 3
                if step == -1 and there(k - 2):
                    wait_apart(dve, "dve", "route_mm", k - 1)
                    v.tensor_copy(r_lg[:].rearrange("p i e -> p (i e)"), logits_ps).then_inc(sem("logits_made"), 1)
                if 0 <= step < STEPS and there(k - 2):
                    if step == 0:
                        wait_apart(dve, "dve", "logits_made", k - 1)
                    if step == STEPS - 1:
                        wait_apart(dve, "dve", "rank_mm", k - 2)
                    wait_apart(dve, "dve", "routing", STEPS * (k - 2) + step)
                    ROUTE[step]().then_inc(sem("routing"), 1)

            def run(k, p):
                if there(k + 2):
                    wait_apart(dve, "dve", "v_mm", k + 2)
                    v.tensor_scalar(f_spk[:], row(k + 2), 1.0, mod_cm[:, 2, ds(k + 2)], ALU.is_gt, ALU.mult
                                    ).then_inc(sem("spk_made"), 1)
                for u in range(QUADS):
                    s_b, s_u = k + (u + 2) // QUADS, (u + 2) % QUADS
                    for j in range(HQ):
                        if there(s_b):
                            dve.wait_ge(sem("S_a_mm"), HEADS * s_b + HQ * s_u + j + 1)
                            v.tensor_reduce(blkmax[u % 2][:, j, 0:4],
                                            S_ps[:, 0:T].rearrange("p (n t) -> p n t", n=NT), AX.X, ALU.max
                                            ).then_inc(sem("blk_a_made"), 1)
                        route_step(k, (u, j), 0)
                        if j == 2 and job_index(("max", u, u + 1), k) is not None:
                            n = QUADS * k + u + 1
                            w = (u + 1) % 2
                            dve.wait_ge(sem("max_out"), n + 1)
                            v.scalar_tensor_tensor(shift[w][:, 1, :], max_T[w][:], -1.0, shift[w][:, 0, :],
                                                   ALU.mult, ALU.subtract).then_inc(sem("shift_made"), 1)
                        if j == 2 and job_index(("o", u, u - 2), k) is not None:
                            n = QUADS * k + u - 2
                            h0 = HQ * ((u - 2) % QUADS)
                            dve.wait_ge(sem("o_tr"), n + 1)
                            heads = M_ps[:, :].rearrange("p (i h w) -> p i h w", i=NT, h=HQ)
                            v.reciprocal(o_rec[:], heads[:, :, :, HD]).then_inc(sem("o_rec"), 1)
                            dve.wait_ge(sem("o_rec"), n + 1)
                            if u == 2:
                                wait(dve, "y_tr", k)
                            v.tensor_tensor(b_y[:, :, h0 * HD:(h0 + HQ) * HD].rearrange("p i (h d) -> p i h d", h=HQ),
                                            heads[:, :, :, 0:HD],
                                            bcast(o_rec[:].rearrange("p i (h o) -> p i h o", o=1), [P, NT, HQ, HD]),
                                            ALU.mult).then_inc(sem("y_made"), 1)
                        if (u, j) == (2, 3) and there(k - 2):
                            wait_apart(dve, "dve", "rank_mm", k - 1)
                            v.tensor_tensor(r_pos[:], ranks_ps[:, 0:NT * LISTS].rearrange("p (i l) -> p i l", i=NT),
                                            bcast(r_next[:].rearrange("p (o l) -> p o l", o=1), [P, NT, LISTS]),
                                            ALU.add).then_inc(sem("ranked"), 1)
                            wait_apart(dve, "dve", "ranked", k - 1)
                            v.tensor_tensor(r_next[:], r_next[:], ranks_ps[:, NT * LISTS:(NT + 1) * LISTS], ALU.add
                                            ).then_inc(sem("pos_made"), 1)
                        if (u, j) == (3, 0) and there(k - 2):
                            wait_apart(dve, "dve", "hit_made", k - 1)
                            v.tensor_reduce(r_row[:].rearrange("p i c -> p (i c)"),
                                            r_hit[:].rearrange("p i (c e) -> p (i c) e", c=2), AX.X, ALU.add
                                            ).then_inc(sem("slot_found"), 1)
                        if there(s_b):
                            dve.wait_ge(sem("S_mm"), HEADS * s_b + HQ * s_u + j + 1)
                            v.tensor_reduce(blkmax[u % 2][:, j, 4:NBLK],
                                            S_ps[:, T:SCORES].rearrange("p (n t) -> p n t", n=NBLK - NT), AX.X, ALU.max
                                            ).then_inc(sem("blk_made"), 1)
                        route_step(k, (u, j), 1)
                        if (u, j) == (1, 3) and there(k - 2):
                            wait_apart(dve, "dve", "gates_exp", k - 2)
                            v.tensor_tensor(r_d[:], SECOND, FIRST, ALU.subtract).then_inc(sem("margin_made"), 1)
                        if (u, j) == (2, 3) and there(k - 2):
                            wait_apart(dve, "dve", "ranked", k - 1)
                            v.tensor_tensor(r_hit[:], r_one[:].rearrange("p i c e -> p i (c e)"), r_pos[:], ALU.mult
                                            ).then_inc(sem("hit_made"), 1)
                        if (u, j) == (3, 0) and there(k - 2):
                            wait_apart(dve, "dve", "slot_found", k - 1)
                            wait_apart(dve, "dve", "listed", 16 * 2 * NT * (k - 2))
                            v.tensor_copy(r_slot[:], r_row[:]).then_inc(sem("slot_made"), 1)
                        if (u, j) == (2, 2) and there(k - 2):
                            wait_apart(dve, "dve", "gates_exp", k - 1)
                            v.tensor_scalar_add(r_s[:], r_e2[:], 1.0).then_inc(sem("sum_made"), 1)
                        if (u, j) == (2, 3) and there(k - 2):
                            wait_apart(dve, "dve", "sum_made", k - 1)
                            v.reciprocal(r_w[:, 0, :], r_s[:]).then_inc(sem("weight0"), 1)
                        if (u, j) == (3, 0) and there(k - 2):
                            wait_apart(dve, "dve", "weight0", k - 1)
                            v.tensor_tensor(r_w[:, 1, :], r_w[:, 0, :], r_e2[:], ALU.mult).then_inc(sem("weights_made"), 1)
                        if u == 3 and j in (1, 2) and there(k - 2):
                            if j == 1:
                                dve.wait_ge(sem("weights_made"), k - 1)
                                dve.wait_ge(sem("x1_back"), 32 * (k - 1))
                            for i in range(NT):
                                last = v.tensor_scalar(rows[p][j - 1][:, i, D:2 * D], b_gate[p][:],
                                                       r_w[:, j - 1, i:i + 1], None, ALU.mult)
                            if j == 2:
                                last.then_inc(sem("rows_gated"), 1)
                        if (u, j) == (0, 3) and there(k + 2):
                            b = k + 2
                            dve.wait_ge(sem("spk_tr"), b + 1)
                            dve.wait_ge(sem("x_in_f"), 32 * (b + 1))
                            wait(dve, "x1_saved", 16 * b)
                            v.tensor_tensor(f_x1[:], f_x[:], M_tiles, ALU.add).then_inc(sem("x1_made"), 1)
                            dve.wait_ge(sem("x1_made"), b + 1)
                            stats(f_x1, ln_stats[0], ln_mv[0], ln_var[0][:], "var0", b, None)
                        if (u, j) == (1, 0) and there(k + 2):
                            dve.wait_ge(sem("rstd0"), k + 3)
                            wait(dve, "z1_tr", k + 2)
                            normalise(f_z, f_x1, ln_mv[0], ln_rstd[0]).then_inc(sem("z_made"), 1)
                        if (u, j) == (1, 3) and there(k + 2):
                            dve.wait_ge(sem("h_made"), k + 3)
                            stats(f_h, ln_stats[1], ln_mv[1], ln_var[1][:], "var1", k + 2, None)
                        if (u, j) == (2, 1) and there(k + 2):
                            dve.wait_ge(sem("rstd1"), k + 3)
                            normalise(f_z, f_h, ln_mv[1], ln_rstd[1]).then_inc(sem("z1_made"), 1)
                        if (u, j) == (2, 0) and there(k - 1):
                            b = k - 1
                            dve.wait_ge(sem("proj_mm"), b + 1)
                            dve.wait_ge(sem("h_kept"), b + 1)
                            wait(dve, "base_made", b)
                            v.tensor_tensor(b_x2[:].rearrange("p i d -> p (i d)"), row(b), M_ps[:, :], ALU.add
                                            ).then_inc(sem("x2_made"), 1)
                            dve.wait_ge(sem("x2_made"), b + 1)
                            stats(b_x2, ln_stats[2], ln_mv[2], ln_var[2][:], "var2", b, None)
                        if (u, j) == (3, 0) and there(k - 1):
                            dve.wait_ge(sem("rstd2"), k)
                            wait(dve, "z2_tr", k - 1)
                            wait_apart(dve, "dve", "listed", 16 * 2 * NT * (k - 2))
                            normalise(rows[1 - p][0], b_x2, ln_mv[2], ln_rstd[2]).then_inc(sem("z2_made"), 1)
                    if there(s_b):
                        n = QUADS * s_b + s_u
                        dve.wait_ge(sem("blk_made"), HQ * n + HQ)
                        wait(dve, "max_tr", n - 1)
                        bm, rm = blkmax[u % 2], rowmax[u % 2]
                        v.tensor_reduce(rm[:, :, 3], bm[:, :, 0:4], AX.X, ALU.max)
                        v.tensor_reduce(rm[:, :, 2], bm[:, :, 4:7], AX.X, ALU.max)
                        v.tensor_copy(rm[:, :, 0], bm[:, :, 7])
                        v.tensor_reduce(rm[:, :, 1], bm[:, :, 8:10], AX.X, ALU.max).then_inc(sem("max_made"), 1)

            iterations(run)(dve)

            n_table = [0]

            def chain(ins):
                n_table[0] += 1
                ins.then_inc(sem("table"), 1)
                dve.wait_ge(sem("table"), n_table[0])

            def one(ap):
                return ap[0:1]

            def by_tile(ap):
                return bcast(one(ap).rearrange("p (t o) -> p t o", o=1), [1, NTAB, LISTS])

            def by_list(ap, n=NTAB):
                return bcast(one(ap).rearrange("p (o l) -> p o l", o=1), [1, n, LISTS])
            dve.wait_ge(sem("pv_mm"), QUADS * B)
            dve.wait_ge(sem("T_mm"), HEADS * B)
            dve.wait_ge(sem("pos_made"), B)
            dve.wait_ge(sem("tiles_counted"), 1)
            STEP = TOK // TS
            choices = lambda ap: one(ap).rearrange("p (c e) -> p c e", c=2)
            v.tensor_copy(one(t_no), tile_no[:])
            for e in range(E):
                v.memset(choices(n_exp)[:, :, e], float(e))
            for i in range(LISTS):
                v.memset(l_cap[0:1, i:i + 1], float(i * CAP))
            v.memset(n_exc[0:1, 0:1], 0.0)
            chain(v.memset(n_exc[0:1, E:E + 1], float(HALF)))
            chain(v.tensor_tensor(one(n_cnt), r_next[0:1], one(l_cap), ALU.subtract))
            v.tensor_scalar(one(t_first), one(t_no), float(TS), None, ALU.mult)
            chain(v.tensor_scalar(one(n_cnt), one(n_cnt), 1.0 / TS, None, ALU.mult))
            chain(v.tensor_tensor(one(n_gt), bcast(one(n_cnt).rearrange("p (l o) -> p l o", o=1), [1, LISTS, STEP]),
                                  bcast(t_no[0:1, 0:STEP].rearrange("p (o j) -> p o j", o=1), [1, LISTS, STEP]),
                                  ALU.is_gt))
            chain(v.tensor_reduce(one(n_tiles), one(n_gt), AX.X, ALU.add))
            for e in range(1, E):
                chain(v.tensor_tensor(choices(n_exc)[:, :, e], choices(n_exc)[:, :, e - 1], choices(n_tiles)[:, :, e - 1],
                                      ALU.add))
            chain(v.tensor_tensor(one(n_end), one(n_exc), one(n_tiles), ALU.add))
            v.tensor_scalar(n_used[0:1, 0:1], n_end[0:1, E - 1:E], float(-TS), float(LISTS * CAP), ALU.mult, ALU.add)
            v.tensor_scalar(n_used[0:1, 1:2], n_end[0:1, LISTS - 1:LISTS], float(-TS), float(LISTS * CAP + E * TS),
                            ALU.mult, ALU.add)
            v.scalar_tensor_tensor(one(n_first), one(n_exc), float(-TS), one(l_cap), ALU.mult, ALU.add)
            v.tensor_tensor(one(t_ge), by_tile(t_no), by_list(n_exc), ALU.is_ge)
            chain(v.tensor_tensor(one(t_lt), by_tile(t_no), by_list(n_end), ALU.is_lt))
            chain(v.tensor_tensor(one(t_in), one(t_ge), one(t_lt), ALU.mult))
            chain(v.tensor_tensor(one(t_at), by_tile(t_first), by_list(n_first), ALU.add))
            chain(v.tensor_tensor(one(t_row), one(t_in), one(t_at), ALU.mult))
            v.tensor_reduce(one(t_rows), one(t_row), AX.X, ALU.add)
            v.tensor_reduce(one(t_sum), one(t_in), AX.X, ALU.add)
            v.tensor_scalar(t_spare[0:1, 0:HALF], t_first[0:1, 0:HALF], n_used[0:1, 0:1], None, ALU.add)
            v.tensor_scalar(t_spare[0:1, HALF:NTAB], t_first[0:1, HALF:NTAB], n_used[0:1, 1:2], None, ALU.add)
            chain(v.tensor_tensor(one(t_ge), one(t_in), by_list(n_exp), ALU.mult))
            chain(v.tensor_scalar(one(t_free), one(t_sum), -1.0, 1.0, ALU.mult, ALU.add))
            chain(v.tensor_tensor(one(t_spare), one(t_spare), one(t_free), ALU.mult))
            chain(v.tensor_tensor(one(t_rows), one(t_rows), one(t_spare), ALU.add))
            chain(v.tensor_reduce(one(t_sum), one(t_ge), AX.X, ALU.add))
            v.tensor_copy(tab[0:1, 0:NTAB], one(t_rows))
            v.tensor_copy(tab[0:1, NTAB:2 * NTAB], one(t_sum))
            v.tensor_copy(tab[0:1, 2 * NTAB:], r_next[0:1]).then_inc(sem("tab_made"), 1)
            dve.wait_ge(sem("tab_made"), 1)

            dve.wait_ge(sem("w12_in"), 48)

            def weights(n, r):
                e = dve.value_load(tab[0:1, ds(n + NTAB)], min_val=0, max_val=E - 1)
                if not isinstance(n, int):
                    dve.wait_ge(sem("down_mm"), n - 1)
                v.tensor_scalar(w_tile[r % 4], w_all[:, bass.ds(e, 1), :].rearrange("p o w -> p (o w)"), 1.0, None,
                                ALU.mult).then_inc(sem("w_made"), 1)
            dve.sem_inc(sem("res_made"), 2)
            weights(0, 0)
            weights(1, 1)
            with dve.Fori(0, TILES // TURN) as i:
                for r in range(TURN):
                    weights(i * TURN + (r + 2), r + 2)
                    dve.wait_ge(sem("down_mm"), i * TURN + (r + 3))
                    v.tensor_tensor(res[r], (S_ps, T_ps)[r % 2][:, 1024:1024 + TS].rearrange("p (s d) -> p s d", s=NS),
                                    x_tile[r][:, :, D:2 * D], ALU.mult).then_inc(sem("res_made"), 1)


_INS = ['x', 'W_r', 'b_r', 'W_k', 'b_k', 'W_v', 'b_v', 'W_td', 'b_td', 'global_decay']
_FFN = ['ln1_w', 'c_attn_w', 'c_proj_w', 'ln2_w', 'router_w', 'w1', 'w2']
_NAMES = ['L0_attn_' + n for n in _INS] + ['L0_ffn_' + n for n in _FFN] + ['L0_c', 'L0_wmod']


def kernel(**inputs):
    import numpy as _np
    import concourse.bacc as _bacc
    from concourse import mybir as _mybir
    from concourse.bass_utils import run_bass_kernel_spmd as _run

    nc = _bacc.Bacc("TRN2", target_bir_lowering=False, num_devices=1)
    arrays, args = {}, []
    for name in _NAMES:
        a = _np.ascontiguousarray(inputs[name])
        arrays[f"in_{name}_dram"] = a
        args.append(nc.dram_tensor(f"in_{name}_dram", a.shape, _mybir.dt.from_np(a.dtype), kind="ExternalInput").ap())
    shape = inputs['L0_attn_x'].shape
    experts, tile = 8, 256
    tokens = shape[0] * shape[1]
    out = nc.dram_tensor("out_0_dram", (tokens + (3 * experts + 2) * tile, shape[2]), _mybir.dt.float32, kind="ExternalOutput").ap()
    adaln_spiking_moe_layer(nc, *args, out)
    r = _run(nc, [arrays], core_ids=[0])
    return r.results[0]["out_0_dram"][:tokens].reshape(shape)
```
